# Optimizing a Trainium2 kernel written in Bass

```python
import numpy as np
import jax
import jax.numpy as jnp

def _softmax(x, axis=-1):
    return jax.nn.softmax(x, axis=axis)

def _gelu(x):
    return jax.nn.gelu(x, approximate=True)

def _silu(x):
    return jax.nn.silu(x)

def _sigmoid(x):
    return jax.nn.sigmoid(x)

def _layernorm(x, axis=-1, eps=1e-05):
    m = jnp.mean(x, axis=axis, keepdims=True)
    v = jnp.var(x, axis=axis, keepdims=True)
    return (x - m) / jnp.sqrt(v + eps)

def _scatter_add(tgt, idx, src, axis=0):
    return tgt.at[idx].add(src)

def _segment_sum(src, seg, n):
    return jax.ops.segment_sum(src, seg, n)
kernel_name = 'mk_flamingo_gated_d2_seqx_r8_2299b9'

def setup_inputs(seed: int=0):
    np.random.seed(seed)
    _w = jnp.asarray

    def _rec_inputs():
        import jax
        import jax.numpy as jnp
        _rk = jax.random.key(seed)
        x = 0.0001212 + 1 * jax.random.normal(jax.random.fold_in(_rk, 1), (4, 256, 256), jnp.float32)
        _lenS = 256 - jax.random.randint(jax.random.fold_in(_rk, 7), (4,), 0, max(1, 256 // 4) + 1, jnp.int32)
        _lenS2 = 256 - jax.random.randint(jax.random.fold_in(_rk, 8), (4,), 0, max(1, 256 // 4) + 1, jnp.int32)
        _ctx_2048P = jax.random.normal(jax.random.fold_in(_rk, 11), (4, 16, 256), jnp.float32)
        _ctx_2048c = jax.random.dirichlet(jax.random.fold_in(_rk, 511), 0.3 * jnp.ones((16,), jnp.float32), (4, 256))
        _ctx_2048t = jnp.einsum('bsk,bkd->bsd', _ctx_2048c, _ctx_2048P)
        _ctx_2048t = _ctx_2048t * jax.lax.rsqrt(jnp.mean(jnp.square(_ctx_2048t)) + 1e-12) * 0.953939
        ctx_2048 = 0.000173663 + 1.0001 * (_ctx_2048t + 0.3 * jax.random.normal(jax.random.fold_in(_rk, 611), (4, 256, 256), jnp.float32))
        _g = jax.random.normal(jax.random.fold_in(_rk, 9001), (2, 2), jnp.float32)
        _g = jnp.sign(_g) * jnp.maximum(jnp.abs(_g), 1.0) + (_g == 0) * 1.0
        g_xattn = _g[0]
        g_ffn = _g[1]
        return (x, ctx_2048, g_xattn, g_ffn)
    x, ctx_2048, g_xattn, g_ffn = _rec_inputs()

    def _L0_xattn_setup():
        import jax, jax.numpy as jnp
        import numpy as np
        B_DIM, T_DIM, C_DIM = (16, 128, 256)

        def _wkv(w, u, k, v):
            Bn, Tn, Cn = k.shape
            NEG_INF = jnp.float32(-1e+38)

            def step(carry, kv_t):
                p, q, o = carry
                kt, vt = kv_t
                no = jnp.maximum(o, u + kt)
                A = jnp.exp(o - no)
                E = jnp.exp(u + kt - no)
                y = (A * p + E * vt) / (A * q + E)
                no2 = jnp.maximum(w + o, kt)
                A2 = jnp.exp(w + o - no2)
                E2 = jnp.exp(kt - no2)
                return ((A2 * p + E2 * vt, A2 * q + E2, no2), y)
            init = (jnp.zeros((Bn, Cn), k.dtype), jnp.zeros((Bn, Cn), k.dtype), jnp.full((Bn, Cn), NEG_INF, k.dtype))
            kT = jnp.moveaxis(k, 1, 0)
            vT = jnp.moveaxis(v, 1, 0)
            _, yT = jax.lax.scan(step, init, (kT, vT))
            return jnp.moveaxis(yT, 0, 1)
        key = jax.random.key(seed)
        k1, k2, k3, k4 = jax.random.split(key, 4)
        w = -jnp.exp(jax.random.normal(k1, (C_DIM,), jnp.float32))
        u = jax.random.normal(k2, (C_DIM,), jnp.float32)
        k = jax.random.normal(k3, (B_DIM, T_DIM, C_DIM), jnp.float32)
        v = jax.random.normal(k4, (B_DIM, T_DIM, C_DIM), jnp.float32)
        return {'B': B_DIM, 'T': T_DIM, 'C': C_DIM, 'w': w, 'u': u, 'k': k, 'v': v}
    _L0_xattn_all = _L0_xattn_setup()
    _L0_xattn_in = {k: v for k, v in _L0_xattn_all.items() if k in ('w', 'u')}
    del _L0_xattn_all

    def _L0_ffn_setup():
        import jax, jax.numpy as jnp
        import numpy as np
        B, S, D = (4, 256, 256)
        E = 8
        H = 352
        CAP_F = 1.0

        def _moe(x, Wg, W1, W3, W2, sw1, sw3, sw2):
            b, sl, d = x.shape
            T = b * sl
            C = int(CAP_F * T / E)
            xt = x.reshape(T, d)
            probs = jax.nn.softmax(xt @ Wg, axis=-1)
            eidx = jnp.argmax(probs, axis=-1)
            gate = jnp.take_along_axis(probs, eidx[:, None], 1)[:, 0]
            oh = jax.nn.one_hot(eidx, E, dtype=jnp.int32)
            pos = (jnp.cumsum(oh, axis=0) * oh).sum(-1) - 1
            keep = pos < C
            flat = jnp.where(keep, eidx * C + pos, E * C)
            xd = jnp.zeros((E * C, d), x.dtype).at[flat].set(xt, mode='drop')
            xd = xd.reshape(E, C, d)
            h = jax.nn.silu(jnp.einsum('ecd,edh->ech', xd, W1)) * jnp.einsum('ecd,edh->ech', xd, W3)
            oe = jnp.einsum('ech,ehd->ecd', h, W2).reshape(E * C, d)
            out = jnp.take(oe, jnp.minimum(flat, E * C - 1), axis=0)
            out = out * (gate * keep.astype(x.dtype))[:, None]
            shared = jax.nn.silu(xt @ sw1) * (xt @ sw3) @ sw2
            return (out + shared).reshape(b, sl, d)
        key = jax.random.key(seed)
        ks = jax.random.split(key, 8)
        s = lambda fan: 1.0 / np.sqrt(fan)
        return {'x': jax.random.normal(ks[0], (B, S, D), jnp.float32), 'Wg': jax.random.normal(ks[1], (D, E), jnp.float32) * s(D), 'W1': jax.random.normal(ks[2], (E, D, H), jnp.float32) * s(D), 'W3': jax.random.normal(ks[3], (E, D, H), jnp.float32) * s(D), 'W2': jax.random.normal(ks[4], (E, H, D), jnp.float32) * s(H), 'sw1': jax.random.normal(ks[5], (D, H), jnp.float32) * s(D), 'sw3': jax.random.normal(ks[6], (D, H), jnp.float32) * s(D), 'sw2': jax.random.normal(ks[7], (H, D), jnp.float32) * s(H)}
    _L0_ffn_all = _L0_ffn_setup()
    _L0_ffn_in = {k: v for k, v in _L0_ffn_all.items() if k in ('Wg', 'W1', 'W3', 'W2', 'sw1', 'sw3', 'sw2')}
    del _L0_ffn_all

    def _L1_xattn_setup():
        import math
        import jax, jax.numpy as jnp
        import numpy as np
        HEADS = 16
        MASKED_BIAS = -10000.0

        def _mha(q, k, v):
            B, Sq, D = q.shape
            Sk = k.shape[-2]
            hd = D // HEADS
            qh = q.reshape(B, Sq, HEADS, hd).transpose(0, 2, 1, 3)
            kh = k.reshape(B, Sk, HEADS, hd).transpose(0, 2, 1, 3)
            vh = v.reshape(B, Sk, HEADS, hd).transpose(0, 2, 1, 3)
            scores = jnp.einsum('bhqd,bhkd->bhqk', qh, kh) / math.sqrt(hd)
            qi = jnp.arange(Sq)[:, None] + (Sk - Sq)
            ki = jnp.arange(Sk)[None, :]
            causal = ki <= qi
            scores = jnp.where(causal[None, None], scores, jnp.asarray(MASKED_BIAS, scores.dtype))
            attn = jax.nn.softmax(scores, axis=-1)
            out = jnp.einsum('bhqk,bhkd->bhqd', attn, vh)
            return out.transpose(0, 2, 1, 3).reshape(B, Sq, D)
        key = jax.random.key(seed)
        kq, kk, kv = jax.random.split(key, 3)
        B, S, D = (4, 128, 256)
        q = jax.random.normal(kq, (B, S, D), dtype=jnp.float32)
        k = jax.random.normal(kk, (B, S, D), dtype=jnp.float32)
        v = jax.random.normal(kv, (B, S, D), dtype=jnp.float32)
        return {'q': q, 'k': k, 'v': v}
    _L1_xattn_all = _L1_xattn_setup()
    _L1_xattn_in = {k: v for k, v in _L1_xattn_all.items() if k in ()}
    del _L1_xattn_all

    def _L1_ffn_setup():
        import jax, jax.numpy as jnp
        import numpy as np
        ALPHA = 1.702
        LIMIT = 7.0
        TOP_K = 2
        E, H, I = (8, 256, 256)
        B, S = (2, 256)
        key = jax.random.key(seed)
        ks = jax.random.split(key, 7)
        return {'hidden_states': jax.random.normal(ks[0], (B, S, H), dtype=jnp.float32), 'router_weight': jax.random.normal(ks[1], (E, H), dtype=jnp.float32) * 0.02, 'router_bias': jax.random.normal(ks[2], (E,), dtype=jnp.float32) * 0.02, 'gate_up_proj': jax.random.normal(ks[3], (E, H, 2 * I), dtype=jnp.float32) * 0.02, 'gate_up_proj_bias': jax.random.normal(ks[4], (E, 2 * I), dtype=jnp.float32) * 0.02, 'down_proj': jax.random.normal(ks[5], (E, I, H), dtype=jnp.float32) * 0.02, 'down_proj_bias': jax.random.normal(ks[6], (E, H), dtype=jnp.float32) * 0.02}
    _L1_ffn_all = _L1_ffn_setup()
    _L1_ffn_in = {k: v for k, v in _L1_ffn_all.items() if k in ('router_weight', 'router_bias', 'gate_up_proj', 'gate_up_proj_bias', 'down_proj', 'down_proj_bias')}
    del _L1_ffn_all
    return {'x': x, 'ctx_2048': ctx_2048, 'g_xattn': g_xattn, 'g_ffn': g_ffn, 'L0_xattn_w': _L0_xattn_in['w'], 'L0_xattn_u': _L0_xattn_in['u'], 'L0_ffn_Wg': _L0_ffn_in['Wg'], 'L0_ffn_W1': _L0_ffn_in['W1'], 'L0_ffn_W3': _L0_ffn_in['W3'], 'L0_ffn_W2': _L0_ffn_in['W2'], 'L0_ffn_sw1': _L0_ffn_in['sw1'], 'L0_ffn_sw3': _L0_ffn_in['sw3'], 'L0_ffn_sw2': _L0_ffn_in['sw2'], 'L1_ffn_router_weight': _L1_ffn_in['router_weight'], 'L1_ffn_router_bias': _L1_ffn_in['router_bias'], 'L1_ffn_gate_up_proj': _L1_ffn_in['gate_up_proj'], 'L1_ffn_gate_up_proj_bias': _L1_ffn_in['gate_up_proj_bias'], 'L1_ffn_down_proj': _L1_ffn_in['down_proj'], 'L1_ffn_down_proj_bias': _L1_ffn_in['down_proj_bias']}

def reference(x, ctx_2048, g_xattn, g_ffn, L0_xattn_w, L0_xattn_u, L0_ffn_Wg, L0_ffn_W1, L0_ffn_W3, L0_ffn_W2, L0_ffn_sw1, L0_ffn_sw3, L0_ffn_sw2, L1_ffn_router_weight, L1_ffn_router_bias, L1_ffn_gate_up_proj, L1_ffn_gate_up_proj_bias, L1_ffn_down_proj, L1_ffn_down_proj_bias):
    import jax
    import jax.numpy as jnp

    def _L0_xattn_ref(B, T, C, w, u, k, v):
        import jax, jax.numpy as jnp
        import numpy as np
        B_DIM, T_DIM, C_DIM = (16, 128, 256)

        def _wkv(w, u, k, v):
            Bn, Tn, Cn = k.shape
            NEG_INF = jnp.float32(-1e+38)

            def step(carry, kv_t):
                p, q, o = carry
                kt, vt = kv_t
                no = jnp.maximum(o, u + kt)
                A = jnp.exp(o - no)
                E = jnp.exp(u + kt - no)
                y = (A * p + E * vt) / (A * q + E)
                no2 = jnp.maximum(w + o, kt)
                A2 = jnp.exp(w + o - no2)
                E2 = jnp.exp(kt - no2)
                return ((A2 * p + E2 * vt, A2 * q + E2, no2), y)
            init = (jnp.zeros((Bn, Cn), k.dtype), jnp.zeros((Bn, Cn), k.dtype), jnp.full((Bn, Cn), NEG_INF, k.dtype))
            kT = jnp.moveaxis(k, 1, 0)
            vT = jnp.moveaxis(v, 1, 0)
            _, yT = jax.lax.scan(step, init, (kT, vT))
            return jnp.moveaxis(yT, 0, 1)
        return _wkv(w, u, k, v)

    def _L0_ffn_ref(x, Wg, W1, W3, W2, sw1, sw3, sw2):
        import jax, jax.numpy as jnp
        import numpy as np
        B, S, D = (4, 256, 256)
        E = 8
        H = 352
        CAP_F = 1.0

        def _moe(x, Wg, W1, W3, W2, sw1, sw3, sw2):
            b, sl, d = x.shape
            T = b * sl
            C = int(CAP_F * T / E)
            xt = x.reshape(T, d)
            probs = jax.nn.softmax(xt @ Wg, axis=-1)
            eidx = jnp.argmax(probs, axis=-1)
            gate = jnp.take_along_axis(probs, eidx[:, None], 1)[:, 0]
            oh = jax.nn.one_hot(eidx, E, dtype=jnp.int32)
            pos = (jnp.cumsum(oh, axis=0) * oh).sum(-1) - 1
            keep = pos < C
            flat = jnp.where(keep, eidx * C + pos, E * C)
            xd = jnp.zeros((E * C, d), x.dtype).at[flat].set(xt, mode='drop')
            xd = xd.reshape(E, C, d)
            h = jax.nn.silu(jnp.einsum('ecd,edh->ech', xd, W1)) * jnp.einsum('ecd,edh->ech', xd, W3)
            oe = jnp.einsum('ech,ehd->ecd', h, W2).reshape(E * C, d)
            out = jnp.take(oe, jnp.minimum(flat, E * C - 1), axis=0)
            out = out * (gate * keep.astype(x.dtype))[:, None]
            shared = jax.nn.silu(xt @ sw1) * (xt @ sw3) @ sw2
            return (out + shared).reshape(b, sl, d)
        return _moe(x, Wg, W1, W3, W2, sw1, sw3, sw2)

    def _L1_xattn_ref(q, k, v):
        import math
        import jax, jax.numpy as jnp
        import numpy as np
        HEADS = 16
        MASKED_BIAS = -10000.0

        def _mha(q, k, v):
            B, Sq, D = q.shape
            Sk = k.shape[-2]
            hd = D // HEADS
            qh = q.reshape(B, Sq, HEADS, hd).transpose(0, 2, 1, 3)
            kh = k.reshape(B, Sk, HEADS, hd).transpose(0, 2, 1, 3)
            vh = v.reshape(B, Sk, HEADS, hd).transpose(0, 2, 1, 3)
            scores = jnp.einsum('bhqd,bhkd->bhqk', qh, kh) / math.sqrt(hd)
            qi = jnp.arange(Sq)[:, None] + (Sk - Sq)
            ki = jnp.arange(Sk)[None, :]
            causal = ki <= qi
            scores = jnp.where(causal[None, None], scores, jnp.asarray(MASKED_BIAS, scores.dtype))
            attn = jax.nn.softmax(scores, axis=-1)
            out = jnp.einsum('bhqk,bhkd->bhqd', attn, vh)
            return out.transpose(0, 2, 1, 3).reshape(B, Sq, D)
        return _mha(q, k, v)

    def _L1_ffn_ref(hidden_states, router_weight, router_bias, gate_up_proj, gate_up_proj_bias, down_proj, down_proj_bias):
        import jax, jax.numpy as jnp
        import numpy as np
        ALPHA = 1.702
        LIMIT = 7.0
        TOP_K = 2
        E, H, I = (8, 256, 256)
        B, S = (2, 256)
        bsz, seq_len, hidden = hidden_states.shape
        h = hidden_states.reshape(-1, hidden)
        T = h.shape[0]
        logits = h @ router_weight.T + router_bias
        top_vals, top_idx = jax.lax.top_k(logits, TOP_K)
        top_w = jax.nn.softmax(top_vals, axis=-1)
        scores = jnp.zeros_like(logits).at[jnp.arange(T)[:, None], top_idx].set(top_w)
        gate_up = jnp.einsum('th,ehj->etj', h, gate_up_proj) + gate_up_proj_bias[:, None, :]
        gate = gate_up[..., ::2]
        up = gate_up[..., 1::2]
        gate = jnp.minimum(gate, LIMIT)
        up = jnp.clip(up, -LIMIT, LIMIT)
        glu = gate * jax.nn.sigmoid(gate * ALPHA)
        act = (up + 1.0) * glu
        expert_out = jnp.einsum('eti,eih->eth', act, down_proj) + down_proj_bias[:, None, :]
        out = jnp.einsum('te,eth->th', scores, expert_out)
        return out.reshape(bsz, seq_len, hidden)
    x = x + jnp.tanh(g_xattn[0]) * _L0_xattn_ref(4, 256, 256, L0_xattn_w, L0_xattn_u, _layernorm(x, axis=-1), ctx_2048)
    x = x + jnp.tanh(g_ffn[0]) * _L0_ffn_ref(_layernorm(x, axis=-1), L0_ffn_Wg, L0_ffn_W1, L0_ffn_W3, L0_ffn_W2, L0_ffn_sw1, L0_ffn_sw3, L0_ffn_sw2)
    x = x + jnp.tanh(g_xattn[1]) * _L1_xattn_ref(_layernorm(x, axis=-1), ctx_2048, ctx_2048)
    x = x + jnp.tanh(g_ffn[1]) * _L1_ffn_ref(_layernorm(x, axis=-1), L1_ffn_router_weight, L1_ffn_router_bias, L1_ffn_gate_up_proj, L1_ffn_gate_up_proj_bias, L1_ffn_down_proj, L1_ffn_down_proj_bias)
    return x

_drawn_inputs = setup_inputs


def setup_inputs(seed=0):
    import zlib

    import numpy as np

    out = dict(_drawn_inputs(seed))
    spreads = {'g_ffn': (-1.0, 0.6)}
    factors = {'L1_ffn_router_bias': 8.0,
     'L1_ffn_gate_up_proj_bias': 22.554,
     'L1_ffn_down_proj_bias': 4.945}
    for name, (base, spread) in spreads.items():
        noise = np.random.default_rng([zlib.crc32(name.encode()), seed]).standard_normal(out[name].shape)
        drawn = base * np.exp(spread * noise) if base else spread * noise
        out[name] = jnp.asarray(drawn.astype(out[name].dtype))
    for name, factor in factors.items():
        out[name] = (out[name] * factor).astype(out[name].dtype)
    return out
```

```python
import concourse.bass as bass
from concourse import mybir
from contextlib import ExitStack

P = 128
FP32 = mybir.dt.float32
FP16 = mybir.dt.float16
BF16 = mybir.dt.bfloat16
U32 = mybir.dt.uint32
I32 = mybir.dt.int32
ALU = mybir.AluOpType
ACT = mybir.ActivationFunctionType
AXX = mybir.AxisListType.X


def flamingo_kernel(nc, x, ctx_in, g_xattn, g_ffn, wkv_w, wkv_u, Wg, W1, W3, W2, sw1, sw3, sw2,
                    router_w, router_b, gate_up, gate_up_b, down, down_b, out):
    B, S, D = x.shape
    T = B * S
    NT = T // P
    TPB = S // P
    KC = D // P
    E = Wg.shape[1]
    H = W1.shape[2]
    HC = -(-H // P)
    HP = HC * P
    HR = H - (HC - 1) * P
    CAP = T // E
    I = down.shape[1]
    GU = 2 * I
    HEADS = 16
    HD = D // HEADS
    NPAIR = HEADS // 2
    NTILE1 = (2 * T) // P + E - 1
    NEG = -1.0e38
    EPS = 1.0e-5
    FAR = 4096.0
    SEQ = S + 1
    NP2 = NT // 4
    NG = NP2 * KC
    MASK = -10000.0
    SMALL = 5 + KC

    x_v = x.rearrange("b s d -> (b s) d").rearrange("(i p) d -> p i d", p=P)
    ctx_v = ctx_in.rearrange("b s d -> (b s) d").rearrange("(i p) d -> p i d", p=P)
    out_v = out.rearrange("b s d -> (b s) d").rearrange("(i p) d -> p i d", p=P)

    disp0 = nc.dram_tensor("disp0", [E * CAP, D], FP32, kind="Internal").ap()
    made0 = nc.dram_tensor("made0", [E * CAP, D], FP32, kind="Internal").ap()
    disp1 = nc.dram_tensor("disp1", [E * T, D], FP32, kind="Internal").ap()
    made1 = nc.dram_tensor("made1", [NTILE1 * P, D], FP32, kind="Internal").ap()

    ctx = ExitStack()
    with ctx:
        def sb(name, shape, dt=FP32):
            return ctx.enter_context(nc.sbuf_tensor(name, shape, dt))

        def sem(name):
            return ctx.enter_context(nc.semaphore(name))

        ident = sb("ident", [P, P])
        ident16 = sb("ident16", [P, P], FP16)
        identb = sb("identb", [P, P], BF16)
        upper = sb("upper", [P, P], BF16)
        onesb = sb("onesb", [P, P], BF16)
        causal = sb("causal", [P, P], BF16)
        iota8 = sb("iota8", [P, E])
        iota_t = sb("iota_t", [P, NTILE1])
        nhalf = sb("nhalf", [P, NT])
        zrow = sb("zrow", [P, 512])
        gates = sb("gates", [P, 4])
        tg = sb("tg", [P, 4])
        w_sb = sb("w_sb", [P, KC])
        u_sb = sb("u_sb", [P, KC])
        wg_sb = sb("wg_sb", [P, KC, E])
        rw_sb = sb("rw_sb", [P, KC, E])
        rb_sb = sb("rb_sb", [P, E])
        NB = E * (GU + D)
        bias_in = sb("bias_in", [P, NB // P])
        bias_r = sb("bias_r", [P, 2, NB // P])
        bias_p = sb("bias_p", [P, 3, NB // P], BF16)
        bias3 = sb("bias3", [3, NB], BF16)
        st = sb("st", [P, 4, NT, 6])
        mv = sb("mv", [P, 4, NT, 2])
        rs = sb("rs", [P, 4, NT])
        lg = sb("lg", [P, NT, E])
        mx = sb("mx", [P, NT, E])
        ix = sb("ix", [P, NT, E], U32)
        ixf = sb("ixf", [P, NT, 2])
        pe_ = sb("pe_", [P, NT, E])
        oh = sb("oh", [P, 2, NT, E])
        ohb = sb("ohb", [P, NT, E], BF16)
        cumoh = sb("cumoh", [P, 2, NT, E])
        ssum = sb("ssum", [P, NT])
        pos = sb("pos", [P, 2, NT])
        keep = sb("keep", [P, NT])
        slotf = sb("slotf", [P, 2, NT])
        sidx = sb("sidx", [P, 2, NT], U32)
        gidx = sb("gidx", [P, 2, NT], U32)
        coef = sb("coef", [P, 2, NT])
        cnt = sb("cnt", [P, 4, E])
        nti = sb("nti", [P, E], I32)
        tle = sb("tle", [P, 2, NTILE1, E])
        tabf = sb("tabf", [P, 3, NTILE1])
        tabi = sb("tabi", [P, 2, NTILE1], I32)
        x_sb = sb("x_sb", [P, NT, D])
        ctx_sb = sb("ctx_sb", [P, NT, D])
        v17 = sb("v17", [P, NT, HEADS, HD + 1])
        xn = sb("xn", [P, NT, D])
        xT = sb("xT", [P, KC, T])
        wts = sb("wts", [P, 3 * E * KC * HP])
        w1_sb = wts[:, 0:E * KC * HP].rearrange("p (e k h) -> p e k h", e=E, k=KC)
        w3_sb = wts[:, E * KC * HP:2 * E * KC * HP].rearrange("p (e k h) -> p e k h", e=E, k=KC)
        w2_sb = wts[:, 2 * E * KC * HP:2 * E * KC * HP + E * HC * D].rearrange("p (e c d) -> p e c d", e=E, c=HC)
        gu_sb = wts[:, 0:E * KC * GU]
        dn_sb = wts[:, E * KC * GU:E * KC * GU + E * KC * D]
        sw1_sb = sb("sw1_sb", [P, KC, HP])
        sw3_sb = sb("sw3_sb", [P, KC, HP])
        sw2_sb = sb("sw2_sb", [P, HC, D])
        hT = sb("hT", [P, HC, 512])
        thb = sb("thb", [P, 2, 512])
        arena = sb("arena", [P, 13700])
        at = [0]

        def take(words):
            at[0] += words
            assert at[0] <= 13700
            return arena[:, at[0] - words:at[0]]

        def seqs(n=1):
            return take(n * 2 * SEQ).rearrange("p (n a t) -> p n a t", n=n, a=2)

        w0 = seqs(KC)
        kT = seqs(NG)
        vT = take(NG * 512).rearrange("p (n a t) -> p n a t", n=NG, a=2)
        O, A2, E2, EV, NO, AA, EE, T1 = [seqs(2) for _ in range(8)]
        PP, QQ, T2 = EV, E2, NO
        at[0] = 0
        ktb = take(B * NPAIR * S // 2).bitcast(FP16).rearrange("p (b h t) -> p b h t", b=B, h=NPAIR)
        qtb = take(2 * NPAIR * S // 2).bitcast(FP16).rearrange("p (b h t) -> p b h t", b=2, h=NPAIR)
        pT = take(2 * 3072).rearrange("p (n s c) -> p n s c", n=2, s=3)
        spl = thb[:, :, :].rearrange("p n t -> p (n t)").bitcast(FP16).rearrange("p (n h s c) -> p n h s c", n=2, h=HEADS, s=4)
        sel = hT[:, 0:2, :].rearrange("p n t -> p (n t)").bitcast(BF16).rearrange("p (h k) -> p h k", h=HEADS)
        mmax = take(2 * 2 * HEADS).rearrange("p (n q h) -> p n q h", n=2, q=2)
        mneg = take(2 * HEADS).bitcast(BF16).rearrange("p (n q h) -> p n q h", n=2, q=2)
        mT = take(S).bitcast(BF16).rearrange("p (n q) -> p n q", n=2)
        den = take(2 * 16).rearrange("p (n q h) -> p n q h", n=2, q=2)
        att = sw1_sb[:, :, :].rearrange("p k h -> p (k h)")[:, 0:512].rearrange("p (n q h c) -> p n q h c", n=2, q=2, h=8)
        xrT = sw2_sb[:, :, :].rearrange("p k h -> p (k h)")[:, 0:KC * 256].rearrange("p (k t) -> p k t", k=KC)
        at[0] = 0
        xt = take(4 * D).rearrange("p (n d) -> p n d", n=4)
        xtT = take(2 * D).rearrange("p (n k t) -> p n k t", n=2, k=KC)
        gh = take(2 * I).rearrange("p (n i) -> p n i", n=2)
        up = take(2 * I).rearrange("p (n i) -> p n i", n=2)
        th1 = take(2 * I).rearrange("p (n i) -> p n i", n=2)
        glu = take(2 * I).rearrange("p (n i) -> p n i", n=2)
        actv = take(2 * I).rearrange("p (n i) -> p n i", n=2)
        actT = take(2 * I).rearrange("p (n k t) -> p n k t", n=2, k=KC)
        mk1 = take(4 * D).rearrange("p (n d) -> p n d", n=4)
        got1 = take(2 * NT * D).rearrange("p (k i d) -> p k i d", k=2, i=NT)

        xd = xn
        got0 = xn
        made_sb = xT[:, :, :].rearrange("p k t -> p (k t)").rearrange("p (e d) -> p e d", e=E)
        hTe = hT[:, :, :].rearrange("p c t -> p (c t)")
        xdT = take(2 * D).rearrange("p (n k t) -> p n k t", n=2, k=KC)
        the = take(2 * HP).rearrange("p (n h) -> p n h", n=2)
        he = take(2 * HP).rearrange("p (n h) -> p n h", n=2)

        ps = ctx.enter_context(nc.psum_tensor("ps", [P, 8, 512], FP32))

        def ps16(b):
            return ps[:, b, :].bitcast(FP16).rearrange("p (h t) -> p h t", t=P)

        x_in = [sem(f"x_in{p}") for p in range(NP2)]
        ctx_in_s = [sem(f"ctx_in{p}") for p in range(NP2)]
        small_in = sem("small_in")
        bias_in_s = sem("bias_in_s")
        bias_rows = sem("bias_rows")
        wg_in = sem("wg_in")
        sw_in = sem("sw_in")
        w1_in = [sem(f"w1_in{c}") for c in range(2)]
        w3_in = [sem(f"w3_in{c}") for c in range(2)]
        w2_in = sem("w2_in")
        gu_in = sem("gu_in")
        dn_in = sem("dn_in")
        zero_out = sem("zero_out")
        pool_c = sem("pool_c")
        consts_ok = sem("consts_ok")
        sel_ok = sem("sel_ok")
        bias_p_ok = sem("bias_p_ok")
        zrow_ok = sem("zrow_ok")
        pads_ok = sem("pads_ok")
        w0_ok = sem("w0_ok")
        tg_ok = sem("tg_ok")
        v17_ok = sem("v17_ok")
        var_ok = sem("var_ok")
        rstd_ok = sem("rstd_ok")
        xn_ok = sem("xn_ok")
        kT_ps, vT_ps, kT_ok, vT_ok = sem("kT_ps"), sem("vT_ps"), sem("kT_ok"), sem("vT_ok")
        o_ok, a2_ok, no_ok, ee_ok = sem("o_ok"), sem("a2_ok"), sem("no_ok"), sem("ee_ok")
        e2_ok, aa_ok, ev_ok, t2_ok = sem("e2_ok"), sem("aa_ok"), sem("ev_ok"), sem("t2_ok")
        a2_exp, e2_exp, aa_exp, ee_exp = sem("a2_exp"), sem("e2_exp"), sem("aa_exp"), sem("ee_exp")
        y_ok, yT_ps, x1_ok = sem("y_ok"), sem("yT_ps"), sem("x1_ok")
        x1T_ps, x1T_ok = sem("x1T_ps"), sem("x1T_ok")
        lg0_ps, lg0_ok, ex0_in, ex0_ok = sem("lg0_ps"), sem("lg0_ok"), sem("ex0_in"), sem("ex0_ok")
        oh0_ok, cum0_ps, cum0_ok, idx0_ok = sem("oh0_ok"), sem("cum0_ps"), sem("cum0_ok"), sem("idx0_ok")
        disp0_in, disp0_out = sem("disp0_in"), [sem(f"disp0_out{c}") for c in range(4)]
        sh_ps, sh_th, sh_ok, sho_ps, xs_ok = sem("sh_ps"), sem("sh_th"), sem("sh_ok"), sem("sho_ps"), sem("xs_ok")
        xdT_ps, xdT_ok, h0_ps, h0_th, h0_ok = sem("xdT_ps"), sem("xdT_ok"), sem("h0_ps"), sem("h0_th"), sem("h0_ok")
        oe0_ps, oe0_ok, made0_in, got0_in = sem("oe0_ps"), sem("oe0_ok"), sem("made0_in"), [sem(f"got0_in{b}") for b in range(B)]
        x2_ok = sem("x2_ok")
        k_hi, k_lo, q_hi, q_lo = sem("k_hi"), sem("k_lo"), sem("q_hi"), sem("q_lo")
        misc_ps, misc_free = sem("misc_ps"), sem("misc_free")
        nat_ps, nat_ok, mneg_ok = sem("nat_ps"), sem("nat_ok"), sem("mneg_ok")
        st_ps, st_exp, causal_ok, pv_ps, pv_ok = sem("st_ps"), sem("st_exp"), sem("causal_ok"), sem("pv_ps"), sem("pv_ok")
        ex1_in, ex1_ok, oh1_ok, idx1_ok = sem("ex1_in"), sem("ex1_ok"), sem("oh1_ok"), sem("idx1_ok")
        disp1_in, tab_ok, gidx1_ok = sem("disp1_in"), sem("tab_ok"), sem("gidx1_ok")
        xt_in = [sem(f"xt_in{c}") for c in range(4)]
        xtT_ps, xtT_ok, gu_ps, gh_ok, th1_ok, act_ok = sem("xtT_ps"), sem("xtT_ok"), sem("gu_ps"), sem("gh_ok"), sem("th1_ok"), sem("act_ok")
        actT_ps, actT_ok, oe1_ps, mk1_ok = sem("actT_ps"), sem("actT_ok"), sem("oe1_ps"), sem("mk1_ok")
        made1_in, got1_in, x4_ok, out_done = [sem(f"made1_in{c}") for c in range(4)], [sem(f"got1_in{b}") for b in range(B)], sem("x4_ok"), sem("out_done")
        v_chain, a_chain = sem("v_chain"), sem("a_chain")


        block = ctx.enter_context(nc.Block())

        @block.sync
        def _(sp):
            for p in range(NP2):
                sp.dma_start(x_sb[:, 4 * p:4 * p + 4, :], x_v[:, 4 * p:4 * p + 4, :]).then_inc(x_in[p], 16)
                sp.dma_start(ctx_sb[:, 4 * p:4 * p + 4, :], ctx_v[:, 4 * p:4 * p + 4, :]).then_inc(ctx_in_s[p], 16)
            sp.dma_start(wg_sb[:, :, :], Wg.rearrange("(k p) e -> p k e", p=P)).then_inc(wg_in, 16)
            sp.dma_start(sw1_sb[:, :, 0:H], sw1.rearrange("(k p) h -> p k h", p=P)).then_inc(sw_in, 16)
            sp.dma_start(sw3_sb[:, :, 0:H], sw3.rearrange("(k p) h -> p k h", p=P)).then_inc(sw_in, 16)
            sp.wait_ge(pads_ok, 1)
            sp.dma_start(sw2_sb[:, 0:HC - 1, :], sw2[0:(HC - 1) * P, :].rearrange("(c p) d -> p c d", p=P)).then_inc(sw_in, 16)
            sp.dma_start(sw2_sb[0:HR, HC - 1, :], sw2[(HC - 1) * P:H, :]).then_inc(sw_in, 16)
            for c in range(2):
                es = slice(c * E // 2, (c + 1) * E // 2)
                for w, dst, done in ((W1, w1_sb, w1_in), (W3, w3_sb, w3_in)):
                    for e in range(es.start, es.stop):
                        sp.dma_start(dst[:, e, :, 0:H], w[e].rearrange("(k p) h -> p k h", p=P)).then_inc(done[c], 16)
            for e in range(E):
                sp.dma_start(w2_sb[:, e, 0:HC - 1, :], W2[e, 0:(HC - 1) * P, :].rearrange("(c p) d -> p c d", p=P)).then_inc(w2_in, 16)
            sp.dma_start(w2_sb[0:HR, :, HC - 1, :], W2[:, (HC - 1) * P:H, :].rearrange("e p d -> p e d")).then_inc(w2_in, 16)
            sp.wait_ge(disp0_in, 16 * NT)
            for c in range(4):
                sp.dma_start(xd[:, 2 * c:2 * c + 2, :], disp0[2 * c * P:(2 * c + 2) * P, :].rearrange("(e p) d -> p e d", p=P)).then_inc(disp0_out[c], 16)
            for e in range(E):
                sp.wait_ge(oe0_ok, e + 1)
                sp.dma_start(made0[e * P:(e + 1) * P, :], made_sb[:, e, :]).then_inc(made0_in, 16)
            sp.wait_ge(oe0_ps, E)
            for e in range(E):
                sp.dma_start(gu_sb[:, e * KC * GU:(e + 1) * KC * GU].rearrange("p (k j) -> p k j", k=KC),
                             gate_up[e].rearrange("(k p) j -> p k j", p=P)).then_inc(gu_in, 16)
                sp.dma_start(dn_sb[:, e * KC * D:(e + 1) * KC * D].rearrange("p (k j) -> p k j", k=KC),
                             down[e].rearrange("(k p) j -> p k j", p=P)).then_inc(dn_in, 16)
            sp.wait_ge(disp1_in, 16 * 2 * NT)
            sp.wait_ge(tab_ok, 1)
            for t in range(NTILE1):
                if t >= 4:
                    sp.wait_ge(xtT_ps, t - 3)
                row = sp.value_load(tabi[0:1, 1, t:t + 1], min_val=0, max_val=E * T - P)
                sp.dma_start(xt[:, t % 4, :], disp1[bass.ds(row, P), :]).then_inc(xt_in[t % 4], 16)
            for i in range(NT):
                sp.wait_ge(x4_ok, i + 1)
                sp.dma_start(out_v[:, i, :], x_sb[:, i, :]).then_inc(out_done, 16)
            sp.wait_ge(out_done, 16 * NT)
            sp.wait_ge(zero_out, 16 * 9)

        def cur(buf, n):
            return buf[:, n, :, 1:SEQ]

        def prev(buf, n):
            return buf[:, n, :, 0:S]

        def flat(buf, n):
            return buf[:, n, :, :].rearrange("p a t -> p (a t)")

        NAT = [(4 * s, 4, 1) if s < 2 else (0, 8, 0) for s in range(3)] + [(8 + 4 * s, 4, 1) if s < 2 else (8, 8, 0) for s in range(3)]

        def sub_cols(buf2, nh):
            return buf2[:, :, 0:nh // 2 * (1024 // nh)].rearrange("p a (h c) -> p a h c", h=nh // 2)

        @block.gpsimd
        def _(pool):
            step = [0]

            def link(ins):
                step[0] += 1
                ins.then_inc(pool_c, 1)
                pool.wait_ge(pool_c, step[0])

            g = nc.gpsimd
            g.memset(zrow[:, :], 0.0).then_inc(zrow_ok, 1)
            g.memset(nhalf[:, :], -0.5)
            link(g.memset(ident[:, :], 0.0))
            link(g.affine_select(out=ident[:, :], in_=ident[:, :], compare_op=ALU.not_equal, fill=1.0, base=0,
                                 pattern=[[-1, P]], channel_multiplier=1))
            g.tensor_copy(ident16[:, :], ident[:, :])
            g.tensor_copy(identb[:, :], ident[:, :])
            link(g.memset(onesb[:, :], 1.0))
            g.affine_select(out=upper[:, :], in_=onesb[:, :], compare_op=ALU.is_ge, fill=0.0, base=0,
                            pattern=[[1, P]], channel_multiplier=-1)
            link(g.memset(causal[:, :], 0.0))
            g.affine_select(out=causal[:, :], in_=causal[:, :], compare_op=ALU.is_ge, fill=MASK, base=0,
                            pattern=[[-1, P]], channel_multiplier=1)
            g.iota(iota8[:, :], pattern=[[1, E]], base=0, channel_multiplier=0, allow_small_or_imprecise_dtypes=True)
            g.iota(iota_t[:, :], pattern=[[1, NTILE1]], base=0, channel_multiplier=0,
                   allow_small_or_imprecise_dtypes=True).then_inc(consts_ok, 1)
            g.memset(w0[:, :, :, 0:1], NEG)
            g.memset(kT[:, :, :, 0:1], NEG)
            g.memset(A2[:, :, :, 0:1], 0.0)
            g.memset(E2[:, :, :, 0:1], 0.0)
            g.memset(EV[:, :, :, 0:1], 0.0)
            g.memset(sw1_sb[:, :, H:HP], 0.0)
            g.memset(sw3_sb[:, :, H:HP], 0.0)
            g.memset(w1_sb[:, :, :, H:HP], 0.0)
            link(g.memset(w3_sb[:, :, :, H:HP], 0.0))
            link(g.memset(sw2_sb[HR:P, HC - 1, :], 0.0))
            g.memset(w2_sb[HR:P, :, HC - 1, :], 0.0).then_inc(pads_ok, 1)
            pool.wait_ge(pads_ok, 1)

            def rstd(n, stage, i0, ni, scale=1.0):
                pool.wait_ge(var_ok, n + 1)
                r = rs[:, stage, i0:i0 + ni]
                link(g.tensor_scalar(r, mv[:, stage, i0:i0 + ni, 1], EPS, None, ALU.add))
                last = g.tensor_tensor(r, r, nhalf[:, 0:ni], ALU.pow)
                if scale != 1.0:
                    link(last)
                    last = g.tensor_scalar(r, r, scale, None, ALU.mult)
                last.then_inc(rstd_ok, 1)

            rstd(0, 0, 0, 4)
            rstd(1, 0, 4, 4)
            pool.wait_ge(small_in, 16 * SMALL)
            for h in range(KC):
                last = g.tensor_copy(w0[:, h, :, 1:SEQ], w_sb[:, h:h + 1].unsqueeze(2).to_broadcast([P, 2, S]))
            last.then_inc(w0_ok, 1)

            pool.wait_ge(bias_in_s, 32)
            src = bias_in[:, :]
            for k in range(3):
                link(g.tensor_copy(bias_p[:, k, :], src))
                if k < 2:
                    link(g.tensor_tensor(bias_r[:, k, :], src, bias_p[:, k, :], ALU.subtract))
                    src = bias_r[:, k, :]
            g.memset(v17[:, :, :, HD:HD + 1], 1.0).then_inc(bias_p_ok, 1)

            def wkv(n):
                p, h = divmod(n, KC)
                b = n % 2
                pool.wait_ge(kT_ok, n + 1)
                pool.wait_ge(o_ok, n + 1)
                if n >= 2:
                    pool.wait_ge(y_ok, n - 1)
                g.tensor_tensor(cur(E2, b), cur(kT, n), cur(O, b), ALU.subtract).then_inc(e2_ok, 1)
                pool.wait_ge(no_ok, n + 1)
                g.tensor_tensor(cur(AA, b), prev(O, b), cur(NO, b), ALU.subtract).then_inc(aa_ok, 1)
                pool.wait_ge(vT_ok, n + 1)
                pool.wait_ge(e2_exp, n + 1)
                g.tensor_tensor(cur(EV, b), cur(E2, b), vT[:, n], ALU.mult).then_inc(ev_ok, 1)
                pool.wait_ge(ee_exp, n + 1)
                pool.wait_ge(aa_ok, n + 1)
                g.tensor_tensor(cur(T2, b), cur(EE, b), vT[:, n], ALU.mult).then_inc(t2_ok, 1)

            def values(i):
                g.tensor_copy(v17[:, i, :, 0:HD], ctx_sb[:, i, :].rearrange("p (h c) -> p h c", h=HEADS)).then_inc(v17_ok, 1)

            wkv(0)
            pool.wait_ge(ctx_in_s[0], 16)
            wkv(1)
            for i in range(4):
                values(i)
            wkv(2)
            rstd(2, 1, 0, 4)
            wkv(3)
            pool.wait_ge(ctx_in_s[1], 16)
            for i in range(4, 8):
                values(i)

            def scatter0(p):
                pool.wait_ge(zero_out, 16 * 9)
                pool.wait_ge(idx0_ok, p + 1)
                for i in range(4 * p, 4 * p + 4):
                    g.indirect_dma_start(
                        out=disp0[:, :], out_offset=bass.IndirectOffsetOnAxis(ap=sidx[:, 0, i:i + 1], axis=0),
                        in_=xn[:, i, :], in_offset=None, bounds_check=E * CAP - 1, oob_is_err=False,
                    ).then_inc(disp0_in, 16)

            scatter0(0)
            rstd(3, 1, 4, 4)
            scatter0(1)

            pool.wait_ge(sho_ps, NP2)
            for t in range(NT):
                c = ctx_sb[:, t, :].rearrange("p (h c) -> p h c", h=HEADS)
                dst = spl[:, t % 2]
                if t >= 2:
                    pool.wait_ge(misc_ps, t - 1)
                for s in (0, 2):
                    last = g.tensor_copy(dst[:, :, s, :], c)
                link(last)
                for s in (1, 3):
                    last = g.tensor_tensor(dst[:, :, s, :], c, dst[:, :, 0, :], ALU.subtract)
                last.then_inc(k_lo, 1)
            link(g.memset(sel[0:HEADS, :, :], 1.0))
            g.affine_select(out=sel[0:HEADS, :, :], in_=sel[0:HEADS, :, :], compare_op=ALU.is_equal, fill=0.0, base=0,
                            pattern=[[-1, HEADS], [0, P]], channel_multiplier=1).then_inc(sel_ok, 1)

            pool.wait_ge(made0_in, 16 * E)
            for i in range(NT):
                if i == 0:
                    pool.wait_ge(xdT_ps, E)
                g.indirect_dma_start(
                    out=got0[:, i, :], out_offset=None, in_=made0[:, :],
                    in_offset=bass.IndirectOffsetOnAxis(ap=gidx[:, 0, i:i + 1], axis=0),
                ).then_inc(got0_in[i // 2], 16)

            for b in range(B):
                rstd(4 + b, 2, 2 * b, 2, scale=float(HD) ** -0.5)

            def q_low(b):
                for j in range(TPB):
                    i = 2 * b + j
                    q = xn[:, i, :].rearrange("p (h c) -> p h c", h=HEADS)
                    pool.wait_ge(q_hi, i + 1)
                    for s in (2, 3):
                        last = g.tensor_tensor(spl[:, i % 2, :, s, :], q, spl[:, i % 2, :, 0, :], ALU.subtract)
                    last.then_inc(q_lo, 1)

            def causal_fill(u):
                for s in range(3):
                    pool.wait_ge(st_exp, 3 * u + s + 1)
                    nh = 4 if s < 2 else 8
                    v = pT[:, u % 2, s, :].rearrange("p (h c) -> p h c", h=nh)[:, :, 0:P]
                    g.affine_select(out=v, in_=v, compare_op=ALU.is_ge, fill=0.0, base=0,
                                    pattern=[[0, nh], [1, P]], channel_multiplier=-1).then_inc(causal_ok, 1)

            def scatter1(b):
                pool.wait_ge(idx1_ok, b + 1)
                for i in range(2 * b, 2 * b + 2):
                    for k in range(2):
                        g.indirect_dma_start(
                            out=disp1[:, :], out_offset=bass.IndirectOffsetOnAxis(ap=sidx[:, k, i:i + 1], axis=0),
                            in_=xn[:, i, :], in_offset=None, bounds_check=E * T - 1, oob_is_err=False,
                        ).then_inc(disp1_in, 16)

            q_low(0)
            for u in range(2 * B):
                if u % 2 == 0 and u // 2 + 1 < B:
                    q_low(u // 2 + 1)
                causal_fill(u)
                if u % 2 == 0 and u >= 2:
                    rstd(8 + u // 2 - 1, 3, u - 2, 2)
                if u % 2 == 0 and u >= 4:
                    scatter1((u - 4) // 2)
            scatter1(2)
            rstd(11, 3, 6, 2)
            scatter1(3)

            pool.wait_ge(gidx1_ok, 1)
            for c in range(4):
                pool.wait_ge(made1_in[c], 16 * len(range(c, NTILE1, 4)))
            for i in range(NT):
                for k in range(2):
                    g.indirect_dma_start(
                        out=got1[:, k, i, :], out_offset=None, in_=made1[:, :],
                        in_offset=bass.IndirectOffsetOnAxis(ap=gidx[:, k, i:i + 1], axis=0),
                    ).then_inc(got1_in[i // 2], 16)
            for b in range(B):
                pool.wait_ge(got1_in[b], 16 * 4)

        USES = [("k", t) for t in range(NT)] + [("q", 0), ("q", 1)]
        for u in range(2 * B + 1):
            if u % 2 == 0 and u < 2 * B:
                USES.append(("m", u // 2))
                if u // 2 + 1 < B:
                    USES += [("q", u + 2), ("q", u + 3)]
            if u % 2 == 1 and u >= 3:
                USES += [("x", (u - 3) // 2), ("l", (u - 3) // 2)]
            if u % 2 == 0 and u >= 4:
                USES.append(("c", (u - 4) // 2))
        USES += [("x", B - 1), ("l", B - 1), ("c", B - 1), ("n", 0)]
        USE = {key: n for n, key in enumerate(USES)}

        @block.scalar
        def _(act):
            a = nc.scalar
            act.dma_start(gates[:, 0:2], g_xattn.partition_broadcast(P)).then_inc(small_in, 16)
            act.dma_start(gates[:, 2:4], g_ffn.partition_broadcast(P)).then_inc(small_in, 16)
            act.dma_start(w_sb[:, :], wkv_w.rearrange("(k p) -> p k", p=P), allow_slow_non_contiguous=True).then_inc(small_in, 16)
            act.dma_start(u_sb[:, :], wkv_u.rearrange("(k p) -> p k", p=P), allow_slow_non_contiguous=True).then_inc(small_in, 16)
            act.dma_start(rb_sb[:, :], router_b.partition_broadcast(P)).then_inc(small_in, 16)
            for k in range(KC):
                act.dma_start(rw_sb[:, k, :], router_w[:, k * P:(k + 1) * P].rearrange("e p -> p e"), allow_slow_non_contiguous=True).then_inc(small_in, 16)
            GB = E * GU // P
            act.dma_start(bias_in[:, 0:GB], gate_up_b.rearrange("e j -> (e j)").rearrange("(p c) -> p c", p=P)).then_inc(bias_in_s, 16)
            act.dma_start(bias_in[:, GB:], down_b.rearrange("e j -> (e j)").rearrange("(p c) -> p c", p=P)).then_inc(bias_in_s, 16)
            act.wait_ge(zrow_ok, 1)
            zsrc = zrow[:, :].unsqueeze(1).to_broadcast([P, 4, 512])
            for n in range(9):
                dst = disp0[:, :] if n == 0 else disp1[(n - 1) * T:n * T, :]
                act.dma_start(dst.rearrange("(p r) d -> p (r d)", p=P).rearrange("p (a c) -> p a c", c=512), zsrc).then_inc(zero_out, 16)
            act.wait_ge(small_in, 16 * SMALL)
            a.activation(tg[:, :], gates[:, :], ACT.Tanh).then_inc(tg_ok, 1)

            def evac(dst, src, ready, n, done):
                act.wait_ge(ready, n)
                a.activation(dst, src, ACT.Copy).then_inc(done, 1)

            def kv(n):
                if n == 0:
                    act.wait_ge(pads_ok, 1)
                evac(cur(kT, n), ps[:, n % 2, :].rearrange("p (a t) -> p a t", a=2), kT_ps, n + 1, kT_ok)
                evac(vT[:, n], ps[:, 2 + n % 2, :].rearrange("p (a t) -> p a t", a=2), vT_ps, n + 1, vT_ok)

            def exps(n):
                for buf, ready, done in ((A2, a2_ok, a2_exp), (E2, e2_ok, e2_exp), (EE, ee_ok, ee_exp), (AA, aa_ok, aa_exp)):
                    act.wait_ge(ready, n + 1)
                    a.activation(cur(buf, n % 2), cur(buf, n % 2), ACT.Exp).then_inc(done, 1)

            kv(0)
            kv(1)
            act.wait_ge(bias_p_ok, 1)
            for k in range(3):
                act.dma_start(bias3[k:k + 1, 0:E * GU], bias_p[:, k, 0:GB]).then_inc(bias_rows, 16)
                act.dma_start(bias3[k:k + 1, E * GU:], bias_p[:, k, GB:]).then_inc(bias_rows, 16)
            exps(0)
            kv(2)
            exps(1)
            kv(3)
            exps(2)
            exps(3)

            def x1_evac(p):
                for h in range(KC):
                    evac(xT[:, h, 512 * p:512 * p + 512], ps[:, h, :], x1T_ps, 2 * p + h + 1, x1T_ok)

            def ex0(p):
                act.wait_ge(ex0_in, p + 1)
                a.activation(pe_[:, 4 * p:4 * p + 4, :], pe_[:, 4 * p:4 * p + 4, :], ACT.Exp).then_inc(ex0_ok, 1)

            def sh_tanh(p):
                for m in range(HC):
                    n = HC * p + m
                    act.wait_ge(sh_ps, n + 1)
                    if n >= 2:
                        act.wait_ge(sh_ok, n - 1)
                    a.activation(thb[:, n % 2, :], ps[:, 2 * (m % 2), :], ACT.Tanh, scale=0.5).then_inc(sh_th, 1)

            for p in range(NP2):
                x1_evac(p)
                ex0(p)
                sh_tanh(p)

            def k_evac(t):
                b, j = divmod(t, TPB)
                act.wait_ge(misc_ps, t + 1)
                a.activation(ktb[:, b, :, j * P:(j + 1) * P], ps16(7), ACT.Copy).then_inc(misc_free, 1)

            for t in range(NT):
                k_evac(t)

            def xd_evac(e):
                act.wait_ge(xdT_ps, e + 1)
                a.activation(xdT[:, e % 2], ps[:, e % 2, 0:D].rearrange("p (k t) -> p k t", k=KC), ACT.Copy).then_inc(xdT_ok, 1)

            def h_tanh(e):
                act.wait_ge(h0_ps, e + 1)
                a.activation(the[:, e % 2, :], ps[:, 2 + 2 * (e % 2), 0:HP], ACT.Tanh, scale=0.5).then_inc(h0_th, 1)

            def oe_evac(e):
                act.wait_ge(oe0_ps, e + 1)
                a.activation(made_sb[:, e, :], ps[:, 6 + e % 2, 0:D], ACT.Copy).then_inc(oe0_ok, 1)

            xd_evac(0)
            xd_evac(1)
            h_tanh(0)
            for e in range(E):
                if e + 2 < E:
                    xd_evac(e + 2)
                if e + 1 < E:
                    h_tanh(e + 1)
                oe_evac(e)

            def misc_evac(key, dst, src):
                n = USE[key]
                act.wait_ge(misc_ps, n + 1)
                a.activation(dst, src, ACT.Copy).then_inc(misc_free, 1)

            def q_split(b):
                for j in range(TPB):
                    i = 2 * b + j
                    act.wait_ge(xn_ok, 2 * NT + i + 1)
                    act.wait_ge(misc_ps, USE[("q", i - 2)] + 1 if i >= 2 else NT)
                    q = xn[:, i, :].rearrange("p (h c) -> p h c", h=HEADS).unsqueeze(2).to_broadcast([P, HEADS, 2, HD])
                    a.activation(spl[:, i % 2, :, 0:2, :], q, ACT.Copy).then_inc(q_hi, 1)

            def q_evac(b):
                for j in range(TPB):
                    misc_evac(("q", 2 * b + j), qtb[:, b % 2, :, j * P:(j + 1) * P], ps16(7))

            def exp_t(u):
                for s in range(3):
                    n = 3 * u + s
                    act.wait_ge(st_ps, n + 1)
                    if u >= 2 and s == 0:
                        act.wait_ge(pv_ps, u - 1)
                    nh = 4 if s < 2 else 8
                    src = sub_cols(ps[:, 2 + 2 * (n % 2):4 + 2 * (n % 2), :], nh)
                    dst = pT[:, u % 2, s, :].rearrange("p (h a c) -> p a h c", a=2, h=nh // 2)
                    a.activation(dst, src, ACT.Exp).then_inc(st_exp, 1)

            def ex1(b):
                act.wait_ge(ex1_in, b + 1)
                a.activation(ssum[:, 2 * b:2 * b + 2], ssum[:, 2 * b:2 * b + 2], ACT.Exp).then_inc(ex1_ok, 1)

            def x_evac(b):
                misc_evac(("x", b), xrT[:, :, :], ps[:, 7, :].rearrange("p (k t) -> p k t", k=KC))

            q_split(0)
            q_evac(0)
            for u in range(2 * B):
                if u % 2 == 0:
                    b = u // 2
                    misc_evac(("m", b), mT[0:HEADS, b % 2, :], ps[0:HEADS, 7, 0:S // 2].bitcast(BF16))
                    if b + 1 < B:
                        q_split(b + 1)
                        q_evac(b + 1)
                exp_t(u)
                if u % 2 == 1 and u >= 3:
                    x_evac((u - 3) // 2)
                    ex1((u - 3) // 2)
            x_evac(B - 1)
            ex1(B - 1)

            def xt_evac(t):
                evac(xtT[:, t % 2], ps[:, t % 2, 0:D].rearrange("p (k t) -> p k t", k=KC), xtT_ps, t + 1, xtT_ok)

            def tile_tanh(t):
                act.wait_ge(gh_ok, t + 1)
                a.activation(th1[:, t % 2, :], gh[:, t % 2, :], ACT.Tanh, scale=1.702).then_inc(th1_ok, 1)

            def at_evac(t):
                evac(actT[:, t % 2], ps[:, 4 + t % 2, 0:I].rearrange("p (k t) -> p k t", k=KC), actT_ps, t + 1, actT_ok)

            def mk_evac(t):
                if t >= 4:
                    act.wait_ge(made1_in[t % 4], 16 * (t // 4))
                evac(mk1[:, t % 4, :], ps[:, 6 + t % 2, 0:D], oe1_ps, t + 1, mk1_ok)

            def mk_store(t):
                act.wait_ge(mk1_ok, t + 1)
                act.dma_start(made1[t * P:(t + 1) * P, :], mk1[:, t % 4, :]).then_inc(made1_in[t % 4], 16)

            xt_evac(0)
            xt_evac(1)
            tile_tanh(0)
            for t in range(NTILE1):
                if t + 2 < NTILE1:
                    xt_evac(t + 2)
                if t + 1 < NTILE1:
                    tile_tanh(t + 1)
                at_evac(t)
                if t >= 1:
                    mk_evac(t - 1)
                if t >= 2:
                    mk_store(t - 2)
            mk_evac(NTILE1 - 1)
            mk_store(NTILE1 - 2)
            mk_store(NTILE1 - 1)

        @block.vector
        def _(dve):
            v = nc.vector
            step = [0]

            def link(ins):
                step[0] += 1
                ins.then_inc(v_chain, 1)
                dve.wait_ge(v_chain, step[0])

            def stats(n, stage, i0, ni):
                for i in range(i0, i0 + ni):
                    link(v.bn_stats(st[:, stage, i, :], x_sb[:, i, :]))
                for i in range(i0, i0 + ni):
                    last = v.bn_aggr(mv[:, stage, i, :], st[:, stage, i, :])
                last.then_inc(var_ok, 1)

            def normal(n, stage, i0, ni):
                dve.wait_ge(var_ok, n + 1)
                dve.wait_ge(rstd_ok, n + 1)
                for i in range(i0, i0 + ni):
                    v.tensor_scalar(xn[:, i, :], x_sb[:, i, :], mv[:, stage, i, 0:1], rs[:, stage, i:i + 1],
                                    ALU.subtract, ALU.mult).then_inc(xn_ok, 1)

            for p in range(NP2):
                dve.wait_ge(x_in[p], 16)
                stats(p, 0, 4 * p, 4)
            for p in range(NP2):
                normal(p, 0, 4 * p, 4)

            dve.wait_ge(w0_ok, 1)

            def head(n):
                p, h = divmod(n, KC)
                b = n % 2
                dve.wait_ge(kT_ok, n + 1)
                v.tensor_tensor_scan(flat(O, b), flat(w0, h), flat(kT, n), NEG, ALU.add, ALU.max).then_inc(o_ok, 1)
                dve.wait_ge(o_ok, n + 1)
                v.scalar_tensor_tensor(cur(A2, b), prev(O, b), w_sb[:, h:h + 1], cur(O, b), ALU.add, ALU.subtract).then_inc(a2_ok, 1)
                v.scalar_tensor_tensor(cur(NO, b), cur(kT, n), u_sb[:, h:h + 1], prev(O, b), ALU.add, ALU.max).then_inc(no_ok, 1)
                dve.wait_ge(no_ok, n + 1)
                if n >= 2:
                    dve.wait_ge(t2_ok, n - 1)
                v.scalar_tensor_tensor(cur(EE, b), cur(kT, n), u_sb[:, h:h + 1], cur(NO, b), ALU.add, ALU.subtract).then_inc(ee_ok, 1)

            def tail(n):
                b = n % 2
                dve.wait_ge(a2_exp, n + 1)
                dve.wait_ge(e2_exp, n + 1)
                dve.wait_ge(ev_ok, n + 1)
                link(v.tensor_tensor_scan(flat(QQ, b), flat(A2, b), flat(E2, b), 0.0, ALU.mult, ALU.add))
                link(v.tensor_tensor_scan(flat(PP, b), flat(A2, b), flat(EV, b), 0.0, ALU.mult, ALU.add))
                dve.wait_ge(aa_exp, n + 1)
                if n >= 2:
                    dve.wait_ge(yT_ps, n // 2)
                link(v.tensor_tensor(cur(T1, b), cur(AA, b), prev(PP, b), ALU.mult))
                link(v.tensor_tensor(cur(AA, b), cur(AA, b), prev(QQ, b), ALU.mult))
                dve.wait_ge(ee_exp, n + 1)
                link(v.tensor_tensor(cur(AA, b), cur(AA, b), cur(EE, b), ALU.add))
                dve.wait_ge(t2_ok, n + 1)
                link(v.tensor_tensor(cur(T1, b), cur(T1, b), cur(T2, b), ALU.add))
                link(v.reciprocal(cur(AA, b), cur(AA, b)))
                v.tensor_tensor(cur(T1, b), cur(T1, b), cur(AA, b), ALU.mult).then_inc(y_ok, 1)
                dve.wait_ge(y_ok, n + 1)

            def residual(p, gate, ready, n, done):
                dve.wait_ge(ready, n)
                dve.wait_ge(tg_ok, 1)
                for k in range(2):
                    xs = x_sb[:, 4 * p + 2 * k:4 * p + 2 * k + 2, :].rearrange("p i d -> p (i d)")
                    last = v.scalar_tensor_tensor(xs, ps[:, 4 + k, :], tg[:, gate:gate + 1], xs, ALU.mult, ALU.add)
                    if k == 0:
                        link(last)
                last.then_inc(done, 1)

            def choose(i, src):
                link(v.max(mx[:, i, :], src))
                v.max_index(ix[:, i, :], mx[:, i, :], src).then_inc(v_chain, 1)
                step[0] += 1

            def route0(p):
                i0 = 4 * p
                sl = slice(i0, i0 + 4)
                dve.wait_ge(lg0_ps, p + 1)
                v.tensor_copy(lg[:, sl, :], ps[:, 6, 0:4 * E].rearrange("p (i e) -> p i e", e=E)).then_inc(lg0_ok, 1)
                dve.wait_ge(lg0_ok, p + 1)
                for i in range(i0, i0 + 4):
                    choose(i, lg[:, i, :])
                dve.wait_ge(v_chain, step[0])
                v.tensor_tensor(pe_[:, sl, :], lg[:, sl, :], mx[:, sl, 0:1].to_broadcast([P, 4, E]), ALU.subtract).then_inc(ex0_in, 1)
                link(v.tensor_copy(ixf[:, sl, 0:1], ix[:, sl, 0:1]))
                link(v.tensor_tensor(oh[:, 0, sl, :], iota8[:, :].unsqueeze(1).to_broadcast([P, 4, E]),
                                     ixf[:, sl, 0:1].to_broadcast([P, 4, E]), ALU.is_equal))
                v.tensor_copy(ohb[:, sl, :], oh[:, 0, sl, :]).then_inc(oh0_ok, 1)

            def slots0(p):
                i0 = 4 * p
                sl = slice(i0, i0 + 4)
                dve.wait_ge(cum0_ps, p + 1)
                v.tensor_tensor(cumoh[:, 0, sl, :], ps[:, 7, 0:4 * E].rearrange("p (i e) -> p i e", e=E), oh[:, 0, sl, :],
                                ALU.mult).then_inc(cum0_ok, 1)
                dve.wait_ge(cum0_ok, p + 1)
                link(v.reduce_sum(pos[:, 0, sl], cumoh[:, 0, sl, :], AXX))
                link(v.tensor_scalar(keep[:, sl], pos[:, 0, sl], float(CAP), None, ALU.is_le))
                link(v.tensor_scalar(slotf[:, 0, sl], ixf[:, sl, 0], float(CAP), FAR - 1.0, ALU.mult, ALU.add))
                link(v.tensor_tensor(slotf[:, 0, sl], slotf[:, 0, sl], pos[:, 0, sl], ALU.add))
                link(v.scalar_tensor_tensor(slotf[:, 0, sl], keep[:, sl], -FAR, slotf[:, 0, sl], ALU.mult, ALU.add))
                link(v.tensor_copy(sidx[:, 0, sl], slotf[:, 0, sl]))
                link(v.tensor_scalar(gidx[:, 0, sl], slotf[:, 0, sl], float(E * CAP - 1), None, ALU.min))
                dve.wait_ge(ex0_ok, p + 1)
                link(v.reduce_sum(ssum[:, sl], pe_[:, sl, :], AXX))
                link(v.reciprocal(ssum[:, sl], ssum[:, sl]))
                v.scalar_tensor_tensor(coef[:, 0, sl], ssum[:, sl], tg[:, 2:3], keep[:, sl], ALU.mult, ALU.mult).then_inc(idx0_ok, 1)

            def swiglu_shared(p, m):
                n = HC * p + m
                dve.wait_ge(sh_th, n + 1)
                if m == 0 and p > 0:
                    dve.wait_ge(sho_ps, p)
                t = thb[:, n % 2, :]
                link(v.scalar_tensor_tensor(t, t, 1.0, ps[:, 2 * (m % 2), :], ALU.add, ALU.mult))
                v.scalar_tensor_tensor(hT[:, m, :], t, 0.5, ps[:, 2 * (m % 2) + 1, :], ALU.mult, ALU.mult).then_inc(sh_ok, 1)

            head(0)
            head(1)
            tail(0)
            head(2)
            tail(1)
            head(3)
            residual(0, 0, yT_ps, 1, x1_ok)
            dve.wait_ge(x1_ok, 1)
            stats(2, 1, 0, 4)
            normal(2, 1, 0, 4)
            tail(2)
            route0(0)
            tail(3)
            for m in range(HC):
                swiglu_shared(0, m)
            slots0(0)
            residual(0, 2, sho_ps, 1, xs_ok)
            residual(1, 0, yT_ps, 2, x1_ok)
            dve.wait_ge(x1_ok, 2)
            stats(3, 1, 4, 4)
            normal(3, 1, 4, 4)
            route0(1)
            slots0(1)
            for m in range(HC):
                swiglu_shared(1, m)
            residual(1, 2, sho_ps, 2, xs_ok)
            dve.wait_ge(xs_ok, 2)

            for e in range(E):
                dve.wait_ge(h0_th, e + 1)
                t = the[:, e % 2, :]
                b = 2 + 2 * (e % 2)
                link(v.scalar_tensor_tensor(t, t, 1.0, ps[:, b, 0:HP], ALU.add, ALU.mult))
                v.scalar_tensor_tensor(he[:, e % 2, :], t, 0.5, ps[:, b + 1, 0:HP], ALU.mult, ALU.mult).then_inc(h0_ok, 1)

            for b in range(B):
                dve.wait_ge(got0_in[b], 32)
                for i in range(2 * b, 2 * b + 2):
                    link(v.scalar_tensor_tensor(x_sb[:, i, :], got0[:, i, :], coef[:, 0, i:i + 1], x_sb[:, i, :], ALU.mult, ALU.add))
                stats(4 + b, 2, 2 * b, 2)
            for b in range(B):
                normal(4 + b, 2, 2 * b, 2)

            def nat_max(b, s):
                n = 6 * b + s
                h0, nh, qt = NAT[s]
                dve.wait_ge(nat_ps, n + 1)
                v.reduce_max(mmax[:, b % 2, qt, h0:h0 + nh].rearrange("p (h a) -> p a h", a=2),
                             sub_cols(ps[:, 0:2, :], nh), AXX).then_inc(nat_ok, 1)
                if s == 5:
                    dve.wait_ge(nat_ok, 6 * b + 6)
                    v.tensor_scalar(mneg[:, b % 2], mmax[:, b % 2], -1.0, None, ALU.mult).then_inc(mneg_ok, 1)

            def attend(u):
                b, hg = divmod(u, 2)
                dve.wait_ge(pv_ps, u + 1)
                o = ps[:, 6, 0:2 * 8 * (HD + 1)].rearrange("p (q h c) -> p q h c", q=2, h=8)
                r = den[:, u % 2]
                link(v.reciprocal(r, o[:, :, :, HD]))
                link(v.tensor_scalar(r, r, tg[:, 1:2], None, ALU.mult))
                v.tensor_tensor(att[:, u % 2], o[:, :, :, 0:HD], r.unsqueeze(3).to_broadcast([P, 2, 8, HD]), ALU.mult).then_inc(pv_ok, 1)
                dve.wait_ge(pv_ok, u + 1)
                xs = x_sb[:, 2 * b:2 * b + 2, hg * P:(hg + 1) * P]
                link(v.tensor_tensor(xs, xs, att[:, u % 2].rearrange("p q h c -> p q (h c)"), ALU.add))

            def norm3(b):
                stats(8 + b, 3, 2 * b, 2)
                normal(8 + b, 3, 2 * b, 2)

            def route1(b):
                sl = slice(2 * b, 2 * b + 2)
                n = USE[("l", b)]
                dve.wait_ge(misc_ps, n + 1)
                v.tensor_tensor(lg[:, sl, :], ps[:, 7, 0:2 * E].rearrange("p (i e) -> p i e", e=E),
                                rb_sb[:, :].unsqueeze(1).to_broadcast([P, 2, E]), ALU.add).then_inc(misc_free, 1)
                dve.wait_ge(misc_free, n + 1)
                for i in range(2 * b, 2 * b + 2):
                    choose(i, lg[:, i, :])
                dve.wait_ge(v_chain, step[0])
                v.tensor_tensor(ssum[:, sl], mx[:, sl, 1], mx[:, sl, 0], ALU.subtract).then_inc(ex1_in, 1)
                link(v.tensor_copy(ixf[:, sl, :], ix[:, sl, 0:2]))
                for k in range(2):
                    link(v.tensor_tensor(oh[:, k, sl, :], iota8[:, :].unsqueeze(1).to_broadcast([P, 2, E]),
                                         ixf[:, sl, k:k + 1].to_broadcast([P, 2, E]), ALU.is_equal))
                v.tensor_tensor(ohb[:, sl, :], oh[:, 0, sl, :], oh[:, 1, sl, :], ALU.add).then_inc(oh1_ok, 1)

            def slots1(b):
                sl = slice(2 * b, 2 * b + 2)
                n = USE[("c", b)]
                cum = ps[:, 7, 0:2 * E].rearrange("p (i e) -> p i e", e=E)
                dve.wait_ge(misc_ps, n + 1)
                link(v.tensor_tensor(cumoh[:, 0, sl, :], cum, oh[:, 0, sl, :], ALU.mult))
                v.tensor_tensor(cumoh[:, 1, sl, :], cum, oh[:, 1, sl, :], ALU.mult).then_inc(misc_free, 1)
                dve.wait_ge(misc_free, n + 1)
                link(v.reduce_sum(pos[:, :, sl], cumoh[:, :, sl, :], AXX))
                for k in range(2):
                    link(v.scalar_tensor_tensor(slotf[:, k, sl], ixf[:, sl, k], float(T), pos[:, k, sl], ALU.mult, ALU.add))
                v.tensor_scalar(sidx[:, :, sl], slotf[:, :, sl], -1.0, None, ALU.add).then_inc(idx1_ok, 1)
                dve.wait_ge(ex1_ok, b + 1)
                link(v.tensor_scalar(keep[:, sl], ssum[:, sl], 1.0, None, ALU.add))
                link(v.reciprocal(keep[:, sl], keep[:, sl]))
                link(v.tensor_scalar(coef[:, 0, sl], keep[:, sl], tg[:, 3:4], None, ALU.mult))
                link(v.tensor_tensor(coef[:, 1, sl], coef[:, 0, sl], ssum[:, sl], ALU.mult))

            for s in range(6):
                nat_max(0, s)
            for u in range(2 * B):
                for s in range(3):
                    if u // 2 + 1 < B:
                        nat_max(u // 2 + 1, 3 * (u % 2) + s)
                if u >= 1:
                    attend(u - 1)
                if u % 2 == 0 and u >= 2:
                    norm3(u // 2 - 1)
                if u % 2 == 1 and u >= 3:
                    route1((u - 3) // 2)
                if u % 2 == 0 and u >= 4:
                    slots1((u - 4) // 2)
            attend(2 * B - 1)
            slots1(B - 2)
            norm3(B - 1)
            route1(B - 1)
            slots1(B - 1)

            dve.wait_ge(misc_ps, USE[("n", 0)] + 1)
            v.tensor_copy(cnt[:, 0, :], ps[:, 7, 0:E]).then_inc(misc_free, 1)
            dve.wait_ge(misc_free, USE[("n", 0)] + 1)
            link(v.tensor_scalar(cnt[:, 1, :], cnt[:, 0, :], 1.0 / P, (P - 1.0) / P - 0.5 + 1.0 / 512, ALU.mult, ALU.add))
            link(v.tensor_copy(nti[:, :], cnt[:, 1, :]))
            link(v.tensor_copy(cnt[:, 1, :], nti[:, :]))
            link(v.memset(cnt[:, 0, :], 1.0))
            link(v.tensor_tensor_scan(cnt[:, 2, :], cnt[:, 0, :], cnt[:, 1, :], 0.0, ALU.mult, ALU.add))
            ends = cnt[:, 2, :].unsqueeze(1).to_broadcast([P, NTILE1, E])
            link(v.tensor_tensor(tle[:, 0], ends, iota_t[:, :].unsqueeze(2).to_broadcast([P, NTILE1, E]), ALU.is_le))
            link(v.tensor_tensor(tle[:, 1], tle[:, 0], ends, ALU.mult))
            link(v.reduce_sum(tabf[:, 0, :], tle[:, 0], AXX))
            link(v.reduce_max(tabf[:, 1, :], tle[:, 1], AXX))
            link(v.tensor_tensor(tabf[:, 1, :], iota_t[:, :], tabf[:, 1, :], ALU.subtract))
            link(v.tensor_scalar(tabf[:, 2, :], tabf[:, 0, :], float(T), None, ALU.mult))
            link(v.scalar_tensor_tensor(tabf[:, 2, :], tabf[:, 1, :], float(P), tabf[:, 2, :], ALU.mult, ALU.add))
            link(v.tensor_scalar(tabi[:, 0, :], tabf[:, 0, :], float(E - 1), None, ALU.min))
            v.tensor_scalar(tabi[:, 1, :], tabf[:, 2, :], float(E * T - P), None, ALU.min).then_inc(tab_ok, 1)
            link(v.tensor_tensor(cnt[:, 3, :], cnt[:, 2, :], cnt[:, 1, :], ALU.subtract))
            link(v.tensor_scalar(cnt[:, 3, :], cnt[:, 3, :], float(P), None, ALU.mult))
            for k in range(2):
                link(v.tensor_tensor(oh[:, k], oh[:, k], cnt[:, 3, :].unsqueeze(1).to_broadcast([P, NT, E]), ALU.mult))
            link(v.reduce_sum(slotf[:, :, :], oh[:, :, :, :], AXX))
            link(v.tensor_tensor(slotf[:, :, :], slotf[:, :, :], pos[:, :, :], ALU.add))
            v.tensor_scalar(gidx[:, :, :], slotf[:, :, :], -1.0, None, ALU.add).then_inc(gidx1_ok, 1)

            def clip(t):
                b = t % 2
                g = ps[:, 2 + b, :].rearrange("p (i c) -> p c i", c=2)
                dve.wait_ge(gu_ps, t + 1)
                v.tensor_scalar(gh[:, b, :], g[:, 0, :], 7.0, 0.5, ALU.min, ALU.mult).then_inc(gh_ok, 1)
                link(v.tensor_scalar(up[:, b, :], g[:, 1, :], -7.0, 7.0, ALU.max, ALU.min))

            def act_tile(t):
                b = t % 2
                dve.wait_ge(gh_ok, t + 1)
                dve.wait_ge(th1_ok, t + 1)
                link(v.scalar_tensor_tensor(glu[:, b, :], th1[:, b, :], 1.0, gh[:, b, :], ALU.add, ALU.mult))
                if t >= 2:
                    dve.wait_ge(actT_ps, t - 1)
                v.scalar_tensor_tensor(actv[:, b, :], up[:, b, :], 1.0, glu[:, b, :], ALU.add, ALU.mult).then_inc(act_ok, 1)

            clip(0)
            act_tile(0)
            for t in range(1, NTILE1):
                clip(t)
                act_tile(t)

            for b in range(B):
                dve.wait_ge(got1_in[b], 64)
                for i in range(2 * b, 2 * b + 2):
                    link(v.scalar_tensor_tensor(x_sb[:, i, :], got1[:, 0, i, :], coef[:, 0, i:i + 1], x_sb[:, i, :], ALU.mult, ALU.add))
                    v.scalar_tensor_tensor(x_sb[:, i, :], got1[:, 1, i, :], coef[:, 1, i:i + 1], x_sb[:, i, :], ALU.mult, ALU.add).then_inc(x4_ok, 1)

        @block.tensor
        def _(pe):
            t_ = nc.tensor

            def mm(o, l, r, start, stop):
                return t_.matmul(o, lhsT=l, rhs=r, start=start, stop=stop)

            pe.wait_ge(consts_ok, 1)
            for n in range(NG):
                p, h = divmod(n, KC)
                if n >= 2:
                    pe.wait_ge(kT_ok, n - 1)
                pe.wait_ge(xn_ok, 4 * p + 4)
                for j in range(4):
                    last = t_.transpose(ps[:, n % 2, j * P:(j + 1) * P], xn[:, 4 * p + j, h * P:(h + 1) * P], ident[:, :])
                last.then_inc(kT_ps, 1)
                if n >= 2:
                    pe.wait_ge(vT_ok, n - 1)
                pe.wait_ge(ctx_in_s[p], 16)
                for j in range(4):
                    last = t_.transpose(ps[:, 2 + n % 2, j * P:(j + 1) * P], ctx_sb[:, 4 * p + j, h * P:(h + 1) * P], ident[:, :])
                last.then_inc(vT_ps, 1)

            def y_back(p):
                pe.wait_ge(y_ok, KC * p + KC)
                if p > 0:
                    pe.wait_ge(xs_ok, p)
                for j in range(4):
                    for h in range(KC):
                        last = t_.transpose(ps[:, 4 + j // 2, (j % 2) * D + h * P:(j % 2) * D + (h + 1) * P],
                                            T1[:, h, j // 2, 1 + (j % 2) * P:1 + (j % 2 + 1) * P], ident[:, :])
                last.then_inc(yT_ps, 1)

            def x1_turn(p):
                pe.wait_ge(xn_ok, NT + 4 * p + 4)
                pe.wait_ge(kT_ok, NG)
                if p > 0:
                    pe.wait_ge(sh_ok, HC * p)
                for h in range(KC):
                    for j in range(4):
                        last = t_.transpose(ps[:, h, j * P:(j + 1) * P], xn[:, 4 * p + j, h * P:(h + 1) * P], ident[:, :])
                    last.then_inc(x1T_ps, 1)

            def logits0(p):
                pe.wait_ge(x1T_ok, KC * (p + 1))
                pe.wait_ge(wg_in, 16)
                if p > 0:
                    pe.wait_ge(lg0_ok, p)
                for j in range(4):
                    for k in range(KC):
                        last = mm(ps[:, 6, j * E:(j + 1) * E], xT[:, k, (4 * p + j) * P:(4 * p + j + 1) * P], wg_sb[:, k, :],
                                  k == 0, k == KC - 1)
                last.then_inc(lg0_ps, 1)

            def shared_up(p, m):
                n = HC * p + m
                pe.wait_ge(sw_in, 64)
                pe.wait_ge(pads_ok, 1)
                pe.wait_ge(vT_ok, NG)
                if n >= 2:
                    pe.wait_ge(sh_ok, n - 1)
                for c, w in enumerate((sw1_sb, sw3_sb)):
                    for k in range(KC):
                        last = mm(ps[:, 2 * (m % 2) + c, :], w[:, k, m * P:(m + 1) * P], xT[:, k, 512 * p:512 * p + 512],
                                  k == 0, k == KC - 1)
                last.then_inc(sh_ps, 1)

            def count(i, j0, o):
                for j in range(i):
                    mm(o, onesb[:, :], ohb[:, j, :], j == 0, False)
                return mm(o, upper[:, :], ohb[:, i, :], i == 0, True)

            def cum0(p):
                pe.wait_ge(oh0_ok, p + 1)
                if p > 0:
                    pe.wait_ge(cum0_ok, p)
                for j in range(4):
                    last = count(4 * p + j, 0, ps[:, 7, j * E:(j + 1) * E])
                last.then_inc(cum0_ps, 1)

            def shared_down(p):
                pe.wait_ge(sh_ok, HC * (p + 1))
                pe.wait_ge(x1_ok, p + 1)
                for j in range(4):
                    for m in range(HC):
                        last = mm(ps[:, 4 + j // 2, (j % 2) * D:(j % 2 + 1) * D], hT[:, m, j * P:(j + 1) * P], sw2_sb[:, m, :],
                                  m == 0, m == HC - 1)
                last.then_inc(sho_ps, 1)

            for p in range(NP2):
                y_back(p)
                x1_turn(p)
                logits0(p)
                shared_up(p, 0)
                if p > 0:
                    cum0(p)
                shared_up(p, 1)
                if p == 0:
                    cum0(p)
                shared_up(p, 2)
                shared_down(p)

            def misc_take(key):
                n = USE[key]
                if n >= 1:
                    pe.wait_ge(misc_free, n)
                else:
                    pe.wait_ge(cum0_ok, NP2)

            for t in range(NT):
                pe.wait_ge(k_lo, t + 1)
                misc_take(("k", t))
                for h in range(NPAIR):
                    last = t_.transpose(ps16(7)[:, h, :], spl[:, t % 2, 2 * h:2 * h + 2, :, :].rearrange("p h s c -> p (h s c)"), ident16[:, :])
                last.then_inc(misc_ps, 1)

            def xd_turn(e):
                if e % 2 == 0:
                    pe.wait_ge(disp0_out[e // 2], 16)
                pe.wait_ge(sh_ok, HC * NP2)
                if e >= 2:
                    pe.wait_ge(xdT_ok, e - 1)
                for k in range(KC):
                    last = t_.transpose(ps[:, e % 2, k * P:(k + 1) * P], xd[:, e, k * P:(k + 1) * P], ident[:, :])
                last.then_inc(xdT_ps, 1)

            def expert_up(e):
                if e % (E // 2) == 0:
                    pe.wait_ge(w1_in[e // (E // 2)], 16 * (E // 2))
                    pe.wait_ge(w3_in[e // (E // 2)], 16 * (E // 2))
                    pe.wait_ge(xs_ok, NP2)
                pe.wait_ge(xdT_ok, e + 1)
                if e >= 2:
                    pe.wait_ge(h0_ok, e - 1)
                for c, w in enumerate((w1_sb, w3_sb)):
                    for m in range(HC):
                        for k in range(KC):
                            last = mm(ps[:, 2 + 2 * (e % 2) + c, m * P:(m + 1) * P], w[:, e, k, m * P:(m + 1) * P], xdT[:, e % 2, k, :],
                                      k == 0, k == KC - 1)
                last.then_inc(h0_ps, 1)

            def expert_down(e):
                pe.wait_ge(h0_ok, e + 1)
                if e == 0:
                    pe.wait_ge(w2_in, 16 * (E + 1))
                    pe.wait_ge(lg0_ok, NP2)
                    pe.wait_ge(misc_free, NT)
                if e >= 2:
                    pe.wait_ge(oe0_ok, e - 1)
                for m in range(HC):
                    last = mm(ps[:, 6 + e % 2, 0:D], he[:, e % 2, m * P:(m + 1) * P], w2_sb[:, e, m, :], m == 0, m == HC - 1)
                last.then_inc(oe0_ps, 1)

            xd_turn(0)
            xd_turn(1)
            expert_up(0)
            for e in range(E):
                if e + 2 < E:
                    xd_turn(e + 2)
                if e + 1 < E:
                    expert_up(e + 1)
                expert_down(e)

            def q_turn(i):
                pe.wait_ge(q_lo, i + 1)
                misc_take(("q", i))
                if i == 0:
                    pe.wait_ge(oe0_ok, E)
                for h in range(NPAIR):
                    last = t_.transpose(ps16(7)[:, h, :], spl[:, i % 2, 2 * h:2 * h + 2, :, :].rearrange("p h s c -> p (h s c)"), ident16[:, :])
                last.then_inc(misc_ps, 1)

            def nat(b, s):
                n = 6 * b + s
                h0, nh, qt = NAT[s]
                if s == 0:
                    pe.wait_ge(misc_free, USE[("q", 2 * b + 1)] + 1)
                if n >= 1:
                    pe.wait_ge(nat_ok, n)
                w = (qt + 1) * P
                for h in range(h0, h0 + nh):
                    r = 64 * (h % 2)
                    o = ps[:, h % 2, (h - h0) // 2 * w:(h - h0) // 2 * w + w]
                    mm(o, qtb[r:r + 64, b % 2, h // 2, qt * P:(qt + 1) * P], ktb[r:r + 64, b, h // 2, 0:w], True, False)
                    last = mm(o[:, w - P:w], identb[:, :], causal[:, :], False, True)
                last.then_inc(nat_ps, 1)

            def scores_t(u, s):
                n = 3 * u + s
                b, hg = divmod(u, 2)
                h0, nh, kt = [(8 * hg, 4, 0), (8 * hg + 4, 4, 0), (8 * hg, 8, 1)][s]
                if s == 0 and hg == 0:
                    pe.wait_ge(misc_free, USE[("m", b)] + 1)
                if n >= 2:
                    pe.wait_ge(st_exp, n - 1)
                w = S - kt * P
                for h in range(h0, h0 + nh):
                    r = 64 * (h % 2)
                    o = ps[:, 2 + 2 * (n % 2) + h % 2, (h - h0) // 2 * w:(h - h0) // 2 * w + w]
                    mm(o, sel[0:HEADS, h, :], mT[0:HEADS, b % 2, kt * P:S], True, False)
                    last = mm(o, ktb[r:r + 64, b, h // 2, kt * P:(kt + 1) * P], qtb[r:r + 64, b % 2, h // 2, kt * P:S], False, True)
                last.then_inc(st_ps, 1)

            def weigh(u):
                b, hg = divmod(u, 2)
                pe.wait_ge(causal_ok, 3 * (u + 1))
                if u >= 1:
                    pe.wait_ge(pv_ok, u)
                for j in range(8):
                    h = 8 * hg + j
                    lo = pT[:, u % 2, j // 4, (j % 4) * S:(j % 4 + 1) * S]
                    hi = pT[:, u % 2, 2, j * P:(j + 1) * P]
                    c = HD + 1
                    mm(ps[:, 6, j * c:(j + 1) * c], lo[:, 0:P], v17[:, 2 * b, h, :], True, True)
                    o = ps[:, 6, (8 + j) * c:(9 + j) * c]
                    mm(o, lo[:, P:S], v17[:, 2 * b, h, :], True, False)
                    last = mm(o, hi, v17[:, 2 * b + 1, h, :], False, True)
                last.then_inc(pv_ps, 1)

            def route_x(b):
                pe.wait_ge(xn_ok, 3 * NT + 2 * b + 2)
                misc_take(("x", b))
                for k in range(KC):
                    for j in range(TPB):
                        last = t_.transpose(ps[:, 7, (k * TPB + j) * P:(k * TPB + j + 1) * P], xn[:, 2 * b + j, k * P:(k + 1) * P], ident[:, :])
                last.then_inc(misc_ps, 1)
                misc_take(("l", b))
                for j in range(TPB):
                    for k in range(KC):
                        last = mm(ps[:, 7, j * E:(j + 1) * E], xrT[:, k, j * P:(j + 1) * P], rw_sb[:, k, :], k == 0, k == KC - 1)
                last.then_inc(misc_ps, 1)

            def route_c(b):
                pe.wait_ge(oh1_ok, b + 1)
                misc_take(("c", b))
                for j in range(TPB):
                    last = count(2 * b + j, 0, ps[:, 7, j * E:(j + 1) * E])
                last.then_inc(misc_ps, 1)

            pe.wait_ge(sel_ok, 1)
            pe.wait_ge(v17_ok, NT)
            pe.wait_ge(bias_p_ok, 1)
            q_turn(0)
            q_turn(1)
            for s in range(6):
                nat(0, s)
            for u in range(2 * B):
                b = u // 2
                if u % 2 == 0:
                    pe.wait_ge(mneg_ok, b + 1)
                    misc_take(("m", b))
                    for q in range(2):
                        last = t_.transpose(ps[0:HEADS, 7, 0:S // 2].bitcast(BF16)[:, q * P:(q + 1) * P], mneg[:, b % 2, q, :], identb[:, :])
                    last.then_inc(misc_ps, 1)
                    if b + 1 < B:
                        q_turn(2 * b + 2)
                        q_turn(2 * b + 3)
                for s in range(3):
                    scores_t(u, s)
                    if b + 1 < B:
                        nat(b + 1, 3 * (u % 2) + s)
                if u >= 1:
                    weigh(u - 1)
                if u % 2 == 1 and u >= 3:
                    route_x((u - 3) // 2)
                if u % 2 == 0 and u >= 4:
                    route_c((u - 4) // 2)
            weigh(2 * B - 1)
            route_c(B - 2)
            route_x(B - 1)
            route_c(B - 1)
            misc_take(("n", 0))
            for j in range(NT):
                last = mm(ps[:, 7, 0:E], onesb[:, :], ohb[:, j, :], j == 0, j == NT - 1)
            last.then_inc(misc_ps, 1)

            pe.wait_ge(tab_ok, 1)
            pe.wait_ge(bias_rows, 96)
            pe.wait_ge(gu_in, 16 * E)
            pe.wait_ge(dn_in, 16 * E)
            ex = {}

            def xt_turn(t):
                pe.wait_ge(xt_in[t % 4], 16 * (t // 4 + 1))
                if t >= 2:
                    pe.wait_ge(xtT_ok, t - 1)
                for k in range(KC):
                    last = t_.transpose(ps[:, t % 2, k * P:(k + 1) * P], xt[:, t % 4, k * P:(k + 1) * P], ident[:, :])
                last.then_inc(xtT_ps, 1)

            def gate_up_tile(t):
                ex[t] = pe.value_load(tabi[0:1, 0, t:t + 1], min_val=0, max_val=E - 1)
                pe.wait_ge(xtT_ok, t + 1)
                if t >= 2:
                    pe.wait_ge(act_ok, t - 1)
                o = ps[:, 2 + t % 2, :]
                mm(o, onesb[0:3, :], bias3[:, bass.ds(ex[t] * GU, GU)], True, False)
                for k in range(KC):
                    last = mm(o, xtT[:, t % 2, k, :], gu_sb[:, bass.ds(ex[t] * (KC * GU) + k * GU, GU)], False, k == KC - 1)
                last.then_inc(gu_ps, 1)

            def act_turn(t):
                pe.wait_ge(act_ok, t + 1)
                if t >= 2:
                    pe.wait_ge(actT_ok, t - 1)
                for k in range(KC):
                    last = t_.transpose(ps[:, 4 + t % 2, k * P:(k + 1) * P], actv[:, t % 2, k * P:(k + 1) * P], ident[:, :])
                last.then_inc(actT_ps, 1)

            def down_tile(t):
                pe.wait_ge(actT_ok, t + 1)
                if t >= 2:
                    pe.wait_ge(mk1_ok, t - 1)
                o = ps[:, 6 + t % 2, 0:D]
                mm(o, onesb[0:3, :], bias3[:, bass.ds(ex[t] * D + E * GU, D)], True, False)
                for k in range(KC):
                    last = mm(o, actT[:, t % 2, k, :], dn_sb[:, bass.ds(ex[t] * (KC * D) + k * D, D)], False, k == KC - 1)
                last.then_inc(oe1_ps, 1)

            xt_turn(0)
            xt_turn(1)
            gate_up_tile(0)
            for t in range(NTILE1):
                if t + 2 < NTILE1:
                    xt_turn(t + 2)
                if t + 1 < NTILE1:
                    gate_up_tile(t + 1)
                act_turn(t)
                if t >= 1:
                    down_tile(t - 1)
            down_tile(NTILE1 - 1)


_INS = ['x', 'ctx_2048', 'g_xattn', 'g_ffn', 'L0_xattn_w', 'L0_xattn_u', 'L0_ffn_Wg', 'L0_ffn_W1', 'L0_ffn_W3', 'L0_ffn_W2',
        'L0_ffn_sw1', 'L0_ffn_sw3', 'L0_ffn_sw2', 'L1_ffn_router_weight', 'L1_ffn_router_bias', 'L1_ffn_gate_up_proj',
        'L1_ffn_gate_up_proj_bias', 'L1_ffn_down_proj', 'L1_ffn_down_proj_bias']


def kernel(**inputs):
    import numpy as np
    import concourse.bacc as bacc
    from concourse.bass_utils import run_bass_kernel_spmd as run

    nc = bacc.Bacc("TRN2", target_bir_lowering=False, num_devices=1)
    arrays, args = {}, []
    for name in _INS:
        a = np.ascontiguousarray(inputs[name])
        arrays[f"in_{name}"] = a
        args.append(nc.dram_tensor(f"in_{name}", a.shape, mybir.dt.from_np(a.dtype), kind="ExternalInput").ap())
    out = nc.dram_tensor("out_x", inputs['x'].shape, FP32, kind="ExternalOutput").ap()
    flamingo_kernel(nc, *args, out)
    r = run(nc, [arrays], core_ids=[0])
    return r.results[0]["out_x"]
```

```python
import concourse.bass as bass
from concourse import mybir
from contextlib import ExitStack

P = 128
FP32 = mybir.dt.float32
FP16 = mybir.dt.float16
BF16 = mybir.dt.bfloat16
U32 = mybir.dt.uint32
I32 = mybir.dt.int32
ALU = mybir.AluOpType
ACT = mybir.ActivationFunctionType
AXX = mybir.AxisListType.X


def flamingo_kernel(nc, x, ctx_in, g_xattn, g_ffn, wkv_w, wkv_u, Wg, W1, W3, W2, sw1, sw3, sw2,
                    router_w, router_b, gate_up, gate_up_b, down, down_b, out):
    B, S, D = x.shape
    T = B * S
    NT = T // P
    TPB = S // P
    KC = D // P
    E = Wg.shape[1]
    H = W1.shape[2]
    HC = -(-H // P)
    HP = HC * P
    HR = H - (HC - 1) * P
    CAP = T // E
    I = down.shape[1]
    GU = 2 * I
    HEADS = 16
    HD = D // HEADS
    NPAIR = HEADS // 2
    NTILE1 = (2 * T) // P + E - 1
    NEG = -1.0e38
    EPS = 1.0e-5
    FAR = 4096.0
    SEQ = S + 1
    NP2 = NT // 4
    NG = NP2 * KC
    MASK = -1.0e30
    NXT = 8
    RW = D + 4
    SMALL = 5 + KC

    x_v = x.rearrange("b s d -> (b s) d").rearrange("(i p) d -> p i d", p=P)
    ctx_v = ctx_in.rearrange("b s d -> (b s) d").rearrange("(i p) d -> p i d", p=P)
    out_v = out.rearrange("b s d -> (b s) d").rearrange("(i p) d -> p i d", p=P)

    disp0 = nc.dram_tensor("disp0", [E * CAP, RW], FP32, kind="Internal").ap()
    made0 = nc.dram_tensor("made0", [T, D], FP32, kind="Internal").ap()
    disp1 = nc.dram_tensor("disp1", [E * T, RW], FP32, kind="Internal").ap()
    made1 = nc.dram_tensor("made1", [2 * T, D], FP32, kind="Internal").ap()

    ctx = ExitStack()
    with ctx:
        def sb(name, shape, dt=FP32):
            return ctx.enter_context(nc.sbuf_tensor(name, shape, dt))

        def sem(name):
            return ctx.enter_context(nc.semaphore(name))

        ident = sb("ident", [P, P])
        ident16 = sb("ident16", [P, P], FP16)
        identb = sb("identb", [P, P], BF16)
        upper = sb("upper", [P, P], BF16)
        onesb = sb("onesb", [P, P], BF16)
        causal = sb("causal", [P, P], BF16)
        causalT = sb("causalT", [P, P], BF16)
        iota8 = sb("iota8", [P, E])
        iota_t = sb("iota_t", [P, NTILE1])
        nhalf = sb("nhalf", [P, NT])
        zrow = sb("zrow", [P, 2 * RW])
        ids = sb("ids", [P, 2, NT], U32)
        gates = sb("gates", [P, 4])
        tg = sb("tg", [P, 4])
        w_sb = sb("w_sb", [P, KC])
        u_sb = sb("u_sb", [P, KC])
        wg_sb = sb("wg_sb", [P, KC, E])
        rw_sb = sb("rw_sb", [P, KC, E])
        rb_sb = sb("rb_sb", [P, E])
        NB = E * (GU + D)
        bias_in = sb("bias_in", [P, NB // P])
        bias_r = sb("bias_r", [P, 2, NB // P])
        bias_p = sb("bias_p", [P, 3, NB // P], BF16)
        bias3 = sb("bias3", [P, NB], BF16)
        st = sb("st", [P, 4, NT, 6])
        mv = sb("mv", [P, 4, NT, 2])
        rs = sb("rs", [P, 4, NT])
        lg = sb("lg", [P, NT, E])
        mx = sb("mx", [P, NT, E])
        ix = sb("ix", [P, NT, E], U32)
        ixf = sb("ixf", [P, NT, 2])
        pe_ = sb("pe_", [P, NT, E])
        oh = sb("oh", [P, 2, NT, E])
        ohb = sb("ohb", [P, NT, E], BF16)
        cumoh = sb("cumoh", [P, 2, NT, E])
        ssum = sb("ssum", [P, NT])
        pos = sb("pos", [P, 2, NT])
        keep = sb("keep", [P, NT])
        slotf = sb("slotf", [P, 2, NT])
        sidx = sb("sidx", [P, 2, NT], U32)
        coef = sb("coef", [P, 2, NT])
        cnt = sb("cnt", [P, 4, E])
        nti = sb("nti", [P, E], I32)
        tle = sb("tle", [P, 2, NTILE1, E])
        tabf = sb("tabf", [P, 3, NTILE1])
        tabi = sb("tabi", [P, 2, NTILE1], I32)
        x_sb = sb("x_sb", [P, NT, D])
        ctx_sb = sb("ctx_sb", [P, NT, D])
        v17 = sb("v17", [P, 2, NT, HEADS, HD + 1], FP16)
        xn = sb("xn", [P, NT, RW])
        xT = sb("xT", [P, KC, T])
        wts = sb("wts", [P, 3 * E * KC * HP])
        w1_sb = wts[:, 0:E * KC * HP].rearrange("p (e k h) -> p e k h", e=E, k=KC)
        w3_sb = wts[:, E * KC * HP:2 * E * KC * HP].rearrange("p (e k h) -> p e k h", e=E, k=KC)
        w2_sb = wts[:, 2 * E * KC * HP:2 * E * KC * HP + E * HC * D].rearrange("p (e c d) -> p e c d", e=E, c=HC)
        gu_sb = wts[:, 0:E * KC * GU]
        dn_sb = wts[:, E * KC * GU:E * KC * GU + E * KC * D]
        sw1_sb = sb("sw1_sb", [P, KC, HP])
        sw3_sb = sb("sw3_sb", [P, KC, HP])
        sw2_sb = sb("sw2_sb", [P, HC, D])
        hT = sb("hT", [P, HC, 512])
        thb = sb("thb", [P, 2, 512])
        arena = sb("arena", [P, 13600])
        at = [0]

        def take(words):
            at[0] += words
            assert at[0] <= 13600
            return arena[:, at[0] - words:at[0]]

        def seqs(n=1):
            return take(n * 2 * SEQ).rearrange("p (n a t) -> p n a t", n=n, a=2)

        w0 = seqs(KC)
        kT = seqs(NG)
        vT = take(NG * 512).rearrange("p (n a t) -> p n a t", n=NG, a=2)
        O, A2, E2, EV, NO, AA, EE, T1 = [seqs(2) for _ in range(8)]
        PP, QQ, T2 = EV, E2, NO
        at[0] = 0
        ktb = take(B * NPAIR * S // 2).bitcast(FP16).rearrange("p (b h t) -> p b h t", b=B, h=NPAIR)
        p32 = take(2 * 1024).rearrange("p (n c) -> p n c", n=2)
        pT = take(2 * 2 * 3 * 512).bitcast(FP16).rearrange("p (l n s c) -> p l n s c", l=2, n=2, s=3)
        qtb = [buf.bitcast(FP16).rearrange("p (a h t) -> p a h t", a=2, h=NPAIR)
               for buf in (ctx_sb[:, :, :].rearrange("p i d -> p (i d)"), xT[:, :, :].rearrange("p k t -> p (k t)"))]
        spl = thb[:, :, :].rearrange("p n t -> p (n t)").bitcast(FP16).rearrange("p (n h s c) -> p n h s c", n=2, h=HEADS, s=4)
        sel = hT[:, 0:2, :].rearrange("p n t -> p (n t)").bitcast(BF16).rearrange("p (h k) -> p h k", h=HEADS)
        assert at[0] >= 4096 + 4 * D + 2 * KC * P + 4 * HP
        mmax = take(2 * 2 * HEADS).rearrange("p (n q h) -> p n q h", n=2, q=2)
        mneg = take(4 * HEADS).bitcast(BF16).rearrange("p (n q l h) -> p n q l h", n=2, q=2, l=2)
        mT = take(S).bitcast(BF16).rearrange("p (n q) -> p n q", n=2)
        den = take(2 * 16).rearrange("p (n q h) -> p n q h", n=2, q=2)
        att = sw1_sb[:, :, :].rearrange("p k h -> p (k h)")[:, 0:512].rearrange("p (n q h c) -> p n q h c", n=2, q=2, h=8)
        xrT = sw2_sb[:, :, :].rearrange("p k h -> p (k h)")[:, 0:KC * 256].rearrange("p (k t) -> p k t", k=KC)
        at[0] = 0
        xt = take(NXT * RW).rearrange("p (n d) -> p n d", n=NXT)
        xtT = take(2 * D).rearrange("p (n k t) -> p n k t", n=2, k=KC)
        gh = take(2 * I).rearrange("p (n i) -> p n i", n=2)
        up = take(2 * I).rearrange("p (n i) -> p n i", n=2)
        th1 = take(2 * I).rearrange("p (n i) -> p n i", n=2)
        glu = take(2 * I).rearrange("p (n i) -> p n i", n=2)
        actv = take(2 * I).rearrange("p (n i) -> p n i", n=2)
        actT = take(2 * I).rearrange("p (n k t) -> p n k t", n=2, k=KC)
        mk1 = take(4 * D).rearrange("p (n d) -> p n d", n=4)
        got1 = take(2 * NT * D).rearrange("p (k i d) -> p k i d", k=2, i=NT)

        xd = xn
        got0 = xT[:, :, :].rearrange("p k t -> p (k t)").rearrange("p (i d) -> p i d", i=NT)
        xn2 = wts[:, 3 * E * KC * HP - NT * RW:3 * E * KC * HP].rearrange("p (i d) -> p i d", i=NT)
        at[0] = B * NPAIR * S // 2
        xdT = take(2 * D).rearrange("p (n k t) -> p n k t", n=2, k=KC)
        the = take(2 * HP).rearrange("p (n h) -> p n h", n=2)
        he = take(2 * HP).rearrange("p (n h) -> p n h", n=2)
        mk0 = take(4 * D).rearrange("p (n d) -> p n d", n=4)

        ps = ctx.enter_context(nc.psum_tensor("ps", [P, 8, 512], FP32))

        def ps16(b):
            return ps[:, b, :].bitcast(FP16).rearrange("p (h t) -> p h t", t=P)

        x_in = [sem(f"x_in{p}") for p in range(NP2)]
        ctx_in_s = [sem(f"ctx_in{p}") for p in range(NP2)]
        small_in = sem("small_in")
        bias_in_s = sem("bias_in_s")
        bias_rows = sem("bias_rows")
        wg_in = sem("wg_in")
        sw_in = sem("sw_in")
        w1_in = [sem(f"w1_in{c}") for c in range(2)]
        w3_in = [sem(f"w3_in{c}") for c in range(2)]
        w2_in = sem("w2_in")
        gu_in = sem("gu_in")
        dn_in = sem("dn_in")
        zero_out, zero1_out = sem("zero_out"), sem("zero1_out")
        pool_c = sem("pool_c")
        consts_ok = sem("consts_ok")
        sel_ok = sem("sel_ok")
        bias_p_ok = sem("bias_p_ok")
        zrow_ok = sem("zrow_ok")
        pads_ok = sem("pads_ok")
        w0_ok = sem("w0_ok")
        tg_ok = sem("tg_ok")
        p32_ok = sem("p32_ok")
        var_ok = sem("var_ok")
        rstd_ok = sem("rstd_ok")
        xn_ok = sem("xn_ok")
        kT_ps, vT_ps, kT_ok, vT_ok = sem("kT_ps"), sem("vT_ps"), sem("kT_ok"), sem("vT_ok")
        o_ok, a2_ok, no_ok, ee_ok = sem("o_ok"), sem("a2_ok"), sem("no_ok"), sem("ee_ok")
        e2_ok, aa_ok, ev_ok, t2_ok = sem("e2_ok"), sem("aa_ok"), sem("ev_ok"), sem("t2_ok")
        aq_ok, den_ok = sem("aq_ok"), sem("den_ok")
        q_ok, t1_ok = sem("q_ok"), sem("t1_ok")
        a2_exp, e2_exp, aa_exp, ee_exp = sem("a2_exp"), sem("e2_exp"), sem("aa_exp"), sem("ee_exp")
        y_ok, yT_ps, x1_ok = sem("y_ok"), sem("yT_ps"), sem("x1_ok")
        x1T_ps, x1T_ok = sem("x1T_ps"), sem("x1T_ok")
        lg0_ps, lg0_ok, ex0_in, ex0_ok = sem("lg0_ps"), sem("lg0_ok"), sem("ex0_in"), sem("ex0_ok")
        oh0_ok, cum0_ps, cum0_ok, idx0_ok = sem("oh0_ok"), sem("cum0_ps"), sem("cum0_ok"), sem("idx0_ok")
        disp0_in, disp0_out = sem("disp0_in"), [sem(f"disp0_out{c}") for c in range(4)]
        sh_ps, sh_th, sh_ok, sho_ps, xs_ok = sem("sh_ps"), sem("sh_th"), sem("sh_ok"), sem("sho_ps"), sem("xs_ok")
        xdT_ps, xdT_ok, h0_ps, h0_th, h0_ok = sem("xdT_ps"), sem("xdT_ok"), sem("h0_ps"), sem("h0_th"), sem("h0_ok")
        oe0_ps, oe0_ok, made0_in, got0_in = sem("oe0_ps"), sem("oe0_ok"), [sem(f"made0_in{c}") for c in range(4)], [sem(f"got0_in{b}") for b in range(B)]
        ids_ok, qz_ok, xn2_ok, x2_all = sem("ids_ok"), [sem("qz_ok0"), sem("qz_ok1")], sem("xn2_ok"), sem("x2_all")
        q_odd, lo_pool, lo_dve, mhi_ok, b3z_ok = sem("q_odd"), sem("lo_pool"), sem("lo_dve"), sem("mhi_ok"), sem("b3z_ok")
        x2_ok = sem("x2_ok")
        k_hi, k_lo, k_ps, ktb_ok, q_hi, q_lo = sem("k_hi"), sem("k_lo"), sem("k_ps"), sem("ktb_ok"), sem("q_hi"), sem("q_lo")
        v_hi, v_lo, spare_ok = sem("v_hi"), sem("v_lo"), sem("spare_ok")
        misc_ps, misc_free = sem("misc_ps"), sem("misc_free")
        nat_ps, nat_ok, mneg_ok = sem("nat_ps"), sem("nat_ok"), sem("mneg_ok")
        st_ps, st_exp, pv_ps, pv_ok = sem("st_ps"), sem("st_exp"), sem("pv_ps"), sem("pv_ok")
        ex1_in, ex1_ok, oh1_ok, idx1_ok = sem("ex1_in"), sem("ex1_ok"), sem("oh1_ok"), sem("idx1_ok")
        disp1_in, tab_ok = sem("disp1_in"), sem("tab_ok")
        xt_in = [sem(f"xt_in{c}") for c in range(NXT)]
        xtT_ps, xtT_ok, gu_ps, gh_ok, th1_ok, act_ok = sem("xtT_ps"), sem("xtT_ok"), sem("gu_ps"), sem("gh_ok"), sem("th1_ok"), sem("act_ok")
        actT_ps, actT_ok, oe1_ps, mk1_ok = sem("actT_ps"), sem("actT_ok"), sem("oe1_ps"), sem("mk1_ok")
        made1_in, got1_in, x4_ok, out_done = [sem(f"made1_in{c}") for c in range(4)], [sem(f"got1_in{b}") for b in range(B)], sem("x4_ok"), sem("out_done")
        v_chain, a_chain = sem("v_chain"), sem("a_chain")


        block = ctx.enter_context(nc.Block())

        @block.sync
        def _(sp):
            for p in range(NP2):
                sp.dma_start(x_sb[:, 4 * p:4 * p + 4, :], x_v[:, 4 * p:4 * p + 4, :]).then_inc(x_in[p], 16)
                sp.dma_start(ctx_sb[:, 4 * p:4 * p + 4, :], ctx_v[:, 4 * p:4 * p + 4, :]).then_inc(ctx_in_s[p], 16)
            sp.dma_start(wg_sb[:, :, :], Wg.rearrange("(k p) e -> p k e", p=P)).then_inc(wg_in, 16)
            sp.dma_start(sw1_sb[:, :, 0:H], sw1.rearrange("(k p) h -> p k h", p=P)).then_inc(sw_in, 16)
            sp.dma_start(sw3_sb[:, :, 0:H], sw3.rearrange("(k p) h -> p k h", p=P)).then_inc(sw_in, 16)
            sp.wait_ge(pads_ok, 1)
            sp.dma_start(sw2_sb[:, 0:HC - 1, :], sw2[0:(HC - 1) * P, :].rearrange("(c p) d -> p c d", p=P)).then_inc(sw_in, 16)
            sp.dma_start(sw2_sb[0:HR, HC - 1, :], sw2[(HC - 1) * P:H, :]).then_inc(sw_in, 16)
            empty = zrow[:, :].unsqueeze(1).to_broadcast([P, NT // 2, 2 * RW])
            sp.wait_ge(zrow_ok, 1)
            sp.dma_start(disp0.rearrange("(p r) d -> p (r d)", p=P).rearrange("p (a c) -> p a c", c=2 * RW), empty).then_inc(zero_out, 16)
            sp.dma_start(made0.rearrange("(p r) d -> p r d", p=P), zrow[:, 0:D].unsqueeze(1).to_broadcast([P, NT, D])).then_inc(zero_out, 16)
            for c in range(2):
                es = slice(c * E // 2, (c + 1) * E // 2)
                for w, dst, done in ((W1, w1_sb, w1_in), (W3, w3_sb, w3_in)):
                    for e in range(es.start, es.stop):
                        sp.dma_start(dst[:, e, :, 0:H], w[e].rearrange("(k p) h -> p k h", p=P)).then_inc(done[c], 16)
            for e in range(E):
                sp.dma_start(w2_sb[:, e, 0:HC - 1, :], W2[e, 0:(HC - 1) * P, :].rearrange("(c p) d -> p c d", p=P)).then_inc(w2_in, 16)
            sp.dma_start(w2_sb[0:HR, :, HC - 1, :], W2[:, (HC - 1) * P:H, :].rearrange("e p d -> p e d")).then_inc(w2_in, 16)
            GB = E * GU // P
            sp.dma_start(bias_in[:, 0:GB], gate_up_b.rearrange("e j -> (e j)").rearrange("(p c) -> p c", p=P)).then_inc(bias_in_s, 16)
            sp.dma_start(bias_in[:, GB:], down_b.rearrange("e j -> (e j)").rearrange("(p c) -> p c", p=P)).then_inc(bias_in_s, 16)
            for n in range(E):
                sp.dma_start(disp1[n * T:(n + 1) * T, :].rearrange("(p r) d -> p (r d)", p=P).rearrange("p (a c) -> p a c", c=2 * RW), empty).then_inc(zero1_out, 16)
            sp.wait_ge(disp0_in, 16 * NT)
            for c in range(4):
                sp.dma_start(xd[:, 2 * c:2 * c + 2, :], disp0[2 * c * P:(2 * c + 2) * P, :].rearrange("(e p) d -> p e d", p=P)).then_inc(disp0_out[c], 16)
            sp.wait_ge(bias_p_ok, 1)
            sp.wait_ge(b3z_ok, 1)
            for k in range(3):
                sp.dma_start(bias3[k:k + 1, 0:E * GU], bias_p[:, k, 0:GB]).then_inc(bias_rows, 16)
                sp.dma_start(bias3[k:k + 1, E * GU:], bias_p[:, k, GB:]).then_inc(bias_rows, 16)
            for c in range(4):
                sp.wait_ge(made0_in[c], 16 * (E // 4))
            for b in range(B):
                sp.dma_start(got0[:, 2 * b:2 * b + 2, :], made0[b * S:(b + 1) * S, :].rearrange("(i p) d -> p i d", p=P)).then_inc(got0_in[b], 16)
            sp.wait_ge(oe0_ps, E)
            for e in range(E):
                sp.dma_start(gu_sb[:, e * KC * GU:(e + 1) * KC * GU].rearrange("p (k j) -> p k j", k=KC),
                             gate_up[e].rearrange("(k p) j -> p k j", p=P)).then_inc(gu_in, 16)
                sp.dma_start(dn_sb[:, e * KC * D:(e + 1) * KC * D].rearrange("p (k j) -> p k j", k=KC),
                             down[e].rearrange("(k p) j -> p k j", p=P)).then_inc(dn_in, 16)
            sp.wait_ge(disp1_in, 16 * 2 * NT)
            sp.wait_ge(tab_ok, 1)
            for t in range(NTILE1):
                if t >= NXT:
                    sp.wait_ge(made1_in[t % 4], 16 * ((t - NXT) // 4 + 1))
                row = sp.value_load(tabi[0:1, 1, t:t + 1], min_val=0, max_val=E * T - P)
                sp.dma_start(xt[:, t % NXT, :], disp1[bass.ds(row, P), :]).then_inc(xt_in[t % NXT], 16)
            for c in range(4):
                sp.wait_ge(made1_in[c], 16 * len(range(c, NTILE1, 4)))
            for b in range(B):
                for k in range(2):
                    sp.dma_start(got1[:, k, 2 * b:2 * b + 2, :], made1[k * T + b * S:k * T + (b + 1) * S, :].rearrange("(i p) d -> p i d", p=P)).then_inc(got1_in[b], 16)
            for i in range(NT):
                sp.wait_ge(x4_ok, i + 1)
                sp.dma_start(out_v[:, i, :], x_sb[:, i, :]).then_inc(out_done, 16)
            sp.wait_ge(out_done, 16 * NT)
            sp.wait_ge(zero_out, 16 * 2)
            sp.wait_ge(zero1_out, 16 * E)

        def cur(buf, n):
            return buf[:, n, :, 1:SEQ]

        def prev(buf, n):
            return buf[:, n, :, 0:S]

        def flat(buf, n):
            return buf[:, n, :, :].rearrange("p a t -> p (a t)")

        NAT = [(4 * s, 4, 1) if s < 2 else (0, 8, 0) for s in range(3)] + [(8 + 4 * s, 4, 1) if s < 2 else (8, 8, 0) for s in range(3)]

        def sub_cols(buf2, nh):
            return buf2[:, :, 0:nh // 2 * (1024 // nh)].rearrange("p a (h c) -> p a h c", h=nh // 2)

        @block.gpsimd
        def _(pool):
            step = [0]

            def link(ins):
                step[0] += 1
                ins.then_inc(pool_c, 1)
                pool.wait_ge(pool_c, step[0])

            g = nc.gpsimd
            link(g.memset(zrow[:, :], 0.0))
            g.memset(zrow[:, D:D + 1].bitcast(U32), int(FAR))
            g.memset(zrow[:, RW + D:RW + D + 1].bitcast(U32), int(FAR)).then_inc(zrow_ok, 1)
            g.memset(nhalf[:, :], -0.5)
            link(g.memset(ident[:, :], 0.0))
            link(g.affine_select(out=ident[:, :], in_=ident[:, :], compare_op=ALU.not_equal, fill=1.0, base=0,
                                 pattern=[[-1, P]], channel_multiplier=1))
            g.tensor_copy(ident16[:, :], ident[:, :])
            g.tensor_copy(identb[:, :], ident[:, :])
            link(g.memset(onesb[:, :], 1.0))
            g.affine_select(out=upper[:, :], in_=onesb[:, :], compare_op=ALU.is_ge, fill=0.0, base=0,
                            pattern=[[1, P]], channel_multiplier=-1)
            link(g.memset(causal[:, :], 0.0))
            g.affine_select(out=causal[:, :], in_=causal[:, :], compare_op=ALU.is_ge, fill=MASK, base=0,
                            pattern=[[-1, P]], channel_multiplier=1)
            link(g.memset(causalT[:, :], 0.0))
            g.affine_select(out=causalT[:, :], in_=causalT[:, :], compare_op=ALU.is_ge, fill=MASK, base=0,
                            pattern=[[1, P]], channel_multiplier=-1)
            g.iota(iota8[:, :], pattern=[[1, E]], base=0, channel_multiplier=0, allow_small_or_imprecise_dtypes=True)
            g.iota(iota_t[:, :], pattern=[[1, NTILE1]], base=0, channel_multiplier=0,
                   allow_small_or_imprecise_dtypes=True).then_inc(consts_ok, 1)
            g.iota(ids[:, :, :], pattern=[[T, 2], [P, NT]], base=0, channel_multiplier=1)
            link(g.memset(xn[:, :, D:RW], 0.0))
            g.tensor_copy(xn[:, :, D].bitcast(U32), ids[:, 0, :])
            g.memset(w0[:, :, :, 0:1], NEG)
            g.memset(kT[:, :, :, 0:1], NEG)
            g.memset(A2[:, :, :, 0:1], 0.0)
            g.memset(E2[:, :, :, 0:1], 0.0)
            g.memset(EV[:, :, :, 0:1], 0.0)
            g.memset(sw1_sb[:, :, H:HP], 0.0)
            g.memset(sw3_sb[:, :, H:HP], 0.0)
            g.memset(w1_sb[:, :, :, H:HP], 0.0)
            link(g.memset(w3_sb[:, :, :, H:HP], 0.0))
            link(g.memset(sw2_sb[HR:P, HC - 1, :], 0.0))
            g.memset(w2_sb[HR:P, :, HC - 1, :], 0.0).then_inc(pads_ok, 1)
            pool.wait_ge(pads_ok, 1)

            def rstd(n, stage, i0, ni, scale=1.0):
                pool.wait_ge(var_ok, n + 1)
                r = rs[:, stage, i0:i0 + ni]
                link(g.tensor_scalar(r, mv[:, stage, i0:i0 + ni, 1], EPS, None, ALU.add))
                last = g.tensor_tensor(r, r, nhalf[:, 0:ni], ALU.pow)
                if scale != 1.0:
                    link(last)
                    last = g.tensor_scalar(r, r, scale, None, ALU.mult)
                last.then_inc(rstd_ok, 1)

            rstd(0, 0, 0, 4)
            rstd(1, 0, 4, 4)
            pool.wait_ge(small_in, 16 * SMALL)
            for h in range(KC):
                last = g.tensor_copy(w0[:, h, :, 1:SEQ], w_sb[:, h:h + 1].unsqueeze(2).to_broadcast([P, 2, S]))
            last.then_inc(w0_ok, 1)

            pool.wait_ge(bias_in_s, 32)
            src = bias_in[:, :]
            for k in range(3):
                link(g.tensor_copy(bias_p[:, k, :], src))
                if k < 2:
                    link(g.tensor_tensor(bias_r[:, k, :], src, bias_p[:, k, :], ALU.subtract))
                    src = bias_r[:, k, :]
            g.memset(v17[:, 1, :, :, HD:HD + 1], 0.0)
            g.memset(v17[:, 0, :, :, HD:HD + 1], 1.0).then_inc(bias_p_ok, 1)

            def wkv(n):
                p, h = divmod(n, KC)
                b = n % 2
                pool.wait_ge(kT_ok, n + 1)
                pool.wait_ge(o_ok, n + 1)
                if n >= 2:
                    pool.wait_ge(y_ok, n - 1)
                g.tensor_tensor(cur(E2, b), cur(kT, n), cur(O, b), ALU.subtract).then_inc(e2_ok, 1)
                pool.wait_ge(no_ok, n + 1)
                g.tensor_tensor(cur(AA, b), prev(O, b), cur(NO, b), ALU.subtract).then_inc(aa_ok, 1)
                pool.wait_ge(vT_ok, n + 1)
                pool.wait_ge(e2_exp, n + 1)
                g.tensor_tensor(cur(EV, b), cur(E2, b), vT[:, n], ALU.mult).then_inc(ev_ok, 1)
                pool.wait_ge(ee_exp, n + 1)
                pool.wait_ge(aa_ok, n + 1)
                g.tensor_tensor(cur(T2, b), cur(EE, b), vT[:, n], ALU.mult).then_inc(t2_ok, 1)

            wkv(0)
            wkv(1)
            wkv(2)
            rstd(2, 1, 0, 4)
            wkv(3)

            def scatter0(p):
                pool.wait_ge(zero_out, 16 * 2)
                pool.wait_ge(idx0_ok, p + 1)
                for i in range(4 * p, 4 * p + 4):
                    g.indirect_dma_start(
                        out=disp0[:, :], out_offset=bass.IndirectOffsetOnAxis(ap=sidx[:, 0, i:i + 1], axis=0),
                        in_=xn[:, i, :], in_offset=None, bounds_check=E * CAP - 1, oob_is_err=False,
                    ).then_inc(disp0_in, 16)

            scatter0(0)
            rstd(3, 1, 4, 4)
            scatter0(1)

            pool.wait_ge(sho_ps, NP2)
            link(g.memset(sel[:, :, :], 0.0))
            for l in range(2):
                last = g.affine_select(out=sel[:, :, :], in_=sel[:, :, :], compare_op=ALU.not_equal, fill=1.0, base=-l * HEADS,
                                       pattern=[[-1, HEADS], [0, P]], channel_multiplier=1)
                if l == 0:
                    link(last)
            last.then_inc(sel_ok, 1)
            for t in range(NT):
                c = ctx_sb[:, t, :].rearrange("p (h c) -> p h c", h=HEADS)
                dst = spl[:, t % 2].rearrange("p h (r l) c -> p h l r c", l=2)
                pool.wait_ge(k_hi, t + 1)
                g.tensor_tensor(dst[:, :, 1], c.unsqueeze(2).to_broadcast([P, HEADS, 2, HD]), dst[:, :, 0], ALU.subtract).then_inc(k_lo, 1)
                pool.wait_ge(v_hi, t + 1)
                g.tensor_tensor(v17[:, 1, t, :, 0:HD], c, v17[:, 0, t, :, 0:HD], ALU.subtract).then_inc(v_lo, 1)
                pool.wait_ge(oe0_ok, t + 1)
                g.indirect_dma_start(
                    out=made0[:, :], out_offset=bass.IndirectOffsetOnAxis(ap=xd[:, t, D:D + 1].bitcast(U32), axis=0),
                    in_=mk0[:, t % 4, :], in_offset=None, bounds_check=T - 1, oob_is_err=False,
                ).then_inc(made0_in[t % 4], 16)
            def query_zeros(n):
                link(g.memset(qtb[n][P // 2:P, 0], 0.0))
                g.memset(qtb[n][0:P // 2, 1], 0.0).then_inc(qz_ok[n], 1)
                pool.wait_ge(qz_ok[n], 1)

            pool.wait_ge(v_lo, NT)
            pool.wait_ge(k_lo, NT)
            query_zeros(0)
            for c in range(4):
                pool.wait_ge(made0_in[c], 16 * (E // 4))
            g.tensor_copy(xn[:, :, D].bitcast(U32), ids[:, 0, :])
            link(g.memset(xn2[:, :, D:RW], 0.0))
            g.tensor_copy(xn2[:, :, D].bitcast(U32), ids[:, 1, :]).then_inc(ids_ok, 1)

            for b in range(B):
                rstd(4 + b, 2, 2 * b, 2, scale=float(HD) ** -0.5)

            def q_low(b):
                for j in range(TPB):
                    i = 2 * b + j
                    q = xn[:, i, 0:D].rearrange("p (h c) -> p h c", h=HEADS)
                    pool.wait_ge(q_hi, i + 1)
                    lo = spl[:, i % 2, :, 2:4, :]
                    g.tensor_tensor(lo, q.unsqueeze(2).to_broadcast([P, HEADS, 2, HD]), spl[:, i % 2, :, 0:2, :], ALU.subtract).then_inc(q_lo, 1)

            def weights_low(u, s):
                n = 3 * u + s
                pool.wait_ge(p32_ok, n + 1)
                pool.wait_ge(st_exp, n + 1)
                g.tensor_tensor(pT[:, 1, u % 2, s, :], p32[:, n % 2, :], pT[:, 0, u % 2, s, :], ALU.subtract).then_inc(lo_pool, 1)

            def scatter1(b):
                pool.wait_ge(idx1_ok, b + 1)
                pool.wait_ge(xn2_ok, b + 1)
                pool.wait_ge(zero1_out, 16 * E)
                for i in range(2 * b, 2 * b + 2):
                    for k, rows in enumerate((xn, xn2)):
                        g.indirect_dma_start(
                            out=disp1[:, :], out_offset=bass.IndirectOffsetOnAxis(ap=sidx[:, k, i:i + 1], axis=0),
                            in_=rows[:, i, :], in_offset=None, bounds_check=E * T - 1, oob_is_err=False,
                        ).then_inc(disp1_in, 16)

            q_low(0)
            pool.wait_ge(x2_all, 1)
            pool.wait_ge(q_lo, TPB)
            query_zeros(1)
            q_low(1)
            for u in range(2 * B):
                for s in range(2):
                    weights_low(u, s)
                if u % 2 == 0 and u >= 2:
                    rstd(8 + u // 2 - 1, 3, u - 2, 2)
                if u % 2 == 1 and u // 2 + 2 < B:
                    q_low(u // 2 + 2)
                if u % 2 == 0 and u >= 4:
                    scatter1((u - 4) // 2)
            scatter1(B - 2)
            rstd(7 + B, 3, 2 * B - 2, 2)
            scatter1(B - 1)

            for t in range(NTILE1):
                pool.wait_ge(mk1_ok, t + 1)
                g.indirect_dma_start(
                    out=made1[:, :], out_offset=bass.IndirectOffsetOnAxis(ap=xt[:, t % NXT, D:D + 1].bitcast(U32), axis=0),
                    in_=mk1[:, t % 4, :], in_offset=None, bounds_check=2 * T - 1, oob_is_err=False,
                ).then_inc(made1_in[t % 4], 16)
            for c in range(4):
                pool.wait_ge(made1_in[c], 16 * len(range(c, NTILE1, 4)))

        USES = [("q", i) for i in range(4)]
        for u in range(2 * B + 1):
            if u % 2 == 0 and u < 2 * B:
                USES.append(("m", u // 2))
            if u % 2 == 1 and u // 2 + 2 < B:
                USES += [("q", u + 3), ("q", u + 4)]
            if u % 2 == 1 and u >= 3:
                USES += [("x", (u - 3) // 2), ("l", (u - 3) // 2)]
            if u % 2 == 0 and u >= 4:
                USES.append(("c", (u - 4) // 2))
        USES += [("x", B - 1), ("l", B - 1), ("c", B - 1), ("n", 0)]
        USE = {key: n for n, key in enumerate(USES)}

        @block.scalar
        def _(act):
            a = nc.scalar
            act.dma_start(gates[:, 0:2], g_xattn.partition_broadcast(P)).then_inc(small_in, 16)
            act.dma_start(gates[:, 2:4], g_ffn.partition_broadcast(P)).then_inc(small_in, 16)
            act.dma_start(w_sb[:, :], wkv_w.rearrange("(k p) -> p k", p=P), allow_slow_non_contiguous=True).then_inc(small_in, 16)
            act.dma_start(u_sb[:, :], wkv_u.rearrange("(k p) -> p k", p=P), allow_slow_non_contiguous=True).then_inc(small_in, 16)
            act.dma_start(rb_sb[:, :], router_b.partition_broadcast(P)).then_inc(small_in, 16)
            for k in range(KC):
                act.dma_start(rw_sb[:, k, :], router_w[:, k * P:(k + 1) * P].rearrange("e p -> p e"), allow_slow_non_contiguous=True).then_inc(small_in, 16)
            act.wait_ge(small_in, 16 * SMALL)
            a.activation(tg[:, :], gates[:, :], ACT.Tanh).then_inc(tg_ok, 1)

            def evac(dst, src, ready, n, done):
                act.wait_ge(ready, n)
                a.activation(dst, src, ACT.Copy).then_inc(done, 1)

            def kv(n):
                if n == 0:
                    act.wait_ge(pads_ok, 1)
                evac(cur(kT, n), ps[:, n % 2, :].rearrange("p (a t) -> p a t", a=2), kT_ps, n + 1, kT_ok)
                evac(vT[:, n], ps[:, 2 + n % 2, :].rearrange("p (a t) -> p a t", a=2), vT_ps, n + 1, vT_ok)

            def exps(n):
                for buf, ready, done in ((A2, a2_ok, a2_exp), (E2, e2_ok, e2_exp), (EE, ee_ok, ee_exp), (AA, aa_ok, aa_exp)):
                    act.wait_ge(ready, n + 1)
                    a.activation(cur(buf, n % 2), cur(buf, n % 2), ACT.Exp).then_inc(done, 1)

            kv(0)
            kv(1)
            exps(0)
            kv(2)
            exps(1)
            kv(3)
            exps(2)
            exps(3)

            def x1_evac(p):
                for h in range(KC):
                    evac(xT[:, h, 512 * p:512 * p + 512], ps[:, h, :], x1T_ps, 2 * p + h + 1, x1T_ok)

            def ex0(p):
                act.wait_ge(ex0_in, p + 1)
                a.activation(pe_[:, 4 * p:4 * p + 4, :], pe_[:, 4 * p:4 * p + 4, :], ACT.Exp).then_inc(ex0_ok, 1)

            def sh_tanh(p):
                for m in range(HC):
                    n = HC * p + m
                    act.wait_ge(sh_ps, n + 1)
                    if n >= 2:
                        act.wait_ge(sh_ok, n - 1)
                    a.activation(thb[:, n % 2, :], ps[:, 2 * (m % 2), :], ACT.Tanh, scale=0.5).then_inc(sh_th, 1)

            for p in range(NP2):
                x1_evac(p)
                ex0(p)
                sh_tanh(p)

            def kv_high(t):
                c = ctx_sb[:, t, :].rearrange("p (h c) -> p h c", h=HEADS)
                if t >= 2:
                    act.wait_ge(k_ps, t - 1)
                dst = spl[:, t % 2].rearrange("p h (r l) c -> p h l r c", l=2)
                a.activation(dst[:, :, 0], c.unsqueeze(2).to_broadcast([P, HEADS, 2, HD]), ACT.Copy).then_inc(k_hi, 1)
                a.activation(v17[:, 0, t, :, 0:HD], c, ACT.Copy).then_inc(v_hi, 1)

            def xd_evac(e):
                act.wait_ge(xdT_ps, e + 1)
                a.activation(xdT[:, e % 2], ps[:, e % 2, 0:D].rearrange("p (k t) -> p k t", k=KC), ACT.Copy).then_inc(xdT_ok, 1)

            def h_tanh(e):
                act.wait_ge(h0_ps, e + 1)
                a.activation(the[:, e % 2, :], ps[:, 2 + 2 * (e % 2), 0:HP], ACT.Tanh, scale=0.5).then_inc(h0_th, 1)

            def oe_evac(e):
                act.wait_ge(oe0_ps, e + 1)
                if e >= 4:
                    act.wait_ge(made0_in[e % 4], 16 * (e // 4))
                a.activation(mk0[:, e % 4, :], ps[:, 6, 0:D], ACT.Copy).then_inc(oe0_ok, 1)

            xd_evac(0)
            xd_evac(1)
            act.wait_ge(sho_ps, NP2)
            kv_high(0)
            h_tanh(0)
            for e in range(E):
                if e + 2 < E:
                    xd_evac(e + 2)
                if e + 1 < E:
                    kv_high(e + 1)
                    h_tanh(e + 1)
                oe_evac(e)

            def misc_evac(key, dst, src):
                n = USE[key]
                act.wait_ge(misc_ps, n + 1)
                a.activation(dst, src, ACT.Copy).then_inc(misc_free, 1)

            def q_split(b):
                for j in range(TPB):
                    i = 2 * b + j
                    act.wait_ge(xn_ok, 2 * NT + i + 1)
                    if i >= 2:
                        act.wait_ge(misc_ps, USE[("q", i - 2)] + 1)
                    else:
                        act.wait_ge(k_ps, NT)
                    q = xn[:, i, 0:D].rearrange("p (h c) -> p h c", h=HEADS).unsqueeze(2).to_broadcast([P, HEADS, 2, HD])
                    a.activation(spl[:, i % 2, :, 0:2, :], q, ACT.Copy).then_inc(q_hi, 1)

            def q_evac(b):
                if b >= 2:
                    act.wait_ge(st_ps, 3 * 2 * (b - 1))
                for j in range(TPB):
                    misc_evac(("q", 2 * b + j), qtb[b % 2][0:P // 2, 0, :, j * P:(j + 1) * P], ps16(7)[0:P // 2])

            def exp_t(u):
                for s in range(3):
                    n = 3 * u + s
                    act.wait_ge(st_ps, n + 1)
                    if u >= 2 and s == 0:
                        act.wait_ge(pv_ps, u - 1)
                    if n >= 2:
                        if (n - 2) % 3 < 2:
                            act.wait_ge(lo_pool, 2 * ((n - 2) // 3) + (n - 2) % 3 + 1)
                        else:
                            act.wait_ge(lo_dve, (n - 2) // 3 + 1)
                    nh = 4 if s < 2 else 8
                    src = sub_cols(ps[:, 2 + 2 * (n % 2):4 + 2 * (n % 2), :], nh)
                    for dst, done in ((p32[:, n % 2, :], p32_ok), (pT[:, 0, u % 2, s, :], st_exp)):
                        a.activation(dst.rearrange("p (h a c) -> p a h c", a=2, h=nh // 2), src, ACT.Exp).then_inc(done, 1)

            def ex1(b):
                act.wait_ge(ex1_in, b + 1)
                a.activation(ssum[:, 2 * b:2 * b + 2], ssum[:, 2 * b:2 * b + 2], ACT.Exp).then_inc(ex1_ok, 1)

            def x_evac(b):
                misc_evac(("x", b), xrT[:, :, :], ps[:, 7, :].rearrange("p (k t) -> p k t", k=KC))

            def second_copy(b):
                act.wait_ge(xn_ok, 3 * NT + 2 * b + 2)
                act.wait_ge(ids_ok, 1)
                a.activation(xn2[:, 2 * b:2 * b + 2, 0:D], xn[:, 2 * b:2 * b + 2, 0:D], ACT.Copy).then_inc(xn2_ok, 1)

            for b in range(2):
                q_split(b)
                if b == 1:
                    act.wait_ge(x2_all, 1)
                q_evac(b)
            for u in range(2 * B):
                b = u // 2
                if u % 2 == 0:
                    misc_evac(("m", b), mT[0:2 * HEADS, b % 2, :], ps[0:2 * HEADS, 7, 0:S // 2].bitcast(BF16))
                elif b + 2 < B:
                    q_split(b + 2)
                if u % 2 == 1 and u >= 3:
                    second_copy((u - 3) // 2)
                exp_t(u)
                if u % 2 == 1 and b + 2 < B:
                    q_evac(b + 2)
                if u % 2 == 1 and u >= 3:
                    x_evac((u - 3) // 2)
                    ex1((u - 3) // 2)
            second_copy(B - 1)
            x_evac(B - 1)
            ex1(B - 1)

            def xt_evac(t):
                evac(xtT[:, t % 2], ps[:, t % 2, 0:D].rearrange("p (k t) -> p k t", k=KC), xtT_ps, t + 1, xtT_ok)

            def tile_tanh(t):
                act.wait_ge(gh_ok, t + 1)
                a.activation(th1[:, t % 2, :], gh[:, t % 2, :], ACT.Tanh, scale=1.702).then_inc(th1_ok, 1)

            def at_evac(t):
                evac(actT[:, t % 2], ps[:, 4 + t % 2, 0:I].rearrange("p (k t) -> p k t", k=KC), actT_ps, t + 1, actT_ok)

            def mk_evac(t):
                if t >= 4:
                    act.wait_ge(made1_in[t % 4], 16 * (t // 4))
                evac(mk1[:, t % 4, :], ps[:, 6 + t % 2, 0:D], oe1_ps, t + 1, mk1_ok)

            xt_evac(0)
            xt_evac(1)
            tile_tanh(0)
            for t in range(NTILE1):
                if t + 2 < NTILE1:
                    xt_evac(t + 2)
                if t + 1 < NTILE1:
                    tile_tanh(t + 1)
                at_evac(t)
                if t >= 1:
                    mk_evac(t - 1)
            mk_evac(NTILE1 - 1)

        @block.vector
        def _(dve):
            v = nc.vector
            step = [0]

            def link(ins):
                step[0] += 1
                ins.then_inc(v_chain, 1)
                dve.wait_ge(v_chain, step[0])

            def stats(n, stage, i0, ni):
                for i in range(i0, i0 + ni):
                    link(v.bn_stats(st[:, stage, i, :], x_sb[:, i, :]))
                for i in range(i0, i0 + ni):
                    last = v.bn_aggr(mv[:, stage, i, :], st[:, stage, i, :])
                last.then_inc(var_ok, 1)

            def normal(n, stage, i0, ni):
                dve.wait_ge(var_ok, n + 1)
                dve.wait_ge(rstd_ok, n + 1)
                for i in range(i0, i0 + ni):
                    v.tensor_scalar(xn[:, i, 0:D], x_sb[:, i, :], mv[:, stage, i, 0:1], rs[:, stage, i:i + 1],
                                    ALU.subtract, ALU.mult).then_inc(xn_ok, 1)

            for p in range(NP2):
                dve.wait_ge(x_in[p], 16)
                stats(p, 0, 4 * p, 4)
            for p in range(NP2):
                normal(p, 0, 4 * p, 4)

            dve.wait_ge(w0_ok, 1)

            def head(n):
                p, h = divmod(n, KC)
                b = n % 2
                dve.wait_ge(kT_ok, n + 1)
                v.tensor_tensor_scan(flat(O, b), flat(w0, h), flat(kT, n), NEG, ALU.add, ALU.max).then_inc(o_ok, 1)
                dve.wait_ge(o_ok, n + 1)
                v.scalar_tensor_tensor(cur(A2, b), prev(O, b), w_sb[:, h:h + 1], cur(O, b), ALU.add, ALU.subtract).then_inc(a2_ok, 1)
                v.scalar_tensor_tensor(cur(NO, b), cur(kT, n), u_sb[:, h:h + 1], prev(O, b), ALU.add, ALU.max).then_inc(no_ok, 1)
                dve.wait_ge(no_ok, n + 1)
                if n >= 2:
                    dve.wait_ge(t2_ok, n - 1)
                v.scalar_tensor_tensor(cur(EE, b), cur(kT, n), u_sb[:, h:h + 1], cur(NO, b), ALU.add, ALU.subtract).then_inc(ee_ok, 1)

            def tail(n):
                b = n % 2
                dve.wait_ge(a2_exp, n + 1)
                dve.wait_ge(e2_exp, n + 1)
                dve.wait_ge(ev_ok, n + 1)
                link(v.tensor_tensor_scan(flat(QQ, b), flat(A2, b), flat(E2, b), 0.0, ALU.mult, ALU.add))
                link(v.tensor_tensor_scan(flat(PP, b), flat(A2, b), flat(EV, b), 0.0, ALU.mult, ALU.add))
                dve.wait_ge(aa_exp, n + 1)
                if n >= 2:
                    dve.wait_ge(yT_ps, n // 2)
                link(v.tensor_tensor(cur(T1, b), cur(AA, b), prev(PP, b), ALU.mult))
                link(v.tensor_tensor(cur(AA, b), cur(AA, b), prev(QQ, b), ALU.mult))
                dve.wait_ge(ee_exp, n + 1)
                link(v.tensor_tensor(cur(AA, b), cur(AA, b), cur(EE, b), ALU.add))
                dve.wait_ge(t2_ok, n + 1)
                link(v.tensor_tensor(cur(T1, b), cur(T1, b), cur(T2, b), ALU.add))
                link(v.reciprocal(cur(AA, b), cur(AA, b)))
                v.tensor_tensor(cur(T1, b), cur(T1, b), cur(AA, b), ALU.mult).then_inc(y_ok, 1)
                dve.wait_ge(y_ok, n + 1)

            def residual(p, gate, ready, n, done):
                dve.wait_ge(ready, n)
                dve.wait_ge(tg_ok, 1)
                for k in range(2):
                    xs = x_sb[:, 4 * p + 2 * k:4 * p + 2 * k + 2, :].rearrange("p i d -> p (i d)")
                    last = v.scalar_tensor_tensor(xs, ps[:, 4 + k, :], tg[:, gate:gate + 1], xs, ALU.mult, ALU.add)
                    if k == 0:
                        link(last)
                last.then_inc(done, 1)

            def choose(i, src):
                link(v.max(mx[:, i, :], src))
                v.max_index(ix[:, i, :], mx[:, i, :], src).then_inc(v_chain, 1)
                step[0] += 1

            def route0(p):
                i0 = 4 * p
                sl = slice(i0, i0 + 4)
                dve.wait_ge(lg0_ps, p + 1)
                v.tensor_copy(lg[:, sl, :], ps[:, 6, 0:4 * E].rearrange("p (i e) -> p i e", e=E)).then_inc(lg0_ok, 1)
                dve.wait_ge(lg0_ok, p + 1)
                for i in range(i0, i0 + 4):
                    choose(i, lg[:, i, :])
                dve.wait_ge(v_chain, step[0])
                v.tensor_tensor(pe_[:, sl, :], lg[:, sl, :], mx[:, sl, 0:1].to_broadcast([P, 4, E]), ALU.subtract).then_inc(ex0_in, 1)
                link(v.tensor_copy(ixf[:, sl, 0:1], ix[:, sl, 0:1]))
                link(v.tensor_tensor(oh[:, 0, sl, :], iota8[:, :].unsqueeze(1).to_broadcast([P, 4, E]),
                                     ixf[:, sl, 0:1].to_broadcast([P, 4, E]), ALU.is_equal))
                v.tensor_copy(ohb[:, sl, :], oh[:, 0, sl, :]).then_inc(oh0_ok, 1)

            def slots0(p):
                i0 = 4 * p
                sl = slice(i0, i0 + 4)
                dve.wait_ge(cum0_ps, p + 1)
                v.tensor_tensor(cumoh[:, 0, sl, :], ps[:, 7, 0:4 * E].rearrange("p (i e) -> p i e", e=E), oh[:, 0, sl, :],
                                ALU.mult).then_inc(cum0_ok, 1)
                dve.wait_ge(cum0_ok, p + 1)
                link(v.reduce_sum(pos[:, 0, sl], cumoh[:, 0, sl, :], AXX))
                link(v.tensor_scalar(keep[:, sl], pos[:, 0, sl], float(CAP), None, ALU.is_le))
                link(v.tensor_scalar(slotf[:, 0, sl], ixf[:, sl, 0], float(CAP), FAR - 1.0, ALU.mult, ALU.add))
                link(v.tensor_tensor(slotf[:, 0, sl], slotf[:, 0, sl], pos[:, 0, sl], ALU.add))
                link(v.scalar_tensor_tensor(slotf[:, 0, sl], keep[:, sl], -FAR, slotf[:, 0, sl], ALU.mult, ALU.add))
                link(v.tensor_copy(sidx[:, 0, sl], slotf[:, 0, sl]))
                dve.wait_ge(ex0_ok, p + 1)
                link(v.reduce_sum(ssum[:, sl], pe_[:, sl, :], AXX))
                link(v.reciprocal(ssum[:, sl], ssum[:, sl]))
                v.scalar_tensor_tensor(coef[:, 0, sl], ssum[:, sl], tg[:, 2:3], keep[:, sl], ALU.mult, ALU.mult).then_inc(idx0_ok, 1)

            def swiglu_shared(p, m):
                n = HC * p + m
                dve.wait_ge(sh_th, n + 1)
                if m == 0 and p > 0:
                    dve.wait_ge(sho_ps, p)
                t = thb[:, n % 2, :]
                link(v.scalar_tensor_tensor(t, t, 1.0, ps[:, 2 * (m % 2), :], ALU.add, ALU.mult))
                v.scalar_tensor_tensor(hT[:, m, :], t, 0.5, ps[:, 2 * (m % 2) + 1, :], ALU.mult, ALU.mult).then_inc(sh_ok, 1)

            head(0)
            head(1)
            tail(0)
            head(2)
            tail(1)
            head(3)
            residual(0, 0, yT_ps, 1, x1_ok)
            dve.wait_ge(x1_ok, 1)
            stats(2, 1, 0, 4)
            normal(2, 1, 0, 4)
            tail(2)
            route0(0)
            tail(3)
            for m in range(HC):
                swiglu_shared(0, m)
            slots0(0)
            residual(0, 2, sho_ps, 1, xs_ok)
            residual(1, 0, yT_ps, 2, x1_ok)
            dve.wait_ge(x1_ok, 2)
            stats(3, 1, 4, 4)
            normal(3, 1, 4, 4)
            route0(1)
            slots0(1)
            for m in range(HC):
                swiglu_shared(1, m)
            residual(1, 2, sho_ps, 2, xs_ok)
            dve.wait_ge(xs_ok, 2)
            v.memset(mT[:, :, :], 0.0)
            v.memset(bias3[:, :], 0.0).then_inc(b3z_ok, 1)

            def swiglu_expert(e):
                dve.wait_ge(h0_th, e + 1)
                t = the[:, e % 2, :]
                b = 2 + 2 * (e % 2)
                link(v.scalar_tensor_tensor(t, t, 1.0, ps[:, b, 0:HP], ALU.add, ALU.mult))
                v.scalar_tensor_tensor(he[:, e % 2, :], t, 0.5, ps[:, b + 1, 0:HP], ALU.mult, ALU.mult).then_inc(h0_ok, 1)

            def k_evac(t):
                b, j = divmod(t, TPB)
                dve.wait_ge(k_ps, t + 1)
                v.tensor_copy(ktb[:, b, :, j * P:(j + 1) * P], ps16(7)).then_inc(ktb_ok, 1)

            swiglu_expert(0)
            for e in range(E):
                if e + 1 < E:
                    swiglu_expert(e + 1)
                k_evac(e)

            for b in range(B):
                dve.wait_ge(got0_in[b], 16)
                for i in range(2 * b, 2 * b + 2):
                    last = v.scalar_tensor_tensor(x_sb[:, i, :], got0[:, i, :], coef[:, 0, i:i + 1], x_sb[:, i, :], ALU.mult, ALU.add)
                    if i < 2 * b + 1 or b < B - 1:
                        link(last)
                if b == B - 1:
                    last.then_inc(x2_all, 1)
                    dve.wait_ge(x2_all, 1)
                stats(4 + b, 2, 2 * b, 2)
            dve.wait_ge(ids_ok, 1)
            for b in range(B):
                normal(4 + b, 2, 2 * b, 2)

            def nat_max(b, s):
                n = 6 * b + s
                h0, nh, qt = NAT[s]
                dve.wait_ge(nat_ps, n + 1)
                bank = 2 * (n % 3) if n < 6 else 0
                v.reduce_max(mmax[:, b % 2, qt, h0:h0 + nh].rearrange("p (h a) -> p a h", a=2),
                             sub_cols(ps[:, bank:bank + 2, :], nh), AXX).then_inc(nat_ok, 1)
                if s == 5:
                    dve.wait_ge(nat_ok, 6 * b + 6)
                    v.tensor_scalar(mneg[:, b % 2, :, 0], mmax[:, b % 2], -1.0, None, ALU.mult).then_inc(mhi_ok, 1)
                    dve.wait_ge(mhi_ok, b + 1)
                    v.scalar_tensor_tensor(mneg[:, b % 2, :, 1], mmax[:, b % 2], -1.0, mneg[:, b % 2, :, 0], ALU.mult, ALU.subtract).then_inc(mneg_ok, 1)

            def q_evac_odd(b):
                if b >= 2:
                    dve.wait_ge(st_ps, 3 * 2 * (b - 1))
                for j in range(TPB):
                    dve.wait_ge(misc_ps, USE[("q", 2 * b + j)] + 1)
                    v.tensor_copy(qtb[b % 2][P // 2:P, 1, :, j * P:(j + 1) * P], ps16(7)[P // 2:P]).then_inc(q_odd, 1)

            def weights_low(u):
                n = 3 * u + 2
                dve.wait_ge(p32_ok, n + 1)
                dve.wait_ge(st_exp, n + 1)
                v.tensor_tensor(pT[:, 1, u % 2, 2, :], p32[:, n % 2, :], pT[:, 0, u % 2, 2, :], ALU.subtract).then_inc(lo_dve, 1)

            def attend(u):
                b, hg = divmod(u, 2)
                dve.wait_ge(pv_ps, u + 1)
                o = ps[:, 6, 0:2 * 8 * (HD + 1)].rearrange("p (q h c) -> p q h c", q=2, h=8)
                r = den[:, u % 2]
                link(v.reciprocal(r, o[:, :, :, HD]))
                link(v.tensor_scalar(r, r, tg[:, 1:2], None, ALU.mult))
                v.tensor_tensor(att[:, u % 2], o[:, :, :, 0:HD], r.unsqueeze(3).to_broadcast([P, 2, 8, HD]), ALU.mult).then_inc(pv_ok, 1)
                dve.wait_ge(pv_ok, u + 1)
                xs = x_sb[:, 2 * b:2 * b + 2, hg * P:(hg + 1) * P]
                link(v.tensor_tensor(xs, xs, att[:, u % 2].rearrange("p q h c -> p q (h c)"), ALU.add))

            def route1(b):
                sl = slice(2 * b, 2 * b + 2)
                n = USE[("l", b)]
                dve.wait_ge(misc_ps, n + 1)
                v.tensor_tensor(lg[:, sl, :], ps[:, 7, 0:2 * E].rearrange("p (i e) -> p i e", e=E),
                                rb_sb[:, :].unsqueeze(1).to_broadcast([P, 2, E]), ALU.add).then_inc(misc_free, 1)
                dve.wait_ge(misc_free, n + 1)
                for i in range(2 * b, 2 * b + 2):
                    choose(i, lg[:, i, :])
                dve.wait_ge(v_chain, step[0])
                v.tensor_tensor(ssum[:, sl], mx[:, sl, 1], mx[:, sl, 0], ALU.subtract).then_inc(ex1_in, 1)
                link(v.tensor_copy(ixf[:, sl, :], ix[:, sl, 0:2]))
                for k in range(2):
                    link(v.tensor_tensor(oh[:, k, sl, :], iota8[:, :].unsqueeze(1).to_broadcast([P, 2, E]),
                                         ixf[:, sl, k:k + 1].to_broadcast([P, 2, E]), ALU.is_equal))
                v.tensor_tensor(ohb[:, sl, :], oh[:, 0, sl, :], oh[:, 1, sl, :], ALU.add).then_inc(oh1_ok, 1)

            def slots1(b):
                sl = slice(2 * b, 2 * b + 2)
                n = USE[("c", b)]
                cum = ps[:, 7, 0:2 * E].rearrange("p (i e) -> p i e", e=E)
                dve.wait_ge(misc_ps, n + 1)
                link(v.tensor_tensor(cumoh[:, 0, sl, :], cum, oh[:, 0, sl, :], ALU.mult))
                v.tensor_tensor(cumoh[:, 1, sl, :], cum, oh[:, 1, sl, :], ALU.mult).then_inc(misc_free, 1)
                dve.wait_ge(misc_free, n + 1)
                link(v.reduce_sum(pos[:, :, sl], cumoh[:, :, sl, :], AXX))
                for k in range(2):
                    link(v.scalar_tensor_tensor(slotf[:, k, sl], ixf[:, sl, k], float(T), pos[:, k, sl], ALU.mult, ALU.add))
                v.tensor_scalar(sidx[:, :, sl], slotf[:, :, sl], -1.0, None, ALU.add).then_inc(idx1_ok, 1)
                dve.wait_ge(ex1_ok, b + 1)
                link(v.tensor_scalar(keep[:, sl], ssum[:, sl], 1.0, None, ALU.add))
                link(v.reciprocal(keep[:, sl], keep[:, sl]))
                link(v.tensor_scalar(coef[:, 0, sl], keep[:, sl], tg[:, 3:4], None, ALU.mult))
                link(v.tensor_tensor(coef[:, 1, sl], coef[:, 0, sl], ssum[:, sl], ALU.mult))

            q_evac_odd(0)
            for s in range(3):
                nat_max(0, s)
            q_evac_odd(1)
            for s in range(3, 6):
                nat_max(0, s)
            for u in range(2 * B):
                if u % 2 == 1 and u >= 3:
                    normal(8 + (u - 3) // 2, 3, u - 3, 2)
                for s in range(3):
                    if u // 2 + 1 < B:
                        nat_max(u // 2 + 1, 3 * (u % 2) + s)
                if u >= 1:
                    attend(u - 1)
                if u % 2 == 1 and u // 2 + 2 < B:
                    q_evac_odd(u // 2 + 2)
                weights_low(u)
                if u % 2 == 0 and u >= 2:
                    stats(8 + u // 2 - 1, 3, u - 2, 2)
                if u % 2 == 1 and u >= 3:
                    route1((u - 3) // 2)
                if u % 2 == 0 and u >= 4:
                    slots1((u - 4) // 2)
            attend(2 * B - 1)
            stats(7 + B, 3, 2 * B - 2, 2)
            slots1(B - 2)
            normal(7 + B, 3, 2 * B - 2, 2)
            route1(B - 1)
            slots1(B - 1)

            dve.wait_ge(misc_ps, USE[("n", 0)] + 1)
            v.tensor_copy(cnt[:, 0, :], ps[:, 7, 0:E]).then_inc(misc_free, 1)
            dve.wait_ge(misc_free, USE[("n", 0)] + 1)
            link(v.tensor_scalar(cnt[:, 1, :], cnt[:, 0, :], 1.0 / P, (P - 1.0) / P - 0.5 + 1.0 / 512, ALU.mult, ALU.add))
            link(v.tensor_copy(nti[:, :], cnt[:, 1, :]))
            link(v.tensor_copy(cnt[:, 1, :], nti[:, :]))
            link(v.memset(cnt[:, 0, :], 1.0))
            link(v.tensor_tensor_scan(cnt[:, 2, :], cnt[:, 0, :], cnt[:, 1, :], 0.0, ALU.mult, ALU.add))
            ends = cnt[:, 2, :].unsqueeze(1).to_broadcast([P, NTILE1, E])
            link(v.tensor_tensor(tle[:, 0], ends, iota_t[:, :].unsqueeze(2).to_broadcast([P, NTILE1, E]), ALU.is_le))
            link(v.tensor_tensor(tle[:, 1], tle[:, 0], ends, ALU.mult))
            link(v.reduce_sum(tabf[:, 0, :], tle[:, 0], AXX))
            link(v.reduce_max(tabf[:, 1, :], tle[:, 1], AXX))
            link(v.tensor_tensor(tabf[:, 1, :], iota_t[:, :], tabf[:, 1, :], ALU.subtract))
            link(v.tensor_scalar(tabf[:, 2, :], tabf[:, 0, :], float(T), None, ALU.mult))
            link(v.scalar_tensor_tensor(tabf[:, 2, :], tabf[:, 1, :], float(P), tabf[:, 2, :], ALU.mult, ALU.add))
            link(v.tensor_scalar(tabi[:, 0, :], tabf[:, 0, :], float(E - 1), None, ALU.min))
            v.tensor_scalar(tabi[:, 1, :], tabf[:, 2, :], float(E * T - P), None, ALU.min).then_inc(tab_ok, 1)
            def clip(t):
                b = t % 2
                g = ps[:, 2 + b, :].rearrange("p (i c) -> p c i", c=2)
                dve.wait_ge(gu_ps, t + 1)
                v.tensor_scalar(gh[:, b, :], g[:, 0, :], 7.0, 0.5, ALU.min, ALU.mult).then_inc(gh_ok, 1)
                link(v.tensor_scalar(up[:, b, :], g[:, 1, :], -7.0, 7.0, ALU.max, ALU.min))

            def act_tile(t):
                b = t % 2
                dve.wait_ge(gh_ok, t + 1)
                dve.wait_ge(th1_ok, t + 1)
                link(v.scalar_tensor_tensor(glu[:, b, :], th1[:, b, :], 1.0, gh[:, b, :], ALU.add, ALU.mult))
                if t >= 2:
                    dve.wait_ge(actT_ps, t - 1)
                v.scalar_tensor_tensor(actv[:, b, :], up[:, b, :], 1.0, glu[:, b, :], ALU.add, ALU.mult).then_inc(act_ok, 1)

            clip(0)
            act_tile(0)
            for t in range(1, NTILE1):
                clip(t)
                act_tile(t)

            for b in range(B):
                dve.wait_ge(got1_in[b], 32)
                for i in range(2 * b, 2 * b + 2):
                    link(v.scalar_tensor_tensor(x_sb[:, i, :], got1[:, 0, i, :], coef[:, 0, i:i + 1], x_sb[:, i, :], ALU.mult, ALU.add))
                    v.scalar_tensor_tensor(x_sb[:, i, :], got1[:, 1, i, :], coef[:, 1, i:i + 1], x_sb[:, i, :], ALU.mult, ALU.add).then_inc(x4_ok, 1)

        @block.tensor
        def _(pe):
            t_ = nc.tensor

            def mm(o, l, r, start, stop):
                return t_.matmul(o, lhsT=l, rhs=r, start=start, stop=stop)

            pe.wait_ge(consts_ok, 1)
            for n in range(NG):
                p, h = divmod(n, KC)
                if n >= 2:
                    pe.wait_ge(kT_ok, n - 1)
                pe.wait_ge(xn_ok, 4 * p + 4)
                for j in range(4):
                    last = t_.transpose(ps[:, n % 2, j * P:(j + 1) * P], xn[:, 4 * p + j, h * P:(h + 1) * P], ident[:, :])
                last.then_inc(kT_ps, 1)
                if n >= 2:
                    pe.wait_ge(vT_ok, n - 1)
                pe.wait_ge(ctx_in_s[p], 16)
                for j in range(4):
                    last = t_.transpose(ps[:, 2 + n % 2, j * P:(j + 1) * P], ctx_sb[:, 4 * p + j, h * P:(h + 1) * P], ident[:, :])
                last.then_inc(vT_ps, 1)

            def y_back(p):
                pe.wait_ge(y_ok, KC * p + KC)
                if p > 0:
                    pe.wait_ge(xs_ok, p)
                for j in range(4):
                    for h in range(KC):
                        last = t_.transpose(ps[:, 4 + j // 2, (j % 2) * D + h * P:(j % 2) * D + (h + 1) * P],
                                            T1[:, h, j // 2, 1 + (j % 2) * P:1 + (j % 2 + 1) * P], ident[:, :])
                last.then_inc(yT_ps, 1)

            def x1_turn(p):
                pe.wait_ge(xn_ok, NT + 4 * p + 4)
                pe.wait_ge(kT_ok, NG)
                if p > 0:
                    pe.wait_ge(sh_ok, HC * p)
                for h in range(KC):
                    for j in range(4):
                        last = t_.transpose(ps[:, h, j * P:(j + 1) * P], xn[:, 4 * p + j, h * P:(h + 1) * P], ident[:, :])
                    last.then_inc(x1T_ps, 1)

            def logits0(p):
                pe.wait_ge(x1T_ok, KC * (p + 1))
                pe.wait_ge(wg_in, 16)
                if p > 0:
                    pe.wait_ge(lg0_ok, p)
                for j in range(4):
                    for k in range(KC):
                        last = mm(ps[:, 6, j * E:(j + 1) * E], xT[:, k, (4 * p + j) * P:(4 * p + j + 1) * P], wg_sb[:, k, :],
                                  k == 0, k == KC - 1)
                last.then_inc(lg0_ps, 1)

            def shared_up(p, m):
                n = HC * p + m
                pe.wait_ge(sw_in, 64)
                pe.wait_ge(pads_ok, 1)
                pe.wait_ge(vT_ok, NG)
                if n >= 2:
                    pe.wait_ge(sh_ok, n - 1)
                for c, w in enumerate((sw1_sb, sw3_sb)):
                    for k in range(KC):
                        last = mm(ps[:, 2 * (m % 2) + c, :], w[:, k, m * P:(m + 1) * P], xT[:, k, 512 * p:512 * p + 512],
                                  k == 0, k == KC - 1)
                last.then_inc(sh_ps, 1)

            def count(i, j0, o):
                for j in range(i):
                    mm(o, onesb[:, :], ohb[:, j, :], j == 0, False)
                return mm(o, upper[:, :], ohb[:, i, :], i == 0, True)

            def cum0(p):
                pe.wait_ge(oh0_ok, p + 1)
                if p > 0:
                    pe.wait_ge(cum0_ok, p)
                for j in range(4):
                    last = count(4 * p + j, 0, ps[:, 7, j * E:(j + 1) * E])
                last.then_inc(cum0_ps, 1)

            def shared_down(p):
                pe.wait_ge(sh_ok, HC * (p + 1))
                pe.wait_ge(x1_ok, p + 1)
                for j in range(4):
                    for m in range(HC):
                        last = mm(ps[:, 4 + j // 2, (j % 2) * D:(j % 2 + 1) * D], hT[:, m, j * P:(j + 1) * P], sw2_sb[:, m, :],
                                  m == 0, m == HC - 1)
                last.then_inc(sho_ps, 1)

            for p in range(NP2):
                y_back(p)
                x1_turn(p)
                logits0(p)
                shared_up(p, 0)
                if p > 0:
                    cum0(p)
                shared_up(p, 1)
                if p == 0:
                    cum0(p)
                shared_up(p, 2)
                shared_down(p)

            def misc_take(key):
                n = USE[key]
                if n >= 1:
                    pe.wait_ge(misc_free, n)
                    if USES[n - 1][0] == "q":
                        pe.wait_ge(q_odd, USES[n - 1][1] + 1)
                else:
                    pe.wait_ge(ktb_ok, NT)

            def k_turn(t):
                pe.wait_ge(k_lo, t + 1)
                if t >= 1:
                    pe.wait_ge(ktb_ok, t)
                else:
                    pe.wait_ge(cum0_ok, NP2)
                for h in range(NPAIR):
                    last = t_.transpose(ps16(7)[:, h, :], spl[:, t % 2, 2 * h:2 * h + 2, :, :].rearrange("p h s c -> p (h s c)"), ident16[:, :])
                last.then_inc(k_ps, 1)

            def xd_turn(e):
                if e % 2 == 0:
                    pe.wait_ge(disp0_out[e // 2], 16)
                pe.wait_ge(sh_ok, HC * NP2)
                if e >= 2:
                    pe.wait_ge(xdT_ok, e - 1)
                for k in range(KC):
                    last = t_.transpose(ps[:, e % 2, k * P:(k + 1) * P], xd[:, e, k * P:(k + 1) * P], ident[:, :])
                last.then_inc(xdT_ps, 1)

            def expert_up(e):
                if e % (E // 2) == 0:
                    pe.wait_ge(w1_in[e // (E // 2)], 16 * (E // 2))
                    pe.wait_ge(w3_in[e // (E // 2)], 16 * (E // 2))
                    pe.wait_ge(xs_ok, NP2)
                pe.wait_ge(xdT_ok, e + 1)
                if e >= 2:
                    pe.wait_ge(h0_ok, e - 1)
                for c, w in enumerate((w1_sb, w3_sb)):
                    for m in range(HC):
                        for k in range(KC):
                            last = mm(ps[:, 2 + 2 * (e % 2) + c, m * P:(m + 1) * P], w[:, e, k, m * P:(m + 1) * P], xdT[:, e % 2, k, :],
                                      k == 0, k == KC - 1)
                last.then_inc(h0_ps, 1)

            def expert_down(e):
                pe.wait_ge(h0_ok, e + 1)
                if e == 0:
                    pe.wait_ge(w2_in, 16 * (E + 1))
                    pe.wait_ge(lg0_ok, NP2)
                if e >= 1:
                    pe.wait_ge(oe0_ok, e)
                for m in range(HC):
                    last = mm(ps[:, 6, 0:D], he[:, e % 2, m * P:(m + 1) * P], w2_sb[:, e, m, :], m == 0, m == HC - 1)
                last.then_inc(oe0_ps, 1)

            xd_turn(0)
            xd_turn(1)
            expert_up(0)
            for e in range(E):
                if e + 2 < E:
                    xd_turn(e + 2)
                if e + 1 < E:
                    expert_up(e + 1)
                k_turn(e)
                expert_down(e)

            def q_turn(i):
                pe.wait_ge(q_lo, i + 1)
                misc_take(("q", i))
                if i == 0:
                    pe.wait_ge(oe0_ok, E)
                for h in range(NPAIR):
                    last = t_.transpose(ps16(7)[:, h, :], spl[:, i % 2, 2 * h:2 * h + 2, :, :].rearrange("p h s c -> p (h s c)"), ident16[:, :])
                last.then_inc(misc_ps, 1)

            def nat(b, s):
                n = 6 * b + s
                h0, nh, qt = NAT[s]
                if s == 0:
                    pe.wait_ge(misc_free, USE[("q", 2 * b + 1)] + 1)
                    pe.wait_ge(q_odd, 2 * b + 2)
                    pe.wait_ge(qz_ok[b % 2], 1)
                if n >= (3 if n < 6 else 1):
                    pe.wait_ge(nat_ok, n - 2 if n < 6 else n)
                w = (qt + 1) * P
                bank = 2 * (n % 3) if n < 6 else 0
                for h in range(h0, h0 + nh):
                    o = ps[:, bank + h % 2, (h - h0) // 2 * w:(h - h0) // 2 * w + w]
                    mm(o, qtb[b % 2][:, h % 2, h // 2, qt * P:(qt + 1) * P], ktb[:, b, h // 2, 0:w], True, False)
                    last = mm(o[:, w - P:w], identb[:, :], causal[:, :], False, True)
                last.then_inc(nat_ps, 1)

            def scores_t(u, s):
                n = 3 * u + s
                b, hg = divmod(u, 2)
                h0, nh, kt = [(8 * hg, 4, 0), (8 * hg + 4, 4, 0), (8 * hg, 8, 1)][s]
                if s == 0 and hg == 0:
                    pe.wait_ge(misc_free, USE[("m", b)] + 1)
                if n >= 2:
                    pe.wait_ge(st_exp, n - 1)
                w = S - kt * P
                for h in range(h0, h0 + nh):
                    o = ps[:, 2 + 2 * (n % 2) + h % 2, (h - h0) // 2 * w:(h - h0) // 2 * w + w]
                    mm(o, sel[:, h, :], mT[:, b % 2, kt * P:S], True, False)
                    mm(o, ktb[:, b, h // 2, kt * P:(kt + 1) * P], qtb[b % 2][:, h % 2, h // 2, kt * P:S], False, False)
                    last = mm(o[:, 0:P], identb[:, :], causalT[:, :], False, True)
                last.then_inc(st_ps, 1)

            def weigh(u):
                b, hg = divmod(u, 2)
                pe.wait_ge(st_exp, 3 * (u + 1))
                pe.wait_ge(lo_pool, 2 * (u + 1))
                pe.wait_ge(lo_dve, u + 1)
                if u >= 1:
                    pe.wait_ge(pv_ok, u)
                parts = ((0, 0), (0, 1), (1, 0))
                c = HD + 1
                for j in range(8):
                    h = 8 * hg + j
                    early = pT[:, :, u % 2, j // 4, (j % 4) * S:(j % 4 + 1) * S]
                    late = pT[:, :, u % 2, 2, j * P:(j + 1) * P]
                    o = ps[:, 6, j * c:(j + 1) * c]
                    for n, (l, m) in enumerate(parts):
                        mm(o, early[:, l, 0:P], v17[:, m, 2 * b, h, :], n == 0, n == 2)
                    o = ps[:, 6, (8 + j) * c:(9 + j) * c]
                    for n, (l, m) in enumerate(parts):
                        mm(o, early[:, l, P:S], v17[:, m, 2 * b, h, :], n == 0, False)
                    for n, (l, m) in enumerate(parts):
                        last = mm(o, late[:, l], v17[:, m, 2 * b + 1, h, :], False, n == 2)
                last.then_inc(pv_ps, 1)

            def route_x(b):
                pe.wait_ge(xn_ok, 3 * NT + 2 * b + 2)
                misc_take(("x", b))
                for k in range(KC):
                    for j in range(TPB):
                        last = t_.transpose(ps[:, 7, (k * TPB + j) * P:(k * TPB + j + 1) * P], xn[:, 2 * b + j, k * P:(k + 1) * P], ident[:, :])
                last.then_inc(misc_ps, 1)
                misc_take(("l", b))
                for j in range(TPB):
                    for k in range(KC):
                        last = mm(ps[:, 7, j * E:(j + 1) * E], xrT[:, k, j * P:(j + 1) * P], rw_sb[:, k, :], k == 0, k == KC - 1)
                last.then_inc(misc_ps, 1)

            def route_c(b):
                pe.wait_ge(oh1_ok, b + 1)
                misc_take(("c", b))
                for j in range(TPB):
                    last = count(2 * b + j, 0, ps[:, 7, j * E:(j + 1) * E])
                last.then_inc(misc_ps, 1)

            pe.wait_ge(sel_ok, 1)
            pe.wait_ge(v_lo, NT)
            pe.wait_ge(bias_p_ok, 1)
            q_turn(0)
            q_turn(1)
            for s in range(3):
                nat(0, s)
            q_turn(2)
            q_turn(3)
            for s in range(3, 6):
                nat(0, s)
            for u in range(2 * B):
                b = u // 2
                if u % 2 == 0:
                    pe.wait_ge(mneg_ok, b + 1)
                    misc_take(("m", b))
                    for q in range(2):
                        last = t_.transpose(ps[0:2 * HEADS, 7, 0:S // 2].bitcast(BF16)[:, q * P:(q + 1) * P],
                                            mneg[:, b % 2, q].rearrange("p l h -> p (l h)"), identb[:, :])
                    last.then_inc(misc_ps, 1)
                for s in range(3):
                    scores_t(u, s)
                    if b + 1 < B:
                        nat(b + 1, 3 * (u % 2) + s)
                if u >= 1:
                    weigh(u - 1)
                if u % 2 == 1 and b + 2 < B:
                    q_turn(u + 3)
                    q_turn(u + 4)
                if u % 2 == 1 and u >= 3:
                    route_x((u - 3) // 2)
                if u % 2 == 0 and u >= 4:
                    route_c((u - 4) // 2)
            weigh(2 * B - 1)
            route_c(B - 2)
            route_x(B - 1)
            route_c(B - 1)
            misc_take(("n", 0))
            for j in range(NT):
                last = mm(ps[:, 7, 0:E], onesb[:, :], ohb[:, j, :], j == 0, j == NT - 1)
            last.then_inc(misc_ps, 1)

            pe.wait_ge(tab_ok, 1)
            pe.wait_ge(bias_rows, 96)
            pe.wait_ge(gu_in, 16 * E)
            pe.wait_ge(dn_in, 16 * E)
            ex = {}

            def xt_turn(t):
                pe.wait_ge(xt_in[t % NXT], 16 * (t // NXT + 1))
                if t >= 2:
                    pe.wait_ge(xtT_ok, t - 1)
                for k in range(KC):
                    last = t_.transpose(ps[:, t % 2, k * P:(k + 1) * P], xt[:, t % NXT, k * P:(k + 1) * P], ident[:, :])
                last.then_inc(xtT_ps, 1)

            def gate_up_tile(t):
                ex[t] = pe.value_load(tabi[0:1, 0, t:t + 1], min_val=0, max_val=E - 1)
                pe.wait_ge(xtT_ok, t + 1)
                if t >= 2:
                    pe.wait_ge(act_ok, t - 1)
                o = ps[:, 2 + t % 2, :]
                mm(o, onesb[:, :], bias3[:, bass.ds(ex[t] * GU, GU)], True, False)
                for k in range(KC):
                    last = mm(o, xtT[:, t % 2, k, :], gu_sb[:, bass.ds(ex[t] * (KC * GU) + k * GU, GU)], False, k == KC - 1)
                last.then_inc(gu_ps, 1)

            def act_turn(t):
                pe.wait_ge(act_ok, t + 1)
                if t >= 2:
                    pe.wait_ge(actT_ok, t - 1)
                for k in range(KC):
                    last = t_.transpose(ps[:, 4 + t % 2, k * P:(k + 1) * P], actv[:, t % 2, k * P:(k + 1) * P], ident[:, :])
                last.then_inc(actT_ps, 1)

            def down_tile(t):
                pe.wait_ge(actT_ok, t + 1)
                if t >= 2:
                    pe.wait_ge(mk1_ok, t - 1)
                o = ps[:, 6 + t % 2, 0:D]
                mm(o, onesb[:, :], bias3[:, bass.ds(ex[t] * D + E * GU, D)], True, False)
                for k in range(KC):
                    last = mm(o, actT[:, t % 2, k, :], dn_sb[:, bass.ds(ex[t] * (KC * D) + k * D, D)], False, k == KC - 1)
                last.then_inc(oe1_ps, 1)

            xt_turn(0)
            xt_turn(1)
            gate_up_tile(0)
            for t in range(NTILE1):
                if t + 2 < NTILE1:
                    xt_turn(t + 2)
                if t + 1 < NTILE1:
                    gate_up_tile(t + 1)
                act_turn(t)
                if t >= 1:
                    down_tile(t - 1)
            down_tile(NTILE1 - 1)


_INS = ['x', 'ctx_2048', 'g_xattn', 'g_ffn', 'L0_xattn_w', 'L0_xattn_u', 'L0_ffn_Wg', 'L0_ffn_W1', 'L0_ffn_W3', 'L0_ffn_W2',
        'L0_ffn_sw1', 'L0_ffn_sw3', 'L0_ffn_sw2', 'L1_ffn_router_weight', 'L1_ffn_router_bias', 'L1_ffn_gate_up_proj',
        'L1_ffn_gate_up_proj_bias', 'L1_ffn_down_proj', 'L1_ffn_down_proj_bias']


def kernel(**inputs):
    import numpy as np
    import concourse.bacc as bacc
    from concourse.bass_utils import run_bass_kernel_spmd as run

    nc = bacc.Bacc("TRN2", target_bir_lowering=False, num_devices=1)
    arrays, args = {}, []
    for name in _INS:
        a = np.ascontiguousarray(inputs[name])
        arrays[f"in_{name}"] = a
        args.append(nc.dram_tensor(f"in_{name}", a.shape, mybir.dt.from_np(a.dtype), kind="ExternalInput").ap())
    out = nc.dram_tensor("out_x", inputs['x'].shape, FP32, kind="ExternalOutput").ap()
    flamingo_kernel(nc, *args, out)
    r = run(nc, [arrays], core_ids=[0])
    return r.results[0]["out_x"]
```

```python
import concourse.bass as bass
from concourse import mybir
from contextlib import ExitStack

P = 128
FP32 = mybir.dt.float32
FP16 = mybir.dt.float16
BF16 = mybir.dt.bfloat16
U32 = mybir.dt.uint32
I32 = mybir.dt.int32
ALU = mybir.AluOpType
ACT = mybir.ActivationFunctionType
AXX = mybir.AxisListType.X


def flamingo_kernel(nc, x, ctx_in, g_xattn, g_ffn, wkv_w, wkv_u, Wg, W1, W3, W2, sw1, sw3, sw2,
                    router_w, router_b, gate_up, gate_up_b, down, down_b, out):
    B, S, D = x.shape
    T = B * S
    NT = T // P
    TPB = S // P
    KC = D // P
    E = Wg.shape[1]
    H = W1.shape[2]
    HC = -(-H // P)
    HP = HC * P
    HR = H - (HC - 1) * P
    CAP = T // E
    I = down.shape[1]
    GU = 2 * I
    HEADS = 16
    HD = D // HEADS
    NPAIR = HEADS // 2
    NTILE1 = (2 * T) // P + E - 1
    NEG = -1.0e38
    EPS = 1.0e-5
    FAR = 4096.0
    SEQ = S + 1
    NP2 = NT // 4
    NG = NP2 * KC
    MASK = -1.0e30
    WS = 64.0
    NXT = 12
    RW = D + 4
    SMALL = 3 + KC

    x_v = x.rearrange("b s d -> (b s) d").rearrange("(i p) d -> p i d", p=P)
    ctx_v = ctx_in.rearrange("b s d -> (b s) d").rearrange("(i p) d -> p i d", p=P)
    out_v = out.rearrange("b s d -> (b s) d").rearrange("(i p) d -> p i d", p=P)

    disp0 = nc.dram_tensor("disp0", [E * CAP, RW], FP32, kind="Internal").ap()
    made0 = nc.dram_tensor("made0", [T, D], FP32, kind="Internal").ap()
    disp1 = nc.dram_tensor("disp1", [E * T, RW], FP32, kind="Internal").ap()
    made1 = nc.dram_tensor("made1", [2 * T, D], FP32, kind="Internal").ap()

    ctx = ExitStack()
    with ctx:
        def sb(name, shape, dt=FP32):
            return ctx.enter_context(nc.sbuf_tensor(name, shape, dt))

        def sem(name):
            return ctx.enter_context(nc.semaphore(name))

        ident = sb("ident", [P, P])
        ident16 = sb("ident16", [P, P], FP16)
        identb = sb("identb", [P, P], BF16)
        upper = sb("upper", [P, P], BF16)
        onesb = sb("onesb", [P, P], BF16)
        scales = sb("scales", [P, 2, P], BF16)
        causal = sb("causal", [P, P], BF16)
        causalT = sb("causalT", [P, P], BF16)
        iota8 = sb("iota8", [P, E])
        iota_t = sb("iota_t", [P, NTILE1])
        nhalf = sb("nhalf", [P, NT])
        zrow = sb("zrow", [P, 2 * RW])
        ids = sb("ids", [P, 2, NT], U32)
        gates = sb("gates", [P, 4])
        tg = sb("tg", [P, 4])
        w_sb = sb("w_sb", [P, KC])
        u_sb = sb("u_sb", [P, KC])
        wg_sb = sb("wg_sb", [P, KC, E])
        rw_sb = sb("rw_sb", [P, KC, E])
        rb_sb = sb("rb_sb", [P, E])
        NB = E * (GU + D)
        bias_in = sb("bias_in", [P, NB // P])
        bias_r = sb("bias_r", [P, 2, NB // P])
        bias_p = sb("bias_p", [P, 3, NB // P], BF16)
        bias3 = sb("bias3", [P, NB], BF16)
        st = sb("st", [P, 4, NT, 6])
        mv = sb("mv", [P, 4, NT, 2])
        rs = sb("rs", [P, 4, NT])
        lg = sb("lg", [P, NT, E])
        mx = sb("mx", [P, NT, E])
        ix = sb("ix", [P, NT, E], U32)
        ixf = sb("ixf", [P, NT, 2])
        pe_ = sb("pe_", [P, NT, E])
        oh = sb("oh", [P, 2, NT, E])
        ohb = sb("ohb", [P, NT, E], BF16)
        cumoh = sb("cumoh", [P, 2, NT, E])
        ssum = sb("ssum", [P, NT])
        pos = sb("pos", [P, 2, NT])
        keep = sb("keep", [P, NT])
        slotf = sb("slotf", [P, 2, NT])
        sidx = sb("sidx", [P, 2, NT], U32)
        coef = sb("coef", [P, 2, NT])
        cnt = sb("cnt", [P, 4, E])
        nti = sb("nti", [P, E], I32)
        tle = sb("tle", [P, 2, NTILE1, E])
        tabf = sb("tabf", [P, 3, NTILE1])
        tabi = sb("tabi", [P, 2, NTILE1], I32)
        x_sb = sb("x_sb", [P, NT, D])
        ctx_sb = sb("ctx_sb", [P, NT, D])
        v17 = sb("v17", [P, 2, NT, HEADS, HD + 1], FP16)
        xn = sb("xn", [P, NT, RW])
        xT = sb("xT", [P, KC, T])
        wts = sb("wts", [P, 3 * E * KC * HP])
        w1_sb = wts[:, 0:E * KC * HP].rearrange("p (e k h) -> p e k h", e=E, k=KC)
        w3_sb = wts[:, E * KC * HP:2 * E * KC * HP].rearrange("p (e k h) -> p e k h", e=E, k=KC)
        w2_sb = wts[:, 2 * E * KC * HP:2 * E * KC * HP + E * HC * D].rearrange("p (e c d) -> p e c d", e=E, c=HC)
        WE = KC * (GU + D)
        w16 = wts[:, 0:E * WE].bitcast(FP16)

        def split_at(e, l, w0, w1):
            return w16[:, (2 * e + l) * WE + w0:(2 * e + l) * WE + w1]

        spare = E * WE + NT * D
        stage_at = [4 * WE, 5 * WE, spare, 6 * WE, 7 * WE, spare, spare, E * WE]
        stage = [wts[:, w:w + WE] for w in stage_at]
        assert 4 * WE >= E * KC * HP and 6 * WE <= (E + E // 2) * KC * HP and 2 * WE <= E // 2 * KC * HP
        assert E == 8 and spare + WE <= 3 * E * KC * HP - NT * RW
        sw1_sb = sb("sw1_sb", [P, KC, HP])
        sw3_sb = sb("sw3_sb", [P, KC, HP])
        sw2_sb = sb("sw2_sb", [P, HC, D])
        hT = sb("hT", [P, HC, 512])
        thb = sb("thb", [P, 2, 512])
        arena = sb("arena", [P, 13440])
        at = [0]

        def take(words):
            at[0] += words
            assert at[0] <= 13440
            return arena[:, at[0] - words:at[0]]

        def seqs(n=1):
            return take(n * 2 * SEQ).rearrange("p (n a t) -> p n a t", n=n, a=2)

        w0 = seqs(KC)
        kT = seqs(NG)
        vT = take(NG * 512).rearrange("p (n a t) -> p n a t", n=NG, a=2)
        O, A2, E2, EV, NO, AA, EE, T1 = [seqs(2) for _ in range(8)]
        PP, QQ, T2 = EV, E2, NO
        at[0] = 0
        ktb = take(B * NPAIR * S // 2).bitcast(FP16).rearrange("p (b h t) -> p b h t", b=B, h=NPAIR)
        p32 = take(2 * 1024).rearrange("p (n c) -> p n c", n=2)
        pT = take(2 * 2 * 3 * 512).bitcast(FP16).rearrange("p (l n s c) -> p l n s c", l=2, n=2, s=3)
        qtb = [buf.bitcast(FP16).rearrange("p (a h t) -> p a h t", a=2, h=NPAIR)
               for buf in (ctx_sb[:, :, :].rearrange("p i d -> p (i d)"), wts[:, E * KC * (GU + D):E * KC * (GU + D) + NT * D],
                           xT[:, :, :].rearrange("p k t -> p (k t)"))]
        assert E * KC * (GU + D) + NT * D <= 3 * E * KC * HP - NT * RW
        spl = thb[:, :, :].rearrange("p n t -> p (n t)").bitcast(FP16).rearrange("p (n h s c) -> p n h s c", n=2, h=HEADS, s=4)
        sel = hT[:, 0:2, :].rearrange("p n t -> p (n t)").bitcast(BF16).rearrange("p (h k) -> p h k", h=HEADS)
        assert at[0] >= 4096 + 4 * D + 2 * KC * P + 4 * HP
        mmax = take(2 * 2 * HEADS).rearrange("p (n q h) -> p n q h", n=2, q=2)
        mneg = take(4 * HEADS).bitcast(BF16).rearrange("p (n q l h) -> p n q l h", n=2, q=2, l=2)
        mT = take(S).bitcast(BF16).rearrange("p (n q) -> p n q", n=2)
        den = take(2 * 16).rearrange("p (n q h) -> p n q h", n=2, q=2)
        att = sw1_sb[:, :, :].rearrange("p k h -> p (k h)")[:, 0:512].rearrange("p (n q h c) -> p n q h c", n=2, q=2, h=8)
        xrT = sw2_sb[:, :, :].rearrange("p k h -> p (k h)")[:, 0:KC * 256].rearrange("p (k t) -> p k t", k=KC)
        at[0] = 0
        xt = take(NXT * RW).rearrange("p (n d) -> p n d", n=NXT)
        xtT = take(3 * D).bitcast(FP16).rearrange("p (n l k t) -> p n l k t", n=3, l=2, k=KC)
        gh = take(2 * I).rearrange("p (n i) -> p n i", n=2)
        up = take(2 * I).rearrange("p (n i) -> p n i", n=2)
        th1 = take(2 * I).rearrange("p (n i) -> p n i", n=2)
        glu = take(2 * I).rearrange("p (n i) -> p n i", n=2)
        actv = take(2 * I).rearrange("p (n i) -> p n i", n=2)
        asp = take(2 * I).bitcast(FP16).rearrange("p (n l i) -> p n l i", n=2, l=2)
        actT = take(2 * I).bitcast(FP16).rearrange("p (n l k t) -> p n l k t", n=2, l=2, k=KC)
        mk1 = take(4 * D).rearrange("p (n d) -> p n d", n=4)
        got1 = take(2 * NT * D).rearrange("p (k i d) -> p k i d", k=2, i=NT)

        xd = xn
        got0 = xT[:, :, :].rearrange("p k t -> p (k t)").rearrange("p (i d) -> p i d", i=NT)
        xn2 = wts[:, 3 * E * KC * HP - NT * RW:3 * E * KC * HP].rearrange("p (i d) -> p i d", i=NT)
        at[0] = B * NPAIR * S // 2
        xdT = take(2 * D).rearrange("p (n k t) -> p n k t", n=2, k=KC)
        the = take(2 * HP).rearrange("p (n h) -> p n h", n=2)
        he = take(2 * HP).rearrange("p (n h) -> p n h", n=2)
        mk0 = take(4 * D).rearrange("p (n d) -> p n d", n=4)

        ps = ctx.enter_context(nc.psum_tensor("ps", [P, 8, 512], FP32))

        def ps16(b):
            return ps[:, b, :].bitcast(FP16).rearrange("p (h t) -> p h t", t=P)

        x_in = [sem(f"x_in{p}") for p in range(NP2)]
        ctx_in_s = [sem(f"ctx_in{p}") for p in range(NP2)]
        small_in, wu_in = sem("small_in"), sem("wu_in")
        bias_in_s = sem("bias_in_s")
        bias_rows = sem("bias_rows")
        sw_in = sem("sw_in")
        w13_in = [sem(f"w13_in{c}") for c in range(2)]
        w2_in = sem("w2_in")
        w_in = [sem(f"w_in{c}") for c in range(3)]
        w_scaled, w_hi, w_lo_pool, w_lo_dve = sem("w_scaled"), sem("w_hi"), sem("w_lo_pool"), sem("w_lo_dve")
        zero_out, zero1_out = sem("zero_out"), sem("zero1_out")
        pool_c = sem("pool_c")
        consts_ok = sem("consts_ok")
        sel_ok = sem("sel_ok")
        bias_p_ok = sem("bias_p_ok")
        zrow_ok = sem("zrow_ok")
        pads_ok, scan_pads_ok = sem("pads_ok"), sem("scan_pads_ok")
        w0_ok = sem("w0_ok")
        tg_ok = sem("tg_ok")
        p32_ok = sem("p32_ok")
        var_ok = sem("var_ok")
        rstd_ok = sem("rstd_ok")
        xn_ok = sem("xn_ok")
        kT_ps, vT_ps, kT_ok, vT_ok = sem("kT_ps"), sem("vT_ps"), sem("kT_ok"), sem("vT_ok")
        o_ok, a2_ok, no_ok, ee_ok = sem("o_ok"), sem("a2_ok"), sem("no_ok"), sem("ee_ok")
        e2_ok, aa_ok, ev_ok, t2_ok = sem("e2_ok"), sem("aa_ok"), sem("ev_ok"), sem("t2_ok")
        den_ok = sem("den_ok")
        q_ok, t1_ok, num_ok = sem("q_ok"), sem("t1_ok"), sem("num_ok")
        a2_exp, e2_exp, aa_exp, ee_exp = sem("a2_exp"), sem("e2_exp"), sem("aa_exp"), sem("ee_exp")
        y_ok, yT_ps, x1_ok = sem("y_ok"), sem("yT_ps"), sem("x1_ok")
        x1T_ps, x1T_ok = sem("x1T_ps"), sem("x1T_ok")
        lg0_ps, lg0_ok, ex0_in, ex0_ok = sem("lg0_ps"), sem("lg0_ok"), sem("ex0_in"), sem("ex0_ok")
        oh0_ok, cum0_ps, cum0_ok, idx0_ok = sem("oh0_ok"), sem("cum0_ps"), sem("cum0_ok"), sem("idx0_ok")
        disp0_in, disp0_out = sem("disp0_in"), [sem(f"disp0_out{c}") for c in range(4)]
        sh_ps, sh_th, sh_ok, sho_ps, xs_ok = sem("sh_ps"), sem("sh_th"), sem("sh_ok"), sem("sho_ps"), sem("xs_ok")
        xdT_ps, xdT_ok, h0_ps, h0_th, h0_ok = sem("xdT_ps"), sem("xdT_ok"), sem("h0_ps"), sem("h0_th"), sem("h0_ok")
        oe0_ps, oe0_ok, made0_in, got0_in = sem("oe0_ps"), sem("oe0_ok"), [sem(f"made0_in{c}") for c in range(4)], [sem(f"got0_in{b}") for b in range(B)]
        ids_ok, qz_ok, xn2_ok = sem("ids_ok"), [sem(f"qz_ok{c}") for c in range(3)], sem("xn2_ok")
        q_odd, lo_pool, lo_dve, b3z_ok = sem("q_odd"), sem("lo_pool"), sem("lo_dve"), sem("b3z_ok")
        k_hi, k_lo, k_ps, ktb_ok, q_hi, q_lo = sem("k_hi"), sem("k_lo"), sem("k_ps"), sem("ktb_ok"), sem("q_hi"), sem("q_lo")
        v_lo = sem("v_lo")
        misc_ps, misc_free = sem("misc_ps"), sem("misc_free")
        nat_ps, nat_ok, mneg_ok = sem("nat_ps"), sem("nat_ok"), sem("mneg_ok")
        st_ps, st_exp, pv_ps, pv_ok = sem("st_ps"), sem("st_exp"), sem("pv_ps"), sem("pv_ok")
        ex1_in, ex1_ok, oh1_ok, idx1_ok = sem("ex1_in"), sem("ex1_ok"), sem("oh1_ok"), sem("idx1_ok")
        disp1_in, tab_ok = sem("disp1_in"), sem("tab_ok")
        xt_in = [sem(f"xt_in{c}") for c in range(8)]
        xtT_ps, xtT_ok, gu_ps, gh_ok, th1_ok, act_ok = sem("xtT_ps"), sem("xtT_ok"), sem("gu_ps"), sem("gh_ok"), sem("th1_ok"), sem("act_ok")
        xlo_ok, act_hi, act_lo, aT_ps, aT_ok, oe1_ps, mk1_ok = sem("xlo_ok"), sem("act_hi"), sem("act_lo"), sem("aT_ps"), sem("aT_ok"), sem("oe1_ps"), sem("mk1_ok")
        made1_in, got1_in, x4_ok, coef_ok, out_done = [sem(f"made1_in{c}") for c in range(4)], [sem(f"got1_in{b}") for b in range(B)], sem("x4_ok"), sem("coef_ok"), sem("out_done")
        v_chain = sem("v_chain")

        block = ctx.enter_context(nc.Block())

        @block.sync
        def _(sp):
            for p in range(NP2):
                sp.dma_start(x_sb[:, 4 * p:4 * p + 4, :], x_v[:, 4 * p:4 * p + 4, :]).then_inc(x_in[p], 16)
                sp.dma_start(ctx_sb[:, 4 * p:4 * p + 4, :], ctx_v[:, 4 * p:4 * p + 4, :]).then_inc(ctx_in_s[p], 16)
            sp.dma_start(wg_sb[:, :, :], Wg.rearrange("(k p) e -> p k e", p=P)).then_inc(sw_in, 16)
            sp.dma_start(sw1_sb[:, :, 0:H], sw1.rearrange("(k p) h -> p k h", p=P)).then_inc(sw_in, 16)
            sp.dma_start(sw3_sb[:, :, 0:H], sw3.rearrange("(k p) h -> p k h", p=P)).then_inc(sw_in, 16)
            sp.wait_ge(pads_ok, 1)
            sp.dma_start(sw2_sb[:, 0:HC - 1, :], sw2[0:(HC - 1) * P, :].rearrange("(c p) d -> p c d", p=P)).then_inc(sw_in, 16)
            sp.dma_start(sw2_sb[0:HR, HC - 1, :], sw2[(HC - 1) * P:H, :]).then_inc(sw_in, 16)
            empty = zrow[:, :].unsqueeze(1).to_broadcast([P, NT // 2, 2 * RW])
            sp.wait_ge(zrow_ok, 1)
            sp.dma_start(disp0.rearrange("(p r) d -> p (r d)", p=P).rearrange("p (a c) -> p a c", c=2 * RW), empty).then_inc(zero_out, 16)
            sp.dma_start(made0.rearrange("(p r) d -> p r d", p=P), zrow[:, 0:D].unsqueeze(1).to_broadcast([P, NT, D])).then_inc(zero_out, 16)
            for c in range(2):
                es = slice(c * E // 2, (c + 1) * E // 2)
                for w, dst in ((W1, w1_sb), (W3, w3_sb)):
                    for e in range(es.start, es.stop):
                        sp.dma_start(dst[:, e, :, 0:H], w[e].rearrange("(k p) h -> p k h", p=P)).then_inc(w13_in[c], 16)
            for e in range(E):
                sp.dma_start(w2_sb[:, e, 0:HC - 1, :], W2[e, 0:(HC - 1) * P, :].rearrange("(c p) d -> p c d", p=P)).then_inc(w2_in, 16)
            sp.dma_start(w2_sb[0:HR, :, HC - 1, :], W2[:, (HC - 1) * P:H, :].rearrange("e p d -> p e d")).then_inc(w2_in, 16)
            GB = E * GU // P
            sp.dma_start(bias_in[:, 0:GB], gate_up_b.rearrange("e j -> (e j)").rearrange("(p c) -> p c", p=P)).then_inc(bias_in_s, 16)
            sp.dma_start(bias_in[:, GB:], down_b.rearrange("e j -> (e j)").rearrange("(p c) -> p c", p=P)).then_inc(bias_in_s, 16)
            for n in range(E):
                sp.dma_start(disp1[n * T:(n + 1) * T, :].rearrange("(p r) d -> p (r d)", p=P).rearrange("p (a c) -> p a c", c=2 * RW), empty).then_inc(zero1_out, 16)
            sp.wait_ge(disp0_in, 16 * NT)
            for c in range(4):
                sp.dma_start(xd[:, 2 * c:2 * c + 2, :], disp0[2 * c * P:(2 * c + 2) * P, :].rearrange("(e p) d -> p e d", p=P)).then_inc(disp0_out[c], 16)
            sp.wait_ge(bias_p_ok, 1)
            sp.wait_ge(b3z_ok, 1)
            for k in range(3):
                sp.dma_start(bias3[k:k + 1, 0:E * GU], bias_p[:, k, 0:GB]).then_inc(bias_rows, 16)
                sp.dma_start(bias3[k:k + 1, E * GU:], bias_p[:, k, GB:]).then_inc(bias_rows, 16)

            def weights1(e):
                sp.dma_start(stage[e][:, 0:KC * GU].rearrange("p (k j) -> p k j", k=KC),
                             gate_up[e].rearrange("(k p) j -> p k j", p=P)).then_inc(w_in[e % 3], 16)
                sp.dma_start(stage[e][:, KC * GU:WE].rearrange("p (k j) -> p k j", k=KC),
                             down[e].rearrange("(k p) j -> p k j", p=P)).then_inc(w_in[e % 3], 16)

            sp.wait_ge(h0_ps, E // 2)
            weights1(0)
            weights1(1)
            for c in range(4):
                sp.wait_ge(made0_in[c], 16 * (E // 4))
            for b in range(B):
                sp.dma_start(got0[:, 2 * b:2 * b + 2, :], made0[b * S:(b + 1) * S, :].rearrange("(i p) d -> p i d", p=P)).then_inc(got0_in[b], 16)
            sp.wait_ge(oe0_ps, E)
            sp.wait_ge(w_lo_dve, 2)
            for e in range(2, E):
                if e == 5:
                    sp.wait_ge(w_lo_pool, 1)
                if e == 6:
                    sp.wait_ge(w_lo_pool, 4)
                if e == E - 1:
                    sp.wait_ge(st_ps, 3 * 4)
                weights1(e)
            sp.wait_ge(disp1_in, 16 * 2 * NT)
            sp.wait_ge(tab_ok, 1)
            for t in range(NTILE1):
                if t >= 8:
                    sp.wait_ge(xtT_ps, t - 7)
                if t >= NXT:
                    sp.wait_ge(made1_in[t % 4], 16 * ((t - NXT) // 4 + 1))
                row = sp.value_load(tabi[0:1, 1, t:t + 1], min_val=0, max_val=E * T - P)
                sp.dma_start(xt[:, t % NXT, :], disp1[bass.ds(row, P), :]).then_inc(xt_in[t % 8], 16)
            for c in range(4):
                sp.wait_ge(made1_in[c], 16 * len(range(c, NTILE1, 4)))
            for b in range(B):
                for k in range(2):
                    sp.dma_start(got1[:, k, 2 * b:2 * b + 2, :], made1[k * T + b * S:k * T + (b + 1) * S, :].rearrange("(i p) d -> p i d", p=P)).then_inc(got1_in[b], 16)
            for i in range(NT):
                sp.wait_ge(x4_ok, i + 1)
                sp.dma_start(out_v[:, i, :], x_sb[:, i, :]).then_inc(out_done, 16)
            sp.wait_ge(out_done, 16 * NT)
            sp.wait_ge(zero_out, 16 * 2)
            sp.wait_ge(zero1_out, 16 * E)

        def cur(buf, n):
            return buf[:, n, :, 1:SEQ]

        def prev(buf, n):
            return buf[:, n, :, 0:S]

        def flat(buf, n):
            return buf[:, n, :, :].rearrange("p a t -> p (a t)")

        NAT = [(4 * s, 4, 1) if s < 2 else (0, 8, 0) for s in range(3)] + [(8 + 4 * s, 4, 1) if s < 2 else (8, 8, 0) for s in range(3)]

        def sub_cols(buf2, nh):
            return buf2[:, :, 0:nh // 2 * (1024 // nh)].rearrange("p a (h c) -> p a h c", h=nh // 2)

        @block.gpsimd
        def _(pool):
            step = [0]

            def link(ins):
                step[0] += 1
                ins.then_inc(pool_c, 1)
                pool.wait_ge(pool_c, step[0])

            g = nc.gpsimd
            link(g.memset(zrow[:, :], 0.0))
            g.memset(zrow[:, D:D + 1].bitcast(U32), int(FAR))
            g.memset(zrow[:, RW + D:RW + D + 1].bitcast(U32), int(FAR)).then_inc(zrow_ok, 1)
            g.memset(nhalf[:, :], -0.5)
            link(g.memset(ident[:, :], 0.0))
            link(g.affine_select(out=ident[:, :], in_=ident[:, :], compare_op=ALU.not_equal, fill=1.0, base=0,
                                 pattern=[[-1, P]], channel_multiplier=1))
            g.tensor_copy(ident16[:, :], ident[:, :])
            g.tensor_copy(identb[:, :], ident[:, :])
            g.memset(scales[:, 0, :], WS)
            g.memset(scales[:, 1, :], WS * WS)
            link(g.memset(onesb[:, :], 1.0))
            g.affine_select(out=upper[:, :], in_=onesb[:, :], compare_op=ALU.is_ge, fill=0.0, base=0,
                            pattern=[[1, P]], channel_multiplier=-1)
            link(g.memset(causal[:, :], 0.0))
            g.affine_select(out=causal[:, :], in_=causal[:, :], compare_op=ALU.is_ge, fill=MASK, base=0,
                            pattern=[[-1, P]], channel_multiplier=1)
            link(g.memset(causalT[:, :], 0.0))
            g.affine_select(out=causalT[:, :], in_=causalT[:, :], compare_op=ALU.is_ge, fill=MASK, base=0,
                            pattern=[[1, P]], channel_multiplier=-1)
            g.iota(iota8[:, :], pattern=[[1, E]], base=0, channel_multiplier=0, allow_small_or_imprecise_dtypes=True)
            g.iota(iota_t[:, :], pattern=[[1, NTILE1]], base=0, channel_multiplier=0,
                   allow_small_or_imprecise_dtypes=True).then_inc(consts_ok, 1)
            g.iota(ids[:, :, :], pattern=[[T, 2], [P, NT]], base=0, channel_multiplier=1)
            link(g.memset(xn[:, :, D:RW], 0.0))
            g.tensor_copy(xn[:, :, D].bitcast(U32), ids[:, 0, :])
            g.memset(w0[:, :, :, 0:1], NEG)
            g.memset(kT[:, :, :, 0:1], NEG)
            g.memset(A2[:, :, :, 0:1], 0.0)
            g.memset(E2[:, :, :, 0:1], 0.0)
            g.memset(EV[:, :, :, 0:1], 0.0).then_inc(scan_pads_ok, 1)
            pool.wait_ge(scan_pads_ok, 1)

            def rstd(n, stage, i0, ni, scale=1.0):
                pool.wait_ge(var_ok, n + 1)
                r = rs[:, stage, i0:i0 + ni]
                link(g.tensor_scalar(r, mv[:, stage, i0:i0 + ni, 1], EPS, None, ALU.add))
                last = g.tensor_tensor(r, r, nhalf[:, 0:ni], ALU.pow)
                if scale != 1.0:
                    link(last)
                    last = g.tensor_scalar(r, r, scale, None, ALU.mult)
                last.then_inc(rstd_ok, 1)

            rstd(0, 0, 0, 4)
            g.memset(sw1_sb[:, :, H:HP], 0.0)
            g.memset(sw3_sb[:, :, H:HP], 0.0)
            g.memset(w1_sb[:, :, :, H:HP], 0.0)
            link(g.memset(w3_sb[:, :, :, H:HP], 0.0))
            link(g.memset(sw2_sb[HR:P, HC - 1, :], 0.0))
            g.memset(w2_sb[HR:P, :, HC - 1, :], 0.0).then_inc(pads_ok, 1)
            pool.wait_ge(pads_ok, 1)

            rstd(1, 0, 4, 4)

            def exponents(n):
                b = n % 2
                pool.wait_ge(kT_ok, n + 1)
                pool.wait_ge(o_ok, n + 1)
                if n >= 2:
                    pool.wait_ge(y_ok, n - 1)
                g.tensor_tensor(cur(E2, b), cur(kT, n), cur(O, b), ALU.subtract).then_inc(e2_ok, 1)
                pool.wait_ge(no_ok, n + 1)
                g.tensor_tensor(cur(AA, b), prev(O, b), cur(NO, b), ALU.subtract).then_inc(aa_ok, 1)

            def weighted_values(n):
                b = n % 2
                pool.wait_ge(vT_ok, n + 1)
                pool.wait_ge(e2_exp, n + 1)
                g.tensor_tensor(cur(EV, b), cur(E2, b), vT[:, n], ALU.mult).then_inc(ev_ok, 1)
                pool.wait_ge(ee_exp, n + 1)
                pool.wait_ge(aa_ok, n + 1)
                g.tensor_tensor(cur(T2, b), cur(EE, b), vT[:, n], ALU.mult).then_inc(t2_ok, 1)

            def denominator(n):
                b = n % 2
                pool.wait_ge(q_ok, n + 1)
                pool.wait_ge(aa_exp, n + 1)
                pool.wait_ge(a2_ok, n + 1)
                pool.wait_ge(no_ok, n + 1)
                link(g.tensor_tensor(cur(O, b), cur(AA, b), prev(QQ, b), ALU.mult))
                g.tensor_tensor(cur(O, b), cur(O, b), cur(EE, b), ALU.add).then_inc(den_ok, 1)
                pool.wait_ge(t1_ok, n + 1)
                g.tensor_tensor(cur(T1, b), cur(T1, b), cur(T2, b), ALU.add).then_inc(num_ok, 1)

            exponents(0)
            weighted_values(0)
            exponents(1)
            weighted_values(1)
            denominator(0)
            denominator(1)
            exponents(2)
            weighted_values(2)
            exponents(3)
            weighted_values(3)
            rstd(2, 1, 0, 4)
            denominator(2)
            denominator(3)

            def scatter0(p):
                pool.wait_ge(zero_out, 16 * 2)
                pool.wait_ge(idx0_ok, p + 1)
                for i in range(4 * p, 4 * p + 4):
                    g.indirect_dma_start(
                        out=disp0[:, :], out_offset=bass.IndirectOffsetOnAxis(ap=sidx[:, 0, i:i + 1], axis=0),
                        in_=xn[:, i, :], in_offset=None, bounds_check=E * CAP - 1, oob_is_err=False,
                    ).then_inc(disp0_in, 16)

            scatter0(0)
            rstd(3, 1, 4, 4)
            pool.wait_ge(bias_in_s, 32)
            src = bias_in[:, :]
            for k in range(3):
                link(g.tensor_copy(bias_p[:, k, :], src))
                if k < 2:
                    link(g.tensor_tensor(bias_r[:, k, :], src, bias_p[:, k, :], ALU.subtract))
                    src = bias_r[:, k, :]
            g.memset(v17[:, 1, :, :, HD:HD + 1], 0.0)
            g.memset(v17[:, 0, :, :, HD:HD + 1], 1.0).then_inc(bias_p_ok, 1)
            scatter0(1)

            pool.wait_ge(sho_ps, NP2)
            link(g.memset(sel[:, :, :], 0.0))
            for l in range(2):
                last = g.affine_select(out=sel[:, :, :], in_=sel[:, :, :], compare_op=ALU.not_equal, fill=1.0, base=-l * HEADS,
                                       pattern=[[-1, HEADS], [0, P]], channel_multiplier=1)
                if l == 0:
                    link(last)
            last.then_inc(sel_ok, 1)
            for t in range(NT):
                c = ctx_sb[:, t, :].rearrange("p (h c) -> p h c", h=HEADS)
                dst = spl[:, t % 2].rearrange("p h (r l) c -> p h l r c", l=2)
                pool.wait_ge(k_hi, 2 * t + 1)
                g.tensor_tensor(dst[:, :, 1], c.unsqueeze(2).to_broadcast([P, HEADS, 2, HD]), dst[:, :, 0], ALU.subtract).then_inc(k_lo, 1)
                pool.wait_ge(k_hi, 2 * t + 2)
                g.tensor_tensor(v17[:, 1, t, :, 0:HD], c, v17[:, 0, t, :, 0:HD], ALU.subtract).then_inc(v_lo, 1)
                pool.wait_ge(oe0_ok, t + 1)
                g.indirect_dma_start(
                    out=made0[:, :], out_offset=bass.IndirectOffsetOnAxis(ap=xd[:, t, D:D + 1].bitcast(U32), axis=0),
                    in_=mk0[:, t % 4, :], in_offset=None, bounds_check=T - 1, oob_is_err=False,
                ).then_inc(made0_in[t % 4], 16)
            for c in range(4):
                pool.wait_ge(made0_in[c], 16 * (E // 4))
            g.tensor_copy(xn[:, :, D].bitcast(U32), ids[:, 0, :])
            link(g.memset(xn2[:, :, D:RW], 0.0))
            g.tensor_copy(xn2[:, :, D].bitcast(U32), ids[:, 1, :]).then_inc(ids_ok, 1)

            def query_rstd(b):
                rstd(4 + b, 2, 2 * b, 2, scale=float(HD) ** -0.5)

            query_rstd(0)
            query_rstd(1)

            def q_low(b):
                for j in range(TPB):
                    i = 2 * b + j
                    q = xn[:, i, 0:D].rearrange("p (h c) -> p h c", h=HEADS)
                    pool.wait_ge(q_hi, i + 1)
                    lo = spl[:, i % 2, :, 2:4, :]
                    g.tensor_tensor(lo, q.unsqueeze(2).to_broadcast([P, HEADS, 2, HD]), spl[:, i % 2, :, 0:2, :], ALU.subtract).then_inc(q_lo, 1)

            def weights_low(u, s):
                n = 3 * u + s
                pool.wait_ge(p32_ok, n + 1)
                pool.wait_ge(st_exp, n + 1)
                g.tensor_tensor(pT[:, 1, u % 2, s, :], p32[:, n % 2, :], pT[:, 0, u % 2, s, :], ALU.subtract).then_inc(lo_pool, 1)

            def scatter1(b):
                pool.wait_ge(idx1_ok, b + 1)
                pool.wait_ge(xn2_ok, b + 1)
                pool.wait_ge(zero1_out, 16 * E)
                for i in range(2 * b, 2 * b + 2):
                    for k, rows in enumerate((xn, xn2)):
                        g.indirect_dma_start(
                            out=disp1[:, :], out_offset=bass.IndirectOffsetOnAxis(ap=sidx[:, k, i:i + 1], axis=0),
                            in_=rows[:, i, :], in_offset=None, bounds_check=E * T - 1, oob_is_err=False,
                        ).then_inc(disp1_in, 16)

            def split_low(e):
                pool.wait_ge(w_hi, e + 1)
                g.tensor_tensor(split_at(e, 1, 0, WE), stage[e], split_at(e, 0, 0, WE), ALU.subtract).then_inc(w_lo_pool, 1)

            q_low(0)
            split_low(2)
            q_low(1)
            query_rstd(2)
            query_rstd(3)
            split_low(3)
            split_low(4)
            split_after = {2: 5}
            for u in range(2 * B):
                for s in range(2):
                    weights_low(u, s)
                    if s == 0 and u % 2 == 1 and u >= 3:
                        rstd(8 + (u - 3) // 2, 3, u - 3, 2)
                if u % 2 == 0 and u // 2 + 2 < B:
                    q_low(u // 2 + 2)
                if u % 2 == 1 and u >= 5 and u + 1 < 2 * B:
                    scatter1((u - 5) // 2)
                if u in split_after:
                    split_low(split_after[u])
            scatter1(B - 3)
            rstd(7 + B, 3, 2 * B - 2, 2)
            scatter1(B - 2)
            scatter1(B - 1)

            def act_low(t):
                pool.wait_ge(act_ok, t + 1)
                pool.wait_ge(act_hi, t + 1)
                g.tensor_tensor(asp[:, t % 2, 1], actv[:, t % 2, :], asp[:, t % 2, 0], ALU.subtract).then_inc(act_lo, 1)

            def scatter_made(t):
                pool.wait_ge(mk1_ok, t + 1)
                g.indirect_dma_start(
                    out=made1[:, :], out_offset=bass.IndirectOffsetOnAxis(ap=xt[:, t % NXT, D:D + 1].bitcast(U32), axis=0),
                    in_=mk1[:, t % 4, :], in_offset=None, bounds_check=2 * T - 1, oob_is_err=False,
                ).then_inc(made1_in[t % 4], 16)

            for t in range(NTILE1):
                act_low(t)
                if t >= 2:
                    scatter_made(t - 2)
            scatter_made(NTILE1 - 2)
            scatter_made(NTILE1 - 1)
            for c in range(4):
                pool.wait_ge(made1_in[c], 16 * len(range(c, NTILE1, 4)))

        USES = [("q", i) for i in range(4)] + [("m", 0)]
        for u in range(2 * B + 1):
            if u % 2 == 1 and u // 2 + 2 < B:
                USES += [("q", u + 3), ("q", u + 4)]
            if u % 2 == 1 and u // 2 + 1 < B:
                USES.append(("m", u // 2 + 1))
            if u % 2 == 1 and u >= 3:
                USES.append(("x", (u - 3) // 2))
            if u % 2 == 0 and u >= 4:
                USES += [("l", (u - 4) // 2), ("c", (u - 4) // 2)]
        USES += [("x", B - 1), ("l", B - 1), ("c", B - 1), ("n", 0)]
        USE = {key: n for n, key in enumerate(USES)}

        @block.scalar
        def _(act):
            a = nc.scalar
            act.dma_start(w_sb[:, :], wkv_w.rearrange("(k p) -> p k", p=P), allow_slow_non_contiguous=True).then_inc(wu_in, 16)
            act.dma_start(u_sb[:, :], wkv_u.rearrange("(k p) -> p k", p=P), allow_slow_non_contiguous=True).then_inc(wu_in, 16)
            act.dma_start(gates[:, 0:2], g_xattn.partition_broadcast(P)).then_inc(small_in, 16)
            act.dma_start(gates[:, 2:4], g_ffn.partition_broadcast(P)).then_inc(small_in, 16)
            act.dma_start(rb_sb[:, :], router_b.partition_broadcast(P)).then_inc(small_in, 16)
            for k in range(KC):
                act.dma_start(rw_sb[:, k, :], router_w[:, k * P:(k + 1) * P].rearrange("e p -> p e"), allow_slow_non_contiguous=True).then_inc(small_in, 16)

            def evac(dst, src, ready, n, done):
                act.wait_ge(ready, n)
                a.activation(dst, src, ACT.Copy).then_inc(done, 1)

            def kv(n):
                if n == 0:
                    act.wait_ge(scan_pads_ok, 1)
                evac(cur(kT, n), ps[:, n % 2, :].rearrange("p (a t) -> p a t", a=2), kT_ps, n + 1, kT_ok)
                evac(vT[:, n], ps[:, 2 + n % 2, :].rearrange("p (a t) -> p a t", a=2), vT_ps, n + 1, vT_ok)

            def exps(n):
                for buf, ready, done in ((A2, a2_ok, a2_exp), (E2, e2_ok, e2_exp), (EE, ee_ok, ee_exp), (AA, aa_ok, aa_exp)):
                    act.wait_ge(ready, n + 1)
                    a.activation(cur(buf, n % 2), cur(buf, n % 2), ACT.Exp).then_inc(done, 1)

            kv(0)
            kv(1)
            exps(0)
            exps(1)
            kv(2)
            kv(3)
            act.wait_ge(small_in, 16 * SMALL)
            a.activation(tg[:, :], gates[:, :], ACT.Tanh).then_inc(tg_ok, 1)
            exps(2)
            exps(3)

            def x1_evac(p):
                for h in range(KC):
                    evac(xT[:, h, 512 * p:512 * p + 512], ps[:, h, :], x1T_ps, 2 * p + h + 1, x1T_ok)

            def ex0(p):
                act.wait_ge(ex0_in, p + 1)
                a.activation(pe_[:, 4 * p:4 * p + 4, :], pe_[:, 4 * p:4 * p + 4, :], ACT.Exp).then_inc(ex0_ok, 1)

            def sh_tanh(p):
                for m in range(HC):
                    n = HC * p + m
                    act.wait_ge(sh_ps, n + 1)
                    if n >= 2:
                        act.wait_ge(sh_ok, n - 1)
                    a.activation(thb[:, n % 2, :], ps[:, 2 * (m % 2), :], ACT.Tanh, scale=0.5).then_inc(sh_th, 1)
                    if m == 0:
                        ex0(p)

            for p in range(NP2):
                x1_evac(p)
                sh_tanh(p)

            def kv_high(t):
                c = ctx_sb[:, t, :].rearrange("p (h c) -> p h c", h=HEADS)
                if t >= 2:
                    act.wait_ge(k_ps, t - 1)
                dst = spl[:, t % 2].rearrange("p h (r l) c -> p h l r c", l=2)
                a.activation(dst[:, :, 0], c.unsqueeze(2).to_broadcast([P, HEADS, 2, HD]), ACT.Copy).then_inc(k_hi, 1)
                a.activation(v17[:, 0, t, :, 0:HD], c, ACT.Copy).then_inc(k_hi, 1)

            def xd_evac(e):
                act.wait_ge(xdT_ps, e + 1)
                a.activation(xdT[:, e % 2], ps[:, e % 2, 0:D].rearrange("p (k t) -> p k t", k=KC), ACT.Copy).then_inc(xdT_ok, 1)

            def h_tanh(e):
                act.wait_ge(h0_ps, e + 1)
                a.activation(the[:, e % 2, :], ps[:, 2 + 2 * (e % 2), 0:HP], ACT.Tanh, scale=0.5).then_inc(h0_th, 1)

            def oe_evac(e):
                act.wait_ge(oe0_ps, e + 1)
                if e >= 4:
                    act.wait_ge(made0_in[e % 4], 16 * (e // 4))
                a.activation(mk0[:, e % 4, :], ps[:, 6, 0:D], ACT.Copy).then_inc(oe0_ok, 1)

            def split_high(e):
                act.wait_ge(w_in[e % 3], 32 * (e // 3 + 1))
                if e >= 6:
                    act.wait_ge(w_lo_pool, e - 4)
                a.activation(stage[e], stage[e], ACT.Copy, scale=WS).then_inc(w_scaled, 1)
                act.wait_ge(w_scaled, e + 1)
                a.activation(split_at(e, 0, 0, WE), stage[e], ACT.Copy).then_inc(w_hi, 1)

            xd_evac(0)
            xd_evac(1)
            act.wait_ge(sho_ps, NP2)
            kv_high(0)
            h_tanh(0)
            for e in range(E):
                if e + 2 < E:
                    xd_evac(e + 2)
                if e + 1 < E:
                    kv_high(e + 1)
                    h_tanh(e + 1)
                oe_evac(e)
                if e in (E - 3, E - 2):
                    split_high(e - (E - 3))

            def misc_evac(key, dst, src):
                n = USE[key]
                act.wait_ge(misc_ps, n + 1)
                a.activation(dst, src, ACT.Copy).then_inc(misc_free, 1)

            def q_split(b):
                for j in range(TPB):
                    i = 2 * b + j
                    act.wait_ge(xn_ok, 2 * NT + i + 1)
                    if i >= 2:
                        act.wait_ge(misc_ps, USE[("q", i - 2)] + 1)
                    else:
                        act.wait_ge(k_ps, NT)
                    q = xn[:, i, 0:D].rearrange("p (h c) -> p h c", h=HEADS).unsqueeze(2).to_broadcast([P, HEADS, 2, HD])
                    a.activation(spl[:, i % 2, :, 0:2, :], q, ACT.Copy).then_inc(q_hi, 1)

            def q_evac(b, tiles=(0, 1)):
                if b >= 3:
                    act.wait_ge(st_ps, 3 * 2 * (b - 2))
                for j in tiles:
                    misc_evac(("q", 2 * b + j), qtb[b % 3][0:P // 2, 0, :, j * P:(j + 1) * P], ps16(7)[0:P // 2])

            def exp_t(u, subs=range(3)):
                for s in subs:
                    n = 3 * u + s
                    act.wait_ge(st_ps, n + 1)
                    if u >= 2 and s == 0:
                        act.wait_ge(pv_ps, u - 1)
                    if n >= 2:
                        if (n - 2) % 3 < 2:
                            act.wait_ge(lo_pool, 2 * ((n - 2) // 3) + (n - 2) % 3 + 1)
                        else:
                            act.wait_ge(lo_dve, (n - 2) // 3 + 1)
                    nh = 4 if s < 2 else 8
                    src = sub_cols(ps[:, 2 + 2 * (n % 2):4 + 2 * (n % 2), :], nh)
                    for dst, done in ((p32[:, n % 2, :], p32_ok), (pT[:, 0, u % 2, s, :], st_exp)):
                        a.activation(dst.rearrange("p (h a c) -> p a h c", a=2, h=nh // 2), src, ACT.Exp).then_inc(done, 1)

            def ex1(b):
                act.wait_ge(ex1_in, b + 1)
                a.activation(ssum[:, 2 * b:2 * b + 2], ssum[:, 2 * b:2 * b + 2], ACT.Exp).then_inc(ex1_ok, 1)

            def x_evac(b):
                misc_evac(("x", b), xrT[:, :, :], ps[:, 7, :].rearrange("p (k t) -> p k t", k=KC))

            def second_copy(b):
                act.wait_ge(xn_ok, 3 * NT + 2 * b + 2)
                act.wait_ge(ids_ok, 1)
                a.activation(xn2[:, 2 * b:2 * b + 2, 0:D], xn[:, 2 * b:2 * b + 2, 0:D], ACT.Copy).then_inc(xn2_ok, 1)

            q_split(0)
            split_high(2)
            q_evac(0)
            q_split(1)
            split_high(3)
            q_evac(1)
            split_high(4)

            def m_evac(b):
                misc_evac(("m", b), mT[0:2 * HEADS, b % 2, :], ps[0:2 * HEADS, 7, 0:S // 2].bitcast(BF16))

            m_evac(0)
            split_after = {1: 5}
            for u in range(2 * B):
                b = u // 2
                ahead = u % 2 == 1 and b + 2 < B
                for c in range(3):
                    exp_t(u, [c])
                    if ahead and c < 2:
                        q_evac(b + 2, [c])
                    if c == 0 and u % 2 == 0 and b + 2 < B:
                        q_split(b + 2)
                if u % 2 == 1 and b + 1 < B:
                    m_evac(b + 1)
                if u in split_after:
                    split_high(split_after[u])
                if u % 2 == 1 and u >= 3:
                    x_evac((u - 3) // 2)
                    second_copy((u - 3) // 2)
                if u % 2 == 0 and u >= 4:
                    ex1((u - 4) // 2)
            ex1(B - 2)
            split_high(6)
            x_evac(B - 1)
            second_copy(B - 1)
            split_high(7)
            ex1(B - 1)

            def xt_evac(t):
                if t >= 3:
                    act.wait_ge(gu_ps, t - 2)
                evac(xtT[:, t % 3, 0], ps[:, t % 2, 0:D].rearrange("p (k t) -> p k t", k=KC), xtT_ps, t + 1, xtT_ok)

            def tile_tanh(t):
                act.wait_ge(gh_ok, t + 1)
                a.activation(th1[:, t % 2, :], gh[:, t % 2, :], ACT.Tanh, scale=1.702).then_inc(th1_ok, 1)

            def act_high(t):
                act.wait_ge(act_ok, t + 1)
                if t >= 2:
                    act.wait_ge(aT_ps, t - 1)
                    act.wait_ge(act_lo, t - 1)
                a.activation(asp[:, t % 2, 0], actv[:, t % 2, :], ACT.Copy).then_inc(act_hi, 1)

            def at_evac(t):
                if t >= 2:
                    act.wait_ge(oe1_ps, t - 1)
                evac(actT[:, t % 2].rearrange("p l k t -> p (l k t)"), ps[:, 4 + t % 2, 0:I].bitcast(FP16), aT_ps, t + 1, aT_ok)

            def mk_evac(t):
                if t >= 4:
                    act.wait_ge(made1_in[t % 4], 16 * (t // 4))
                act.wait_ge(oe1_ps, t + 1)
                a.activation(mk1[:, t % 4, :], ps[:, 6 + t % 2, 0:D], ACT.Copy, scale=1.0 / (WS * WS)).then_inc(mk1_ok, 1)

            for t in range(3):
                xt_evac(t)
            tile_tanh(0)
            for t in range(NTILE1 + 2):
                if t + 3 < NTILE1:
                    xt_evac(t + 3)
                if t < NTILE1:
                    act_high(t)
                if t + 1 < NTILE1:
                    tile_tanh(t + 1)
                if 1 <= t <= NTILE1:
                    at_evac(t - 1)
                if t >= 2:
                    mk_evac(t - 2)

        @block.vector
        def _(dve):
            v = nc.vector
            step = [0]

            def chain(ins):
                step[0] += 1
                ins.then_inc(v_chain, 1)

            def settle():
                dve.wait_ge(v_chain, step[0])

            def link(ins):
                chain(ins)
                settle()

            def stats(n, stage, i0, ni):
                for i in range(i0, i0 + ni):
                    chain(v.bn_stats(st[:, stage, i, :], x_sb[:, i, :]))
                settle()
                for i in range(i0, i0 + ni):
                    last = v.bn_aggr(mv[:, stage, i, :], st[:, stage, i, :])
                last.then_inc(var_ok, 1)

            def normal(n, stage, i0, ni):
                dve.wait_ge(var_ok, n + 1)
                dve.wait_ge(rstd_ok, n + 1)
                for i in range(i0, i0 + ni):
                    v.tensor_scalar(xn[:, i, 0:D], x_sb[:, i, :], mv[:, stage, i, 0:1], rs[:, stage, i:i + 1],
                                    ALU.subtract, ALU.mult).then_inc(xn_ok, 1)

            def first_stats(p):
                dve.wait_ge(x_in[p], 16)
                stats(p, 0, 4 * p, 4)

            first_stats(0)
            dve.wait_ge(wu_in, 32)
            dve.wait_ge(scan_pads_ok, 1)
            for h in range(KC):
                v.tensor_copy(w0[:, h, :, 1:SEQ], w_sb[:, h:h + 1].unsqueeze(2).to_broadcast([P, 2, S])).then_inc(w0_ok, 1)
            normal(0, 0, 0, 4)
            first_stats(1)
            dve.wait_ge(w0_ok, KC)

            def head(n):
                p, h = divmod(n, KC)
                b = n % 2
                dve.wait_ge(kT_ok, n + 1)
                v.tensor_tensor_scan(flat(O, b), flat(w0, h), flat(kT, n), NEG, ALU.add, ALU.max).then_inc(o_ok, 1)
                dve.wait_ge(o_ok, n + 1)
                v.scalar_tensor_tensor(cur(A2, b), prev(O, b), w_sb[:, h:h + 1], cur(O, b), ALU.add, ALU.subtract).then_inc(a2_ok, 1)
                v.scalar_tensor_tensor(cur(NO, b), cur(kT, n), u_sb[:, h:h + 1], prev(O, b), ALU.add, ALU.max).then_inc(no_ok, 1)
                dve.wait_ge(no_ok, n + 1)
                if n >= 2:
                    dve.wait_ge(t2_ok, n - 1)
                    dve.wait_ge(den_ok, n - 1)
                v.scalar_tensor_tensor(cur(EE, b), cur(kT, n), u_sb[:, h:h + 1], cur(NO, b), ALU.add, ALU.subtract).then_inc(ee_ok, 1)

            def scans(n):
                b = n % 2
                dve.wait_ge(a2_exp, n + 1)
                dve.wait_ge(e2_exp, n + 1)
                dve.wait_ge(ev_ok, n + 1)
                v.tensor_tensor_scan(flat(QQ, b), flat(A2, b), flat(E2, b), 0.0, ALU.mult, ALU.add).then_inc(q_ok, 1)
                chain(v.tensor_tensor_scan(flat(PP, b), flat(A2, b), flat(EV, b), 0.0, ALU.mult, ALU.add))

            def old_part(n):
                b = n % 2
                settle()
                dve.wait_ge(aa_exp, n + 1)
                if n >= 2:
                    dve.wait_ge(yT_ps, n // 2)
                v.tensor_tensor(cur(T1, b), cur(AA, b), prev(PP, b), ALU.mult).then_inc(t1_ok, 1)

            def ratio(n):
                b = n % 2
                dve.wait_ge(den_ok, n + 1)
                link(v.reciprocal(cur(O, b), cur(O, b)))
                dve.wait_ge(num_ok, n + 1)
                v.tensor_tensor(cur(T1, b), cur(T1, b), cur(O, b), ALU.mult).then_inc(y_ok, 1)
                dve.wait_ge(y_ok, n + 1)

            def residual(p, gate, bank, ready, n, done):
                dve.wait_ge(ready, n)
                dve.wait_ge(tg_ok, 1)
                for k in range(2):
                    xs = x_sb[:, 4 * p + 2 * k:4 * p + 2 * k + 2, :].rearrange("p i d -> p (i d)")
                    last = v.scalar_tensor_tensor(xs, ps[:, bank + k, :], tg[:, gate:gate + 1], xs, ALU.mult, ALU.add)
                    if k == 0:
                        chain(last)
                last.then_inc(done, 1)

            def choose(tiles):
                for i in tiles:
                    chain(v.max(mx[:, i, :], lg[:, i, :]))
                settle()
                for i in tiles:
                    chain(v.max_index(ix[:, i, :], mx[:, i, :], lg[:, i, :]))

            def route0(p):
                i0 = 4 * p
                sl = slice(i0, i0 + 4)
                dve.wait_ge(lg0_ps, p + 1)
                v.tensor_copy(lg[:, sl, :], ps[:, 6, 0:4 * E].rearrange("p (i e) -> p i e", e=E)).then_inc(lg0_ok, 1)
                dve.wait_ge(lg0_ok, p + 1)
                choose(range(i0, i0 + 4))
                settle()
                v.tensor_tensor(pe_[:, sl, :], lg[:, sl, :], mx[:, sl, 0:1].to_broadcast([P, 4, E]), ALU.subtract).then_inc(ex0_in, 1)
                link(v.tensor_copy(ixf[:, sl, 0:1], ix[:, sl, 0:1]))
                link(v.tensor_tensor(oh[:, 0, sl, :], iota8[:, :].unsqueeze(1).to_broadcast([P, 4, E]),
                                     ixf[:, sl, 0:1].to_broadcast([P, 4, E]), ALU.is_equal))
                v.tensor_copy(ohb[:, sl, :], oh[:, 0, sl, :]).then_inc(oh0_ok, 1)

            def slots0(p):
                i0 = 4 * p
                sl = slice(i0, i0 + 4)
                dve.wait_ge(cum0_ps, p + 1)
                v.tensor_tensor(cumoh[:, 0, sl, :], ps[:, 7, 0:4 * E].rearrange("p (i e) -> p i e", e=E), oh[:, 0, sl, :],
                                ALU.mult).then_inc(cum0_ok, 1)
                dve.wait_ge(cum0_ok, p + 1)
                link(v.reduce_sum(pos[:, 0, sl], cumoh[:, 0, sl, :], AXX))
                link(v.tensor_scalar(keep[:, sl], pos[:, 0, sl], float(CAP), None, ALU.is_le))
                link(v.tensor_scalar(slotf[:, 0, sl], ixf[:, sl, 0], float(CAP), FAR - 1.0, ALU.mult, ALU.add))
                link(v.tensor_tensor(slotf[:, 0, sl], slotf[:, 0, sl], pos[:, 0, sl], ALU.add))
                link(v.scalar_tensor_tensor(slotf[:, 0, sl], keep[:, sl], -FAR, slotf[:, 0, sl], ALU.mult, ALU.add))
                link(v.tensor_copy(sidx[:, 0, sl], slotf[:, 0, sl]))
                dve.wait_ge(ex0_ok, p + 1)
                link(v.reduce_sum(ssum[:, sl], pe_[:, sl, :], AXX))
                link(v.reciprocal(ssum[:, sl], ssum[:, sl]))
                v.scalar_tensor_tensor(coef[:, 0, sl], ssum[:, sl], tg[:, 2:3], keep[:, sl], ALU.mult, ALU.mult).then_inc(idx0_ok, 1)

            def swiglu_shared(p, m):
                n = HC * p + m
                dve.wait_ge(sh_th, n + 1)
                if m == 0 and p > 0:
                    dve.wait_ge(sho_ps, p)
                t = thb[:, n % 2, :]
                link(v.scalar_tensor_tensor(t, t, 1.0, ps[:, 2 * (m % 2), :], ALU.add, ALU.mult))
                v.scalar_tensor_tensor(hT[:, m, :], t, 0.5, ps[:, 2 * (m % 2) + 1, :], ALU.mult, ALU.mult).then_inc(sh_ok, 1)

            head(0)
            head(1)
            normal(1, 0, 4, 4)
            scans(0)
            old_part(0)
            scans(1)
            old_part(1)
            ratio(0)
            head(2)
            ratio(1)
            head(3)
            residual(0, 0, 4, yT_ps, 1, x1_ok)
            dve.wait_ge(x1_ok, 1)
            stats(2, 1, 0, 4)
            scans(2)
            normal(2, 1, 0, 4)
            old_part(2)
            scans(3)
            old_part(3)
            ratio(2)
            ratio(3)
            swiglu_shared(0, 0)
            route0(0)
            swiglu_shared(0, 1)
            slots0(0)
            swiglu_shared(0, 2)
            residual(1, 0, 6, yT_ps, 2, x1_ok)
            dve.wait_ge(x1_ok, 2)
            stats(3, 1, 4, 4)
            normal(3, 1, 4, 4)
            route0(1)
            residual(0, 2, 4, sho_ps, 1, xs_ok)
            slots0(1)
            for m in range(HC):
                swiglu_shared(1, m)
            residual(1, 2, 4, sho_ps, 2, xs_ok)
            dve.wait_ge(xs_ok, 2)
            v.memset(mT[:, :, :], 0.0)
            v.memset(bias3[:, :], 0.0).then_inc(b3z_ok, 1)

            def swiglu_expert(e):
                dve.wait_ge(h0_th, e + 1)
                t = the[:, e % 2, :]
                b = 2 + 2 * (e % 2)
                link(v.scalar_tensor_tensor(t, t, 1.0, ps[:, b, 0:HP], ALU.add, ALU.mult))
                v.scalar_tensor_tensor(he[:, e % 2, :], t, 0.5, ps[:, b + 1, 0:HP], ALU.mult, ALU.mult).then_inc(h0_ok, 1)

            def k_evac(t):
                b, j = divmod(t, TPB)
                dve.wait_ge(k_ps, t + 1)
                v.tensor_copy(ktb[:, b, :, j * P:(j + 1) * P], ps16(7)).then_inc(ktb_ok, 1)

            def split_low(e):
                dve.wait_ge(w_hi, e + 1)
                v.tensor_tensor(split_at(e, 1, 0, WE), stage[e], split_at(e, 0, 0, WE), ALU.subtract).then_inc(w_lo_dve, 1)

            swiglu_expert(0)
            for e in range(E):
                if e + 1 < E:
                    swiglu_expert(e + 1)
                k_evac(e)
                if e == E - 1:
                    split_low(0)
                    split_low(1)

            dve.wait_ge(v_lo, NT)
            dve.wait_ge(oe0_ps, E)

            def query_zeros(n):
                v.memset(qtb[n][P // 2:P, 0], 0.0)
                v.memset(qtb[n][0:P // 2, 1], 0.0).then_inc(qz_ok[n], 1)

            query_zeros(0)
            query_zeros(1)

            def combine0(b):
                dve.wait_ge(got0_in[b], 16)
                for i in range(2 * b, 2 * b + 2):
                    last = v.scalar_tensor_tensor(x_sb[:, i, :], got0[:, i, :], coef[:, 0, i:i + 1], x_sb[:, i, :], ALU.mult, ALU.add)
                link(last)
                stats(4 + b, 2, 2 * b, 2)

            def nat_max(b, s):
                n = 6 * b + s
                h0, nh, qt = NAT[s]
                dve.wait_ge(nat_ps, n + 1)
                bank = 2 * (n % 3) if n < 6 else 0
                v.reduce_max(mmax[:, b % 2, qt, h0:h0 + nh].rearrange("p (h a) -> p a h", a=2),
                             sub_cols(ps[:, bank:bank + 2, :], nh), AXX).then_inc(nat_ok, 1)
                if s == 5:
                    dve.wait_ge(nat_ok, 6 * b + 6)
                    link(v.tensor_scalar(mneg[:, b % 2, :, 0], mmax[:, b % 2], -1.0, None, ALU.mult))
                    v.scalar_tensor_tensor(mneg[:, b % 2, :, 1], mmax[:, b % 2], -1.0, mneg[:, b % 2, :, 0], ALU.mult, ALU.subtract).then_inc(mneg_ok, 1)

            def q_evac_odd(b, tiles=(0, 1)):
                if b >= 3:
                    dve.wait_ge(st_ps, 3 * 2 * (b - 2))
                for j in tiles:
                    dve.wait_ge(misc_ps, USE[("q", 2 * b + j)] + 1)
                    v.tensor_copy(qtb[b % 3][P // 2:P, 1, :, j * P:(j + 1) * P], ps16(7)[P // 2:P]).then_inc(q_odd, 1)

            def weights_low(u):
                n = 3 * u + 2
                dve.wait_ge(p32_ok, n + 1)
                dve.wait_ge(st_exp, n + 1)
                v.tensor_tensor(pT[:, 1, u % 2, 2, :], p32[:, n % 2, :], pT[:, 0, u % 2, 2, :], ALU.subtract).then_inc(lo_dve, 1)

            def attend(u):
                b, hg = divmod(u, 2)
                dve.wait_ge(pv_ps, u + 1)
                o = ps[:, 6, 0:2 * 8 * (HD + 1)].rearrange("p (q h c) -> p q h c", q=2, h=8)
                r = den[:, u % 2]
                link(v.reciprocal(r, o[:, :, :, HD]))
                v.scalar_tensor_tensor(att[:, u % 2], o[:, :, :, 0:HD], tg[:, 1:2], r.unsqueeze(3).to_broadcast([P, 2, 8, HD]),
                                       ALU.mult, ALU.mult).then_inc(pv_ok, 1)
                dve.wait_ge(pv_ok, u + 1)
                xs = x_sb[:, 2 * b:2 * b + 2, hg * P:(hg + 1) * P]
                link(v.tensor_tensor(xs, xs, att[:, u % 2].rearrange("p q h c -> p q (h c)"), ALU.add))

            def route1(b):
                sl = slice(2 * b, 2 * b + 2)
                n = USE[("l", b)]
                dve.wait_ge(misc_ps, n + 1)
                v.tensor_tensor(lg[:, sl, :], ps[:, 7, 0:2 * E].rearrange("p (i e) -> p i e", e=E),
                                rb_sb[:, :].unsqueeze(1).to_broadcast([P, 2, E]), ALU.add).then_inc(misc_free, 1)
                dve.wait_ge(misc_free, n + 1)
                choose(range(2 * b, 2 * b + 2))
                settle()
                v.tensor_tensor(ssum[:, sl], mx[:, sl, 1], mx[:, sl, 0], ALU.subtract).then_inc(ex1_in, 1)
                link(v.tensor_copy(ixf[:, sl, :], ix[:, sl, 0:2]))
                for k in range(2):
                    link(v.tensor_tensor(oh[:, k, sl, :], iota8[:, :].unsqueeze(1).to_broadcast([P, 2, E]),
                                         ixf[:, sl, k:k + 1].to_broadcast([P, 2, E]), ALU.is_equal))
                v.tensor_tensor(ohb[:, sl, :], oh[:, 0, sl, :], oh[:, 1, sl, :], ALU.add).then_inc(oh1_ok, 1)

            def slots1(b):
                sl = slice(2 * b, 2 * b + 2)
                n = USE[("c", b)]
                cum = ps[:, 7, 0:2 * E].rearrange("p (i e) -> p i e", e=E)
                dve.wait_ge(misc_ps, n + 1)
                link(v.tensor_tensor(cumoh[:, 0, sl, :], cum, oh[:, 0, sl, :], ALU.mult))
                v.tensor_tensor(cumoh[:, 1, sl, :], cum, oh[:, 1, sl, :], ALU.mult).then_inc(misc_free, 1)
                dve.wait_ge(misc_free, n + 1)
                link(v.reduce_sum(pos[:, :, sl], cumoh[:, :, sl, :], AXX))
                for k in range(2):
                    link(v.scalar_tensor_tensor(slotf[:, k, sl], ixf[:, sl, k], float(T), pos[:, k, sl], ALU.mult, ALU.add))
                v.tensor_scalar(sidx[:, :, sl], slotf[:, :, sl], -1.0, None, ALU.add).then_inc(idx1_ok, 1)
                dve.wait_ge(ex1_ok, b + 1)
                link(v.tensor_scalar(keep[:, sl], ssum[:, sl], 1.0, None, ALU.add))
                link(v.reciprocal(keep[:, sl], keep[:, sl]))
                link(v.tensor_scalar(coef[:, 0, sl], keep[:, sl], tg[:, 3:4], None, ALU.mult))
                v.tensor_tensor(coef[:, 1, sl], coef[:, 0, sl], ssum[:, sl], ALU.mult).then_inc(coef_ok, 1)

            combine0(0)
            combine0(1)
            dve.wait_ge(ids_ok, 1)
            normal(4, 2, 0, 2)
            combine0(2)
            normal(5, 2, 2, 2)
            q_evac_odd(0)
            combine0(3)
            for s in range(3):
                nat_max(0, s)
            q_evac_odd(1)
            normal(6, 2, 4, 2)
            for s in range(3, 6):
                nat_max(0, s)
            normal(7, 2, 6, 2)
            query_zeros(2)
            for u in range(2 * B):
                ahead = u % 2 == 1 and u // 2 + 2 < B
                for s in range(3):
                    if u // 2 + 1 < B:
                        nat_max(u // 2 + 1, 3 * (u % 2) + s)
                    if s == 0 and u % 2 == 0 and u >= 4:
                        route1((u - 4) // 2)
                    if s == 0 and u % 2 == 1 and u >= 5:
                        slots1((u - 5) // 2)
                    if ahead and s < 2:
                        q_evac_odd(u // 2 + 2, [s])
                    if s == 0 and u % 2 == 1 and u >= 3:
                        stats(8 + (u - 3) // 2, 3, u - 3, 2)
                    if s == 1 and u % 2 == 1 and u >= 3:
                        normal(8 + (u - 3) // 2, 3, u - 3, 2)
                if u >= 1:
                    attend(u - 1)
                weights_low(u)
            route1(B - 2)
            attend(2 * B - 1)
            stats(7 + B, 3, 2 * B - 2, 2)
            slots1(B - 2)
            normal(7 + B, 3, 2 * B - 2, 2)
            route1(B - 1)
            slots1(B - 1)

            dve.wait_ge(misc_ps, USE[("n", 0)] + 1)
            v.tensor_copy(cnt[:, 0, :], ps[:, 7, 0:E]).then_inc(misc_free, 1)
            dve.wait_ge(misc_free, USE[("n", 0)] + 1)
            link(v.tensor_scalar(cnt[:, 1, :], cnt[:, 0, :], 1.0 / P, (P - 1.0) / P - 0.5 + 1.0 / 512, ALU.mult, ALU.add))
            link(v.tensor_copy(nti[:, :], cnt[:, 1, :]))
            link(v.tensor_copy(cnt[:, 1, :], nti[:, :]))
            link(v.memset(cnt[:, 0, :], 1.0))
            link(v.tensor_tensor_scan(cnt[:, 2, :], cnt[:, 0, :], cnt[:, 1, :], 0.0, ALU.mult, ALU.add))
            ends = cnt[:, 2, :].unsqueeze(1).to_broadcast([P, NTILE1, E])
            link(v.tensor_tensor(tle[:, 0], ends, iota_t[:, :].unsqueeze(2).to_broadcast([P, NTILE1, E]), ALU.is_le))
            link(v.tensor_tensor(tle[:, 1], tle[:, 0], ends, ALU.mult))
            link(v.reduce_sum(tabf[:, 0, :], tle[:, 0], AXX))
            link(v.reduce_max(tabf[:, 1, :], tle[:, 1], AXX))
            link(v.tensor_tensor(tabf[:, 1, :], iota_t[:, :], tabf[:, 1, :], ALU.subtract))
            link(v.tensor_scalar(tabf[:, 2, :], tabf[:, 0, :], float(T), None, ALU.mult))
            link(v.scalar_tensor_tensor(tabf[:, 2, :], tabf[:, 1, :], float(P), tabf[:, 2, :], ALU.mult, ALU.add))
            link(v.tensor_scalar(tabi[:, 0, :], tabf[:, 0, :], float(E - 1), None, ALU.min))
            v.tensor_scalar(tabi[:, 1, :], tabf[:, 2, :], float(E * T - P), None, ALU.min).then_inc(tab_ok, 1)
            split_low(6)
            split_low(7)

            def row_low(t):
                dve.wait_ge(xtT_ok, t + 1)
                v.tensor_tensor(xtT[:, t % 3, 1].rearrange("p k t -> p (k t)"), ps[:, t % 2, 0:D],
                                xtT[:, t % 3, 0].rearrange("p k t -> p (k t)"), ALU.subtract).then_inc(xlo_ok, 1)

            def clip(t):
                b = t % 2
                g = ps[:, 2 + b, :].rearrange("p (i c) -> p c i", c=2)
                dve.wait_ge(gu_ps, t + 1)
                v.tensor_scalar(gh[:, b, :], g[:, 0, :], 7.0 * WS, 0.5 / WS, ALU.min, ALU.mult).then_inc(gh_ok, 1)
                link(v.tensor_scalar(up[:, b, :], g[:, 1, :], -7.0 * WS, 7.0 * WS, ALU.max, ALU.min))

            def act_tile(t):
                b = t % 2
                dve.wait_ge(gh_ok, t + 1)
                dve.wait_ge(th1_ok, t + 1)
                link(v.scalar_tensor_tensor(glu[:, b, :], th1[:, b, :], 1.0, gh[:, b, :], ALU.add, ALU.mult))
                if t >= 2:
                    dve.wait_ge(act_lo, t - 1)
                v.scalar_tensor_tensor(actv[:, b, :], up[:, b, :], WS, glu[:, b, :], ALU.add, ALU.mult).then_inc(act_ok, 1)

            row_low(0)
            row_low(1)
            for t in range(NTILE1):
                clip(t)
                if t + 2 < NTILE1:
                    row_low(t + 2)
                act_tile(t)

            dve.wait_ge(coef_ok, B)
            for b in range(B):
                dve.wait_ge(got1_in[b], 32)
                tiles = range(2 * b, 2 * b + 2)
                for i in tiles:
                    chain(v.scalar_tensor_tensor(x_sb[:, i, :], got1[:, 0, i, :], coef[:, 0, i:i + 1], x_sb[:, i, :], ALU.mult, ALU.add))
                settle()
                for i in tiles:
                    v.scalar_tensor_tensor(x_sb[:, i, :], got1[:, 1, i, :], coef[:, 1, i:i + 1], x_sb[:, i, :], ALU.mult, ALU.add).then_inc(x4_ok, 1)

        @block.tensor
        def _(pe):
            t_ = nc.tensor

            def mm(o, l, r, start, stop):
                return t_.matmul(o, lhsT=l, rhs=r, start=start, stop=stop)

            pe.wait_ge(consts_ok, 1)
            for n in range(NG):
                p, h = divmod(n, KC)
                if n >= 2:
                    pe.wait_ge(kT_ok, n - 1)
                pe.wait_ge(xn_ok, 4 * p + 4)
                for j in range(4):
                    last = t_.transpose(ps[:, n % 2, j * P:(j + 1) * P], xn[:, 4 * p + j, h * P:(h + 1) * P], ident[:, :])
                last.then_inc(kT_ps, 1)
                if n >= 2:
                    pe.wait_ge(vT_ok, n - 1)
                pe.wait_ge(ctx_in_s[p], 16)
                for j in range(4):
                    last = t_.transpose(ps[:, 2 + n % 2, j * P:(j + 1) * P], ctx_sb[:, 4 * p + j, h * P:(h + 1) * P], ident[:, :])
                last.then_inc(vT_ps, 1)

            def y_back(p):
                pe.wait_ge(y_ok, KC * p + KC)
                if p > 0:
                    pe.wait_ge(lg0_ok, p)
                    pe.wait_ge(cum0_ok, p)
                for j in range(4):
                    for h in range(KC):
                        last = t_.transpose(ps[:, 4 + 2 * p + j // 2, (j % 2) * D + h * P:(j % 2) * D + (h + 1) * P],
                                            T1[:, h, j // 2, 1 + (j % 2) * P:1 + (j % 2 + 1) * P], ident[:, :])
                last.then_inc(yT_ps, 1)

            def x1_turn(p):
                pe.wait_ge(xn_ok, NT + 4 * p + 4)
                pe.wait_ge(kT_ok, NG)
                if p > 0:
                    pe.wait_ge(sh_ok, HC * p)
                for h in range(KC):
                    for j in range(4):
                        last = t_.transpose(ps[:, h, j * P:(j + 1) * P], xn[:, 4 * p + j, h * P:(h + 1) * P], ident[:, :])
                    last.then_inc(x1T_ps, 1)

            def logits0(p):
                pe.wait_ge(x1T_ok, KC * (p + 1))
                pe.wait_ge(sw_in, 16 * 5)
                if p > 0:
                    pe.wait_ge(x1_ok, p + 1)
                for j in range(4):
                    for k in range(KC):
                        last = mm(ps[:, 6, j * E:(j + 1) * E], xT[:, k, (4 * p + j) * P:(4 * p + j + 1) * P], wg_sb[:, k, :],
                                  k == 0, k == KC - 1)
                last.then_inc(lg0_ps, 1)

            def shared_up(p, m):
                n = HC * p + m
                pe.wait_ge(x1T_ok, KC * (p + 1))
                pe.wait_ge(sw_in, 16 * 5)
                pe.wait_ge(pads_ok, 1)
                pe.wait_ge(vT_ok, NG)
                if n >= 2:
                    pe.wait_ge(sh_ok, n - 1)
                for c, w in enumerate((sw1_sb, sw3_sb)):
                    for k in range(KC):
                        last = mm(ps[:, 2 * (m % 2) + c, :], w[:, k, m * P:(m + 1) * P], xT[:, k, 512 * p:512 * p + 512],
                                  k == 0, k == KC - 1)
                last.then_inc(sh_ps, 1)

            def count(i, o):
                for j in range(i):
                    mm(o, onesb[:, :], ohb[:, j, :], j == 0, False)
                return mm(o, upper[:, :], ohb[:, i, :], i == 0, True)

            def cum0(p):
                pe.wait_ge(oh0_ok, p + 1)
                if p > 0:
                    pe.wait_ge(cum0_ok, p)
                for j in range(4):
                    last = count(4 * p + j, ps[:, 7, j * E:(j + 1) * E])
                last.then_inc(cum0_ps, 1)

            def shared_down(p):
                pe.wait_ge(sh_ok, HC * (p + 1))
                if p > 0:
                    pe.wait_ge(xs_ok, p)
                else:
                    pe.wait_ge(x1_ok, 1)
                for j in range(4):
                    for m in range(HC):
                        last = mm(ps[:, 4 + j // 2, (j % 2) * D:(j % 2 + 1) * D], hT[:, m, j * P:(j + 1) * P], sw2_sb[:, m, :],
                                  m == 0, m == HC - 1)
                last.then_inc(sho_ps, 1)

            y_back(0)
            x1_turn(0)
            shared_up(0, 0)
            logits0(0)
            shared_up(0, 1)
            cum0(0)
            shared_up(0, 2)
            y_back(1)
            shared_down(0)
            x1_turn(1)
            logits0(1)
            shared_up(1, 0)
            cum0(1)
            shared_up(1, 1)
            shared_up(1, 2)
            shared_down(1)

            def misc_take(key):
                n = USE[key]
                if n >= 1:
                    pe.wait_ge(misc_free, n)
                    if USES[n - 1][0] == "q":
                        pe.wait_ge(q_odd, USES[n - 1][1] + 1)
                else:
                    pe.wait_ge(ktb_ok, NT)

            def k_turn(t):
                pe.wait_ge(k_lo, t + 1)
                if t >= 1:
                    pe.wait_ge(ktb_ok, t)
                else:
                    pe.wait_ge(cum0_ok, NP2)
                for h in range(NPAIR):
                    last = t_.transpose(ps16(7)[:, h, :], spl[:, t % 2, 2 * h:2 * h + 2, :, :].rearrange("p h s c -> p (h s c)"), ident16[:, :])
                last.then_inc(k_ps, 1)

            def xd_turn(e):
                if e % 2 == 0:
                    pe.wait_ge(disp0_out[e // 2], 16)
                pe.wait_ge(sh_ok, HC * NP2)
                if e >= 2:
                    pe.wait_ge(xdT_ok, e - 1)
                for k in range(KC):
                    last = t_.transpose(ps[:, e % 2, k * P:(k + 1) * P], xd[:, e, k * P:(k + 1) * P], ident[:, :])
                last.then_inc(xdT_ps, 1)

            def expert_up(e):
                if e % (E // 2) == 0:
                    pe.wait_ge(w13_in[e // (E // 2)], 2 * 16 * (E // 2))
                    pe.wait_ge(xs_ok, NP2)
                pe.wait_ge(xdT_ok, e + 1)
                if e >= 2:
                    pe.wait_ge(h0_ok, e - 1)
                for c, w in enumerate((w1_sb, w3_sb)):
                    for m in range(HC):
                        for k in range(KC):
                            last = mm(ps[:, 2 + 2 * (e % 2) + c, m * P:(m + 1) * P], w[:, e, k, m * P:(m + 1) * P], xdT[:, e % 2, k, :],
                                      k == 0, k == KC - 1)
                last.then_inc(h0_ps, 1)

            def expert_down(e):
                pe.wait_ge(h0_ok, e + 1)
                if e == 0:
                    pe.wait_ge(w2_in, 16 * (E + 1))
                    pe.wait_ge(lg0_ok, NP2)
                if e >= 1:
                    pe.wait_ge(oe0_ok, e)
                for m in range(HC):
                    last = mm(ps[:, 6, 0:D], he[:, e % 2, m * P:(m + 1) * P], w2_sb[:, e, m, :], m == 0, m == HC - 1)
                last.then_inc(oe0_ps, 1)

            xd_turn(0)
            xd_turn(1)
            expert_up(0)
            for e in range(E):
                if e + 2 < E:
                    xd_turn(e + 2)
                if e + 1 < E:
                    expert_up(e + 1)
                k_turn(e)
                expert_down(e)

            def q_turn(i):
                pe.wait_ge(q_lo, i + 1)
                misc_take(("q", i))
                if i == 0:
                    pe.wait_ge(oe0_ok, E)
                for h in range(NPAIR):
                    last = t_.transpose(ps16(7)[:, h, :], spl[:, i % 2, 2 * h:2 * h + 2, :, :].rearrange("p h s c -> p (h s c)"), ident16[:, :])
                last.then_inc(misc_ps, 1)

            def nat(b, s):
                n = 6 * b + s
                h0, nh, qt = NAT[s]
                if s == 0:
                    pe.wait_ge(misc_free, USE[("q", 2 * b + 1)] + 1)
                    pe.wait_ge(q_odd, 2 * b + 2)
                    pe.wait_ge(qz_ok[b % 3], 1)
                if n >= (3 if n < 6 else 1):
                    pe.wait_ge(nat_ok, n - 2 if n < 6 else n)
                w = (qt + 1) * P
                bank = 2 * (n % 3) if n < 6 else 0
                for h in range(h0, h0 + nh):
                    o = ps[:, bank + h % 2, (h - h0) // 2 * w:(h - h0) // 2 * w + w]
                    mm(o, qtb[b % 3][:, h % 2, h // 2, qt * P:(qt + 1) * P], ktb[:, b, h // 2, 0:w], True, False)
                    last = mm(o[:, w - P:w], identb[:, :], causal[:, :], False, True)
                last.then_inc(nat_ps, 1)

            def scores_t(u, s):
                n = 3 * u + s
                b, hg = divmod(u, 2)
                h0, nh, kt = [(8 * hg, 4, 0), (8 * hg + 4, 4, 0), (8 * hg, 8, 1)][s]
                if s == 0 and hg == 0:
                    pe.wait_ge(misc_free, USE[("m", b)] + 1)
                if n >= 2:
                    pe.wait_ge(st_exp, n - 1)
                w = S - kt * P
                for h in range(h0, h0 + nh):
                    o = ps[:, 2 + 2 * (n % 2) + h % 2, (h - h0) // 2 * w:(h - h0) // 2 * w + w]
                    mm(o, sel[:, h, :], mT[:, b % 2, kt * P:S], True, False)
                    mm(o, ktb[:, b, h // 2, kt * P:(kt + 1) * P], qtb[b % 3][:, h % 2, h // 2, kt * P:S], False, False)
                    last = mm(o[:, 0:P], identb[:, :], causalT[:, :], False, True)
                last.then_inc(st_ps, 1)

            def weigh(u):
                b, hg = divmod(u, 2)
                pe.wait_ge(st_exp, 3 * (u + 1))
                pe.wait_ge(lo_pool, 2 * (u + 1))
                pe.wait_ge(lo_dve, u + 1)
                if u >= 1:
                    pe.wait_ge(pv_ok, u)
                parts = ((0, 0), (0, 1), (1, 0))
                c = HD + 1
                for j in range(8):
                    h = 8 * hg + j
                    early = pT[:, :, u % 2, j // 4, (j % 4) * S:(j % 4 + 1) * S]
                    late = pT[:, :, u % 2, 2, j * P:(j + 1) * P]
                    o = ps[:, 6, j * c:(j + 1) * c]
                    for n, (l, m) in enumerate(parts):
                        mm(o, early[:, l, 0:P], v17[:, m, 2 * b, h, :], n == 0, n == 2)
                    o = ps[:, 6, (8 + j) * c:(9 + j) * c]
                    for n, (l, m) in enumerate(parts):
                        mm(o, early[:, l, P:S], v17[:, m, 2 * b, h, :], n == 0, False)
                    for n, (l, m) in enumerate(parts):
                        last = mm(o, late[:, l], v17[:, m, 2 * b + 1, h, :], False, n == 2)
                last.then_inc(pv_ps, 1)

            def route_x(b):
                pe.wait_ge(xn_ok, 3 * NT + 2 * b + 2)
                misc_take(("x", b))
                for k in range(KC):
                    for j in range(TPB):
                        last = t_.transpose(ps[:, 7, (k * TPB + j) * P:(k * TPB + j + 1) * P], xn[:, 2 * b + j, k * P:(k + 1) * P], ident[:, :])
                last.then_inc(misc_ps, 1)

            def route_l(b):
                misc_take(("l", b))
                for j in range(TPB):
                    for k in range(KC):
                        last = mm(ps[:, 7, j * E:(j + 1) * E], xrT[:, k, j * P:(j + 1) * P], rw_sb[:, k, :], k == 0, k == KC - 1)
                last.then_inc(misc_ps, 1)

            def route_c(b):
                pe.wait_ge(oh1_ok, b + 1)
                misc_take(("c", b))
                for j in range(TPB):
                    last = count(2 * b + j, ps[:, 7, j * E:(j + 1) * E])
                last.then_inc(misc_ps, 1)

            pe.wait_ge(sel_ok, 1)
            pe.wait_ge(v_lo, NT)
            pe.wait_ge(bias_p_ok, 1)

            def m_turn(b):
                pe.wait_ge(mneg_ok, b + 1)
                misc_take(("m", b))
                for q in range(2):
                    last = t_.transpose(ps[0:2 * HEADS, 7, 0:S // 2].bitcast(BF16)[:, q * P:(q + 1) * P],
                                        mneg[:, b % 2, q].rearrange("p l h -> p (l h)"), identb[:, :])
                last.then_inc(misc_ps, 1)

            q_turn(0)
            q_turn(1)
            for s in range(3):
                nat(0, s)
            q_turn(2)
            q_turn(3)
            for s in range(3, 6):
                nat(0, s)
            m_turn(0)
            for u in range(2 * B):
                b = u // 2
                for s in range(3):
                    scores_t(u, s)
                    if b + 1 < B:
                        nat(b + 1, 3 * (u % 2) + s)
                    if s < 2 and u % 2 == 1 and b + 2 < B:
                        q_turn(u + 3 + s)
                    if s == 0 and u % 2 == 0 and u >= 4:
                        route_l((u - 4) // 2)
                if u >= 1:
                    weigh(u - 1)
                if u % 2 == 1 and b + 1 < B:
                    m_turn(b + 1)
                if u % 2 == 1 and u >= 3:
                    route_x((u - 3) // 2)
                if u % 2 == 0 and u >= 4:
                    route_c((u - 4) // 2)
            route_l(B - 2)
            weigh(2 * B - 1)
            route_c(B - 2)
            route_x(B - 1)
            route_l(B - 1)
            route_c(B - 1)
            misc_take(("n", 0))
            for j in range(NT):
                last = mm(ps[:, 7, 0:E], onesb[:, :], ohb[:, j, :], j == 0, j == NT - 1)
            last.then_inc(misc_ps, 1)

            pe.wait_ge(tab_ok, 1)
            pe.wait_ge(bias_rows, 96)
            pe.wait_ge(w_lo_pool, 4)
            ex = {}
            parts = ((0, 0), (0, 1), (1, 0))

            def xt_turn(t):
                pe.wait_ge(xt_in[t % 8], 16 * (t // 8 + 1))
                if t >= 2:
                    pe.wait_ge(xlo_ok, t - 1)
                for k in range(KC):
                    last = t_.transpose(ps[:, t % 2, k * P:(k + 1) * P], xt[:, t % NXT, k * P:(k + 1) * P], ident[:, :])
                last.then_inc(xtT_ps, 1)

            def gate_up_tile(t):
                ex[t] = pe.value_load(tabi[0:1, 0, t:t + 1], min_val=0, max_val=E - 1)
                pe.wait_ge(xlo_ok, t + 1)
                if t == 0:
                    pe.wait_ge(w_lo_dve, 4)
                if t >= 2:
                    pe.wait_ge(act_ok, t - 1)
                o = ps[:, 2 + t % 2, :]
                mm(o, scales[:, 0, :], bias3[:, bass.ds(ex[t] * GU, GU)], True, False)
                for k in range(KC):
                    for lx, lw in parts:
                        w = w16[:, bass.ds(ex[t] * (2 * WE) + (lw * WE + k * GU), GU)]
                        last = mm(o, xtT[:, t % 3, lx, k, :], w, False, k == KC - 1 and (lx, lw) == parts[-1])
                last.then_inc(gu_ps, 1)

            def act_turn(t):
                pe.wait_ge(act_hi, t + 1)
                pe.wait_ge(act_lo, t + 1)
                if t >= 2:
                    pe.wait_ge(aT_ok, t - 1)
                o = ps[:, 4 + t % 2, 0:I].bitcast(FP16)
                for l in range(2):
                    for k in range(KC):
                        n = l * KC + k
                        last = t_.transpose(o[:, n * P:(n + 1) * P], asp[:, t % 2, l, k * P:(k + 1) * P], ident16[:, :])
                last.then_inc(aT_ps, 1)

            def down_tile(t):
                pe.wait_ge(aT_ok, t + 1)
                if t >= 2:
                    pe.wait_ge(mk1_ok, t - 1)
                o = ps[:, 6 + t % 2, 0:D]
                mm(o, scales[:, 1, :], bias3[:, bass.ds(ex[t] * D + E * GU, D)], True, False)
                for k in range(KC):
                    for la, lw in parts:
                        w = w16[:, bass.ds(ex[t] * (2 * WE) + (lw * WE + KC * GU + k * D), D)]
                        last = mm(o, actT[:, t % 2, la, k, :], w, False, k == KC - 1 and (la, lw) == parts[-1])
                last.then_inc(oe1_ps, 1)

            xt_turn(0)
            xt_turn(1)
            gate_up_tile(0)
            xt_turn(2)
            for t in range(NTILE1 + 2):
                if t + 3 < NTILE1:
                    xt_turn(t + 3)
                if t + 1 < NTILE1:
                    gate_up_tile(t + 1)
                if 1 <= t <= NTILE1:
                    act_turn(t - 1)
                if t >= 2:
                    down_tile(t - 2)


_INS = ['x', 'ctx_2048', 'g_xattn', 'g_ffn', 'L0_xattn_w', 'L0_xattn_u', 'L0_ffn_Wg', 'L0_ffn_W1', 'L0_ffn_W3', 'L0_ffn_W2',
        'L0_ffn_sw1', 'L0_ffn_sw3', 'L0_ffn_sw2', 'L1_ffn_router_weight', 'L1_ffn_router_bias', 'L1_ffn_gate_up_proj',
        'L1_ffn_gate_up_proj_bias', 'L1_ffn_down_proj', 'L1_ffn_down_proj_bias']


def kernel(**inputs):
    import numpy as np
    import concourse.bacc as bacc
    from concourse.bass_utils import run_bass_kernel_spmd as run

    nc = bacc.Bacc("TRN2", target_bir_lowering=False, num_devices=1)
    arrays, args = {}, []
    for name in _INS:
        a = np.ascontiguousarray(inputs[name])
        arrays[f"in_{name}"] = a
        args.append(nc.dram_tensor(f"in_{name}", a.shape, mybir.dt.from_np(a.dtype), kind="ExternalInput").ap())
    out = nc.dram_tensor("out_x", inputs['x'].shape, FP32, kind="ExternalOutput").ap()
    flamingo_kernel(nc, *args, out)
    r = run(nc, [arrays], core_ids=[0])
    return r.results[0]["out_x"]
```
